# Optimizing a Trainium2 kernel written in Bass

```python
import numpy as np
import jax
import jax.numpy as jnp

def _softmax(x, axis=-1):
    return jax.nn.softmax(x, axis=axis)

def _gelu(x):
    return jax.nn.gelu(x, approximate=True)

def _silu(x):
    return jax.nn.silu(x)

def _sigmoid(x):
    return jax.nn.sigmoid(x)

def _layernorm(x, axis=-1, eps=1e-05):
    m = jnp.mean(x, axis=axis, keepdims=True)
    v = jnp.var(x, axis=axis, keepdims=True)
    return (x - m) / jnp.sqrt(v + eps)

def _scatter_add(tgt, idx, src, axis=0):
    return tgt.at[idx].add(src)

def _segment_sum(src, seg, n):
    return jax.ops.segment_sum(src, seg, n)
kernel_name = 'mk_conv_attn_hybrid_d2_conv_nchw256_r2_8558f2'

def setup_inputs(seed: int=0):
    np.random.seed(seed)
    _w = jnp.asarray

    def _rec_inputs():
        import jax
        import jax.numpy as jnp
        _gk = jax.random.key(seed)
        x = 7.22e-05 + 1 * jax.random.normal(jax.random.fold_in(_gk, 1), (8, 128, 32, 32), jnp.float32)
        return x
    x = _rec_inputs()

    def _L0_conv_setup():
        import jax, jax.numpy as jnp
        import numpy as np
        C = 128
        G = 8
        K = 9
        DWK = 3
        OFFSET_SCALE = 1.0
        N, H, W = (8, 32, 32)
        key = jax.random.key(seed)
        ks = jax.random.split(key, 6)

        def init(k, shape, fan):
            return jax.random.normal(k, shape, jnp.float32) * fan ** (-0.5)
        return {'x': jax.random.normal(ks[0], (N, C, H, W), jnp.float32), 'dw_w': init(ks[1], (C, 1, DWK, DWK), DWK * DWK), 'dw_b': jnp.zeros((C,), jnp.float32), 'om_w': init(ks[2], (G * K * 3, C), C) * 0.01, 'om_b': jnp.zeros((G * K * 3,), jnp.float32), 'vp_w': init(ks[3], (C, C), C), 'vp_b': jnp.zeros((C,), jnp.float32), 'op_w': init(ks[4], (C, C), C)}
    _L0_conv_all = _L0_conv_setup()
    _L0_conv_in = {k: v for k, v in _L0_conv_all.items() if k in ('dw_w', 'dw_b', 'om_w', 'om_b', 'vp_w', 'vp_b', 'op_w')}
    del _L0_conv_all

    def _L1_attn_setup():
        import jax, jax.numpy as jnp
        import numpy as np
        E = 128
        H = 8
        DK = 32
        DV = E // H
        LB = 32
        LF = 32
        WIN = LB + LF + 1
        NEG = -1000000000.0

        def _layer_norm(x, g, b, eps=1e-05):
            m = jnp.mean(x, axis=-1, keepdims=True)
            v = jnp.var(x, axis=-1, keepdims=True)
            return (x - m) * jax.lax.rsqrt(v + eps) * g + b

        def _local_rel_attention(x, Wq, bq, Wk, bk, Wv, bv, Wo, bo, rel_bias):
            B, S, _ = x.shape
            q = (x @ Wq + bq).reshape(B, S, H, DK).transpose(0, 2, 1, 3)
            k = (x @ Wk + bk).reshape(B, S, H, DK).transpose(0, 2, 1, 3)
            v = (x @ Wv + bv).reshape(B, S, H, DV).transpose(0, 2, 1, 3)
            kp = jnp.pad(k, ((0, 0), (0, 0), (LB, LF), (0, 0)))
            vp = jnp.pad(v, ((0, 0), (0, 0), (LB, LF), (0, 0)))
            scale = 1.0 / np.sqrt(DK)
            scores = jnp.stack([jnp.einsum('bhsd,bhsd->bhs', q, kp[:, :, w:w + S]) for w in range(WIN)], axis=-1) * scale
            scores = scores + rel_bias[None, :, None, :]
            key_pos = jnp.arange(S)[:, None] + jnp.arange(WIN)[None, :] - LB
            valid = (key_pos >= 0) & (key_pos < S)
            scores = jnp.where(valid[None, None], scores, NEG)
            p = jax.nn.softmax(scores, axis=-1)
            out = sum((p[..., w, None] * vp[:, :, w:w + S, :] for w in range(WIN)))
            out = out.transpose(0, 2, 1, 3).reshape(B, S, H * DV)
            return out @ Wo + bo
        key = jax.random.key(seed)
        ks = jax.random.split(key, 8)
        B, S = (4, 4096)
        s_in = 1.0 / np.sqrt(E)
        inp = {'x': jax.random.normal(ks[0], (B, S, E), jnp.float32), 'Wq': jax.random.normal(ks[1], (E, H * DK), jnp.float32) * s_in, 'bq': jnp.zeros((H * DK,), jnp.float32), 'Wk': jax.random.normal(ks[2], (E, H * DK), jnp.float32) * s_in, 'bk': jnp.zeros((H * DK,), jnp.float32), 'Wv': jax.random.normal(ks[3], (E, H * DV), jnp.float32) * s_in, 'bv': jnp.zeros((H * DV,), jnp.float32), 'Wo': jax.random.normal(ks[4], (H * DV, E), jnp.float32) * s_in, 'bo': jnp.zeros((E,), jnp.float32), 'rel_bias': jax.random.normal(ks[5], (H, WIN), jnp.float32) * 0.02, 'ln1_g': jnp.ones((E,), jnp.float32), 'ln1_b': jnp.zeros((E,), jnp.float32), 'W_lin': jax.random.normal(ks[6], (E, E), jnp.float32) * s_in, 'b_lin': jnp.zeros((E,), jnp.float32), 'ln2_g': jnp.ones((E,), jnp.float32), 'ln2_b': jnp.zeros((E,), jnp.float32)}
        return inp
    _L1_attn_all = _L1_attn_setup()
    _L1_attn_in = {k: v for k, v in _L1_attn_all.items() if k in ('Wq', 'bq', 'Wk', 'bk', 'Wv', 'bv', 'Wo', 'bo', 'rel_bias', 'ln1_g', 'ln1_b', 'W_lin', 'b_lin', 'ln2_g', 'ln2_b')}
    del _L1_attn_all

    def _L1_ffn_setup():
        import jax, jax.numpy as jnp
        import numpy as np
        TOP_K = 2
        LN_EPS = 1e-05
        key = jax.random.key(seed)
        ks = jax.random.split(key, 8)
        B, S, D, E, H = (16, 512, 128, 8, 512)
        x = jax.random.normal(ks[0], (B, S, D), dtype=jnp.float32)
        Wr = jax.random.normal(ks[1], (D, E), dtype=jnp.float32) * 0.1
        br = jnp.zeros((E,), dtype=jnp.float32)
        ln_g = jnp.ones((E, D), dtype=jnp.float32)
        ln_b = jnp.zeros((E, D), dtype=jnp.float32)
        W1 = jax.random.normal(ks[2], (E, D, H), dtype=jnp.float32) * (1.0 / np.sqrt(D))
        b1 = jnp.zeros((E, H), dtype=jnp.float32)
        W2 = jax.random.normal(ks[3], (E, H, D), dtype=jnp.float32) * (1.0 / np.sqrt(H))
        b2 = jnp.zeros((E, D), dtype=jnp.float32)
        return {'x': x, 'Wr': Wr, 'br': br, 'ln_g': ln_g, 'ln_b': ln_b, 'W1': W1, 'b1': b1, 'W2': W2, 'b2': b2}
    _L1_ffn_all = _L1_ffn_setup()
    _L1_ffn_in = {k: v for k, v in _L1_ffn_all.items() if k in ('Wr', 'br', 'ln_g', 'ln_b', 'W1', 'b1', 'W2', 'b2')}
    del _L1_ffn_all
    return {'x': x, 'L0_conv_dw_w': _L0_conv_in['dw_w'], 'L0_conv_dw_b': _L0_conv_in['dw_b'], 'L0_conv_om_w': _L0_conv_in['om_w'], 'L0_conv_om_b': _L0_conv_in['om_b'], 'L0_conv_vp_w': _L0_conv_in['vp_w'], 'L0_conv_vp_b': _L0_conv_in['vp_b'], 'L0_conv_op_w': _L0_conv_in['op_w'], 'L1_attn_Wq': _L1_attn_in['Wq'], 'L1_attn_bq': _L1_attn_in['bq'], 'L1_attn_Wk': _L1_attn_in['Wk'], 'L1_attn_bk': _L1_attn_in['bk'], 'L1_attn_Wv': _L1_attn_in['Wv'], 'L1_attn_bv': _L1_attn_in['bv'], 'L1_attn_Wo': _L1_attn_in['Wo'], 'L1_attn_bo': _L1_attn_in['bo'], 'L1_attn_rel_bias': _L1_attn_in['rel_bias'], 'L1_attn_ln1_g': _L1_attn_in['ln1_g'], 'L1_attn_ln1_b': _L1_attn_in['ln1_b'], 'L1_attn_W_lin': _L1_attn_in['W_lin'], 'L1_attn_b_lin': _L1_attn_in['b_lin'], 'L1_attn_ln2_g': _L1_attn_in['ln2_g'], 'L1_attn_ln2_b': _L1_attn_in['ln2_b'], 'L1_ffn_Wr': _L1_ffn_in['Wr'], 'L1_ffn_br': _L1_ffn_in['br'], 'L1_ffn_ln_g': _L1_ffn_in['ln_g'], 'L1_ffn_ln_b': _L1_ffn_in['ln_b'], 'L1_ffn_W1': _L1_ffn_in['W1'], 'L1_ffn_b1': _L1_ffn_in['b1'], 'L1_ffn_W2': _L1_ffn_in['W2'], 'L1_ffn_b2': _L1_ffn_in['b2']}

def reference(x, L0_conv_dw_w, L0_conv_dw_b, L0_conv_om_w, L0_conv_om_b, L0_conv_vp_w, L0_conv_vp_b, L0_conv_op_w, L1_attn_Wq, L1_attn_bq, L1_attn_Wk, L1_attn_bk, L1_attn_Wv, L1_attn_bv, L1_attn_Wo, L1_attn_bo, L1_attn_rel_bias, L1_attn_ln1_g, L1_attn_ln1_b, L1_attn_W_lin, L1_attn_b_lin, L1_attn_ln2_g, L1_attn_ln2_b, L1_ffn_Wr, L1_ffn_br, L1_ffn_ln_g, L1_ffn_ln_b, L1_ffn_W1, L1_ffn_b1, L1_ffn_W2, L1_ffn_b2):
    import jax
    import jax.numpy as jnp

    def _L0_conv_ref(x, dw_w, dw_b, om_w, om_b, vp_w, vp_b, op_w):
        import jax, jax.numpy as jnp
        import numpy as np
        C = 128
        G = 8
        K = 9
        DWK = 3
        OFFSET_SCALE = 1.0
        N, H, W = (8, 32, 32)
        n, c, h, w = x.shape
        cg = c // G
        L = h * w
        xf = x.transpose(0, 2, 3, 1).reshape(n, L, c)
        value = (xf @ vp_w.T + vp_b).reshape(n, L, G, cg)
        om_in = jax.lax.conv_general_dilated(x, dw_w, (1, 1), 'SAME', feature_group_count=c, dimension_numbers=('NCHW', 'OIHW', 'NCHW')) + dw_b[None, :, None, None]
        om = om_in.transpose(0, 2, 3, 1).reshape(n, L, c) @ om_w.T + om_b
        om = om.reshape(n, h, w, G, K * 3)
        off = om[..., :2 * K].reshape(n, h, w, G, K, 2) * OFFSET_SCALE
        mask = om[..., 2 * K:]
        d = jnp.arange(-1, 2, dtype=jnp.float32)
        dy, dx = jnp.meshgrid(d, d, indexing='ij')
        base = jnp.stack([dy.ravel(), dx.ravel()], -1)
        py = jnp.arange(h, dtype=jnp.float32).reshape(1, h, 1, 1, 1) + base[:, 0].reshape(1, 1, 1, 1, K) + off[..., 0]
        px = jnp.arange(w, dtype=jnp.float32).reshape(1, 1, w, 1, 1) + base[:, 1].reshape(1, 1, 1, 1, K) + off[..., 1]
        y0 = jnp.floor(py)
        x0 = jnp.floor(px)
        ty = py - y0
        tx = px - x0
        y0i = y0.astype(jnp.int32)
        x0i = x0.astype(jnp.int32)

        def gather(yi, xi, wgt):
            valid = (yi >= 0) & (yi < h) & (xi >= 0) & (xi < w)
            idx = jnp.clip(yi, 0, h - 1) * w + jnp.clip(xi, 0, w - 1)
            idx = idx.transpose(0, 1, 2, 4, 3).reshape(n, L * K, G)[..., None]
            g = jnp.take_along_axis(value, idx, axis=1)
            g = g.reshape(n, h, w, K, G, cg).transpose(0, 1, 2, 4, 3, 5)
            return g * (wgt * valid)[..., None]
        sampled = gather(y0i, x0i, (1 - ty) * (1 - tx)) + gather(y0i, x0i + 1, (1 - ty) * tx) + gather(y0i + 1, x0i, ty * (1 - tx)) + gather(y0i + 1, x0i + 1, ty * tx)
        out = jnp.einsum('nhwgk,nhwgkc->nhwgc', mask, sampled)
        out = out.reshape(n, L, c) @ op_w.T
        return out.reshape(n, h, w, c).transpose(0, 3, 1, 2)

    def _L1_attn_ref(x, Wq, bq, Wk, bk, Wv, bv, Wo, bo, rel_bias, ln1_g, ln1_b, W_lin, b_lin, ln2_g, ln2_b):
        import jax, jax.numpy as jnp
        import numpy as np
        E = 128
        H = 8
        DK = 32
        DV = E // H
        LB = 32
        LF = 32
        WIN = LB + LF + 1
        NEG = -1000000000.0

        def _layer_norm(x, g, b, eps=1e-05):
            m = jnp.mean(x, axis=-1, keepdims=True)
            v = jnp.var(x, axis=-1, keepdims=True)
            return (x - m) * jax.lax.rsqrt(v + eps) * g + b

        def _local_rel_attention(x, Wq, bq, Wk, bk, Wv, bv, Wo, bo, rel_bias):
            B, S, _ = x.shape
            q = (x @ Wq + bq).reshape(B, S, H, DK).transpose(0, 2, 1, 3)
            k = (x @ Wk + bk).reshape(B, S, H, DK).transpose(0, 2, 1, 3)
            v = (x @ Wv + bv).reshape(B, S, H, DV).transpose(0, 2, 1, 3)
            kp = jnp.pad(k, ((0, 0), (0, 0), (LB, LF), (0, 0)))
            vp = jnp.pad(v, ((0, 0), (0, 0), (LB, LF), (0, 0)))
            scale = 1.0 / np.sqrt(DK)
            scores = jnp.stack([jnp.einsum('bhsd,bhsd->bhs', q, kp[:, :, w:w + S]) for w in range(WIN)], axis=-1) * scale
            scores = scores + rel_bias[None, :, None, :]
            key_pos = jnp.arange(S)[:, None] + jnp.arange(WIN)[None, :] - LB
            valid = (key_pos >= 0) & (key_pos < S)
            scores = jnp.where(valid[None, None], scores, NEG)
            p = jax.nn.softmax(scores, axis=-1)
            out = sum((p[..., w, None] * vp[:, :, w:w + S, :] for w in range(WIN)))
            out = out.transpose(0, 2, 1, 3).reshape(B, S, H * DV)
            return out @ Wo + bo
        res = _local_rel_attention(x, Wq, bq, Wk, bk, Wv, bv, Wo, bo, rel_bias)
        xs = _layer_norm(x + res, ln1_g, ln1_b)
        res = jax.nn.relu(xs @ W_lin + b_lin)
        xs = _layer_norm(xs + res, ln2_g, ln2_b)
        return xs

    def _L1_ffn_ref(x, Wr, br, ln_g, ln_b, W1, b1, W2, b2):
        import jax, jax.numpy as jnp
        import numpy as np
        TOP_K = 2
        LN_EPS = 1e-05
        B, S, D = x.shape
        N = B * S
        xt = x.reshape(N, D)
        logits = xt @ Wr + br
        probs = jax.nn.softmax(logits, axis=-1)
        top_p, top_idx = jax.lax.top_k(probs, TOP_K)
        weights = top_p / top_p.sum(axis=-1, keepdims=True)
        mu = xt.mean(axis=-1, keepdims=True)
        var = ((xt - mu) ** 2).mean(axis=-1, keepdims=True)
        xn = (xt - mu) * jax.lax.rsqrt(var + LN_EPS)
        xe = xn[None, :, :] * ln_g[:, None, :] + ln_b[:, None, :]
        h = jax.nn.gelu(jnp.einsum('end,edh->enh', xe, W1) + b1[:, None, :], approximate=False)
        y = jnp.einsum('enh,ehd->end', h, W2) + b2[:, None, :]
        y_tok = jnp.transpose(y, (1, 0, 2))
        sel = jnp.take_along_axis(y_tok, top_idx[:, :, None], axis=1)
        out = (weights[:, :, None] * sel).sum(axis=1)
        return out.reshape(B, S, D)

    def _gn(v, G=32, eps=1e-05):
        B_, C_, H_, W_ = v.shape
        g = v.reshape(B_, G, C_ // G, H_, W_)
        m = jnp.mean(g, axis=(2, 3, 4), keepdims=True)
        s = jnp.var(g, axis=(2, 3, 4), keepdims=True)
        return ((g - m) / jnp.sqrt(s + eps)).reshape(v.shape)

    def _ln_c(v, eps=1e-06):
        m = jnp.mean(v, axis=1, keepdims=True)
        s = jnp.var(v, axis=1, keepdims=True)
        return (v - m) / jnp.sqrt(s + eps)

    def _ln_t(v, eps=1e-05):
        m = jnp.mean(v, axis=-1, keepdims=True)
        s = jnp.var(v, axis=-1, keepdims=True)
        return (v - m) / jnp.sqrt(s + eps)

    def _to_tokens(v):
        B_, C_, H_, W_ = v.shape
        return v.reshape(B_, C_, H_ * W_).transpose(0, 2, 1)

    def _from_tokens(t, like):
        B_, C_, H_, W_ = like.shape
        return t.transpose(0, 2, 1).reshape(B_, C_, H_, W_)
    x = x + _L0_conv_ref(_gn(x), L0_conv_dw_w, L0_conv_dw_b, L0_conv_om_w, L0_conv_om_b, L0_conv_vp_w, L0_conv_vp_b, L0_conv_op_w)
    t = _to_tokens(x)
    t = t + _L1_attn_ref(_ln_t(t), L1_attn_Wq, L1_attn_bq, L1_attn_Wk, L1_attn_bk, L1_attn_Wv, L1_attn_bv, L1_attn_Wo, L1_attn_bo, L1_attn_rel_bias, L1_attn_ln1_g, L1_attn_ln1_b, L1_attn_W_lin, L1_attn_b_lin, L1_attn_ln2_g, L1_attn_ln2_b)
    t = t + _L1_ffn_ref(_ln_t(t), L1_ffn_Wr, L1_ffn_br, L1_ffn_ln_g, L1_ffn_ln_b, L1_ffn_W1, L1_ffn_b1, L1_ffn_W2, L1_ffn_b2)
    x = _from_tokens(t, x)
    return x

_drawn_inputs = setup_inputs


def setup_inputs(seed=0):
    import zlib

    import numpy as np

    out = dict(_drawn_inputs(seed))
    spreads = {'L0_conv_dw_b': (0.0, 0.761),
     'L0_conv_om_b': (0.0, 0.1),
     'L0_conv_vp_b': (0.0, 0.1),
     'L1_attn_bq': (0.0, 0.354),
     'L1_attn_bk': (0.0, 0.8),
     'L1_attn_bv': (0.0, 0.1),
     'L1_attn_bo': (0.0, 0.1),
     'L1_attn_ln1_g': (1.0, 0.2),
     'L1_attn_ln1_b': (0.0, 0.1),
     'L1_attn_b_lin': (0.0, 0.1),
     'L1_attn_ln2_g': (1.0, 0.2),
     'L1_attn_ln2_b': (0.0, 0.1),
     'L1_ffn_br': (0.0, 0.1),
     'L1_ffn_ln_g': (1.0, 0.2),
     'L1_ffn_ln_b': (0.0, 0.319),
     'L1_ffn_b1': (0.0, 0.311),
     'L1_ffn_b2': (0.0, 0.1)}
    factors = {'L1_attn_rel_bias': 7.079}
    for name, (base, spread) in spreads.items():
        noise = np.random.default_rng([zlib.crc32(name.encode()), seed]).standard_normal(out[name].shape)
        drawn = base * np.exp(spread * noise) if base else spread * noise
        out[name] = jnp.asarray(drawn.astype(out[name].dtype))
    for name, factor in factors.items():
        out[name] = (out[name] * factor).astype(out[name].dtype)
    return out
```

```python
from contextlib import ExitStack

import concourse.bass as bass
from concourse import mybir

ALU = mybir.AluOpType
ACT = mybir.ActivationFunctionType
AX = mybir.AxisListType
F32 = mybir.dt.float32
I32 = mybir.dt.int32
BF16 = mybir.dt.bfloat16
U32 = mybir.dt.uint32

P = 128
IMAGES, SIDE = 8, 32
PIX = SIDE * SIDE
TOK = IMAGES * PIX
CH = 512
HALF = SIDE // 2
NCH = TOK // CH
TPC = CH // P
GROUPS, CG, K = 8, 16, 9
GK = GROUPS * K
WIN5 = 25
PAD3, PAD5 = SIDE + 2, SIDE + 4
HEADS, DK, DV = 8, 32, 16
REACH = 32
QB = 64
UNITS = PIX // (2 * QB)
EXPERTS, HID = 8, 512
HC = HID // P
NEG = -1e9
EPS = 1e-5


class Ctx:

    def __init__(self, nc):
        self.nc = nc
        self.outer = ExitStack()

    def scope(self):
        return ExitStack()


def sb(nc, st, name, shape, dt=F32):
    return st.enter_context(nc.sbuf_tensor(name, shape, dt))


def ps(nc, st, name, shape=(P, CH), dt=F32):
    return st.enter_context(nc.psum_tensor(name, list(shape), dt))


def sem(nc, st, name):
    return st.enter_context(nc.semaphore(name))


def front(nc, d, X, VP, OM, flag):
    with ExitStack() as st:
        ident = sb(nc, st, "f_ident", [P, P])
        g4 = sb(nc, st, "f_g4", [P, P])
        vpT = sb(nc, st, "f_vpT", [P, P])
        omT = sb(nc, st, "f_omT", [P, 3 * GK])
        omb = sb(nc, st, "f_omb", [P, 3 * GK])
        dww = sb(nc, st, "f_dww", [P, K])
        dwb = sb(nc, st, "f_dwb", [P, 1])
        vpb = sb(nc, st, "f_vpb", [P, 1])
        stats = sb(nc, st, "f_stats", [P, IMAGES, 2, 6])
        mv = sb(nc, st, "f_mv", [P, IMAGES, 2])
        dev = sb(nc, st, "f_dev", [P, IMAGES])
        gmean = sb(nc, st, "f_gmean", [P, IMAGES])
        var = sb(nc, st, "f_var", [P, IMAGES])
        sd = sb(nc, st, "f_sd", [P, IMAGES])
        rs = sb(nc, st, "f_rs", [P, IMAGES])
        nb = sb(nc, st, "f_nb", [P, IMAGES])
        eps = sb(nc, st, "f_eps", [P, 1])
        xnp = [sb(nc, st, f"f_xnp{j}", [P, PAD3, PAD3]) for j in range(2)]
        omin = [sb(nc, st, f"f_omin{j}", [P, PIX]) for j in range(2)]
        fmax = sb(nc, st, "f_fmax", [P, IMAGES])
        fone = sb(nc, st, "f_fone", [P, 1])
        ftop = sb(nc, st, "f_ftop", [1, 1])

        p_stat = ps(nc, st, "f_pstat")
        p_val = [ps(nc, st, f"f_pval{h}") for h in range(2)]
        p_om = [ps(nc, st, f"f_pom{h}") for h in range(4)]

        x_in = [sem(nc, st, f"x_in{n}") for n in range(IMAGES)]
        w_in = sem(nc, st, "w_in")
        cleared = sem(nc, st, "f_cleared")
        stat = sem(nc, st, "f_stat")
        avg = sem(nc, st, "f_avg")
        rooted = sem(nc, st, "f_rooted")
        normed = sem(nc, st, "f_normed")
        val_done = sem(nc, st, "f_val_done")
        val_out = sem(nc, st, "f_val_out")
        tap_done = sem(nc, st, "f_tap_done")
        om_done = sem(nc, st, "f_om_done")
        om_out = sem(nc, st, "f_om_out")
        folded = sem(nc, st, "f_folded")

        with nc.Block() as block:
            @block.sync
            def _(sp):
                for n in range(IMAGES):
                    sp.dma_start(X[:, n * PIX:(n + 1) * PIX], d["x"][n]).then_inc(x_in[n], 16)
                for dst, src in ((ident, "c_ident"), (g4, "c_group4"), (vpT, "vp_wT"), (omT, "om_wT"),
                                 (dww, "dw_w"), (dwb, "dw_b"), (vpb, "vp_b")):
                    sp.dma_start(dst[:], d[src]).then_inc(w_in, 16)
                sp.dma_start(omb[:], d["om_b"].partition_broadcast(P)).then_inc(w_in, 16)

            @block.gpsimd
            def _(pool):
                for b in xnp:
                    nc.gpsimd.memset(b[:], 0.0).then_inc(cleared, 1)
                nc.gpsimd.memset(eps[:], EPS).then_inc(cleared, 1)
                nc.gpsimd.memset(VP[:], 0.0).then_inc(cleared, 1)

            @block.scalar
            def _(act):
                act.wait_ge(cleared, 4)
                act.wait_ge(avg, 2)
                act.activation(sd[:], p_stat[:, 8:16], ACT.Sqrt, bias=eps[:]).then_inc(rooted, 1)
                act.wait_ge(w_in, 16 * 8)
                act.wait_ge(stat, 5)
                def image(n, j, first):
                    if not first:
                        act.wait_ge(tap_done, (n - 1) * (2 * K))
                        act.wait_ge(val_done, (n - 1) * 2)
                    act.activation(xnp[j][:, 1:1 + SIDE, 1:1 + SIDE],
                                   X[:, bass.ds(n * PIX, PIX)].rearrange("p (a b) -> p a b", a=SIDE),
                                   ACT.Identity, bias=nb[:, bass.ds(n, 1)],
                                   scale=rs[:, bass.ds(n, 1)]).then_inc(normed, 1)
                    for h in range(2):
                        act.wait_ge(val_done, n * 2 + h + 1)
                        act.activation(
                            VP[:, bass.ds(n, 1), 2 + h * HALF:2 + (h + 1) * HALF, 2:2 + SIDE]
                            .rearrange("p o a b -> p (o a) b"),
                            p_val[h][:].rearrange("p (a b) -> p a b", a=HALF),
                            ACT.Identity, bias=vpb[:]).then_inc(val_out, 1)

                image(0, 0, True)
                image(1, 1, True)
                with act.Fori(1, IMAGES // 2) as i:
                    image(i * 2, 0, False)
                    image(i * 2 + 1, 1, False)

            @block.vector
            def _(dve):
                for n in range(IMAGES):
                    dve.wait_ge(x_in[n], 16)
                    for h in range(2):
                        last = dve.bn_stats(stats[:, n, h, :], X[:, n * PIX + h * CH:n * PIX + (h + 1) * CH])
                    last.then_inc(folded, 1)
                for n in range(IMAGES):
                    dve.wait_ge(folded, n + 1)
                    last = dve.bn_aggr(mv[:, n, :], stats[:, n, :, :])
                last.then_inc(stat, 1)
                dve.wait_ge(stat, 1)
                dve.wait_ge(avg, 1)
                dve.tensor_tensor(dev[:], mv[:, :, 0], p_stat[:, 0:8], ALU.subtract).then_inc(stat, 1)
                dve.tensor_copy(gmean[:], p_stat[:, 0:8]).then_inc(folded, 1)
                dve.wait_ge(stat, 2)
                dve.tensor_tensor(var[:], dev[:], dev[:], ALU.mult).then_inc(folded, 1)
                dve.wait_ge(folded, IMAGES + 2)
                dve.tensor_tensor(var[:], var[:], mv[:, :, 1], ALU.add).then_inc(stat, 1)
                dve.wait_ge(rooted, 1)
                dve.reciprocal(rs[:], sd[:]).then_inc(stat, 1)
                dve.wait_ge(stat, 4)
                dve.scalar_tensor_tensor(nb[:], gmean[:], -1.0, rs[:], ALU.mult, ALU.mult).then_inc(stat, 1)
                dve.wait_ge(w_in, 16 * 8)
                with dve.Fori(0, IMAGES // 2) as i:
                    for j in range(2):
                        n = i * 2 + j
                        dve.wait_ge(normed, n + 1)
                        dve.wait_ge(om_done, n * 4)
                        for k in range(K):
                            for h in range(2):
                                out = omin[j][:, h * CH:(h + 1) * CH].rearrange("p (a b) -> p a b", a=HALF)
                                src = xnp[j][:, k // 3 + h * HALF:k // 3 + (h + 1) * HALF, k % 3:k % 3 + SIDE]
                                if k == 0:
                                    ins = dve.tensor_scalar(out, src, dww[:, 0:1], dwb[:], ALU.mult, ALU.add)
                                else:
                                    dve.wait_ge(tap_done, n * (2 * K) + 2 * (k - 1) + h + 1)
                                    ins = dve.scalar_tensor_tensor(out, src, dww[:, k:k + 1], out,
                                                                   ALU.mult, ALU.add)
                                ins.then_inc(tap_done, 1)
                        for q in range(4):
                            dve.wait_ge(om_done, n * 4 + q + 1)
                            dve.tensor_tensor(
                                OM[:, bass.ds(n * 8 + 2 * q, 2), :],
                                p_om[q][:, 0:6 * GK].rearrange("p (t c) -> p t c", t=2),
                                omb[:].rearrange("p (t c) -> p t c", t=1).to_broadcast([P, 2, 3 * GK]),
                                ALU.add).then_inc(om_out, 1)
                        dve.wait_ge(om_out, n * 4 + 4)
                        dve.tensor_reduce(fmax[:, bass.ds(n, 1)], OM[:, bass.ds(n * 8, 8), 0:2 * GK],
                                          AX.XY, ALU.max, apply_absolute_value=True).then_inc(folded, 1)
                dve.wait_ge(folded, 2 * IMAGES + 2)
                dve.tensor_reduce(fone[:], fmax[:], AX.X, ALU.max).then_inc(stat, 1)
                dve.wait_ge(avg, 3)
                dve.tensor_reduce(ftop[:], p_stat[0:1, 0:P], AX.X, ALU.max).then_inc(stat, 1)
                dve.wait_ge(stat, 7)
                dve.tensor_scalar(flag[:], ftop[:], 1.0, None, ALU.is_gt).then_inc(stat, 1)

            @block.tensor
            def _(pe):
                pe.wait_ge(w_in, 16 * 8)
                pe.wait_ge(stat, 1)
                pe.matmul(p_stat[:, 0:8], g4[:], mv[:, :, 0], start=True, stop=True).then_inc(avg, 1)
                pe.wait_ge(stat, 3)
                pe.matmul(p_stat[:, 8:16], g4[:], var[:], start=True, stop=True).then_inc(avg, 1)
                with pe.Fori(0, IMAGES // 2) as i:
                    for j in range(2):
                        n = i * 2 + j
                        pe.wait_ge(normed, n + 1)
                        pe.wait_ge(val_out, n * 2)
                        for h in range(2):
                            pe.matmul(p_val[h][:], vpT[:],
                                      xnp[j][:, 1 + h * HALF:1 + (h + 1) * HALF, 1:1 + SIDE],
                                      start=True, stop=True).then_inc(val_done, 1)
                        pe.wait_ge(om_out, n * 4)
                        for q in range(4):
                            pe.wait_ge(tap_done, n * (2 * K) + 2 * (K - 1) + q // 2 + 1)
                            for t in range(2):
                                last = pe.matmul(p_om[q][:, t * 3 * GK:(t + 1) * 3 * GK],
                                                 omin[j][:, (2 * q + t) * P:(2 * q + t + 1) * P], omT[:],
                                                 start=True, stop=True)
                            last.then_inc(om_done, 1)
                pe.wait_ge(stat, 6)
                pe.transpose(p_stat[0:1, 0:P], fone[:], ident[:]).then_inc(avg, 1)


def sample_fast(nc, d, X, VP, OM):
    ROWS = 3 * GROUPS * 5
    with ExitStack() as st:
        identf = sb(nc, st, "s_identf", [P, P])
        ident = sb(nc, st, "s_ident", [P, P], BF16)
        sel = sb(nc, st, "s_sel", [ROWS, 5, P], BF16)
        self32 = sb(nc, st, "s_self32", [ROWS, 5, P])
        opT = sb(nc, st, "s_opT", [P, P])
        A = sb(nc, st, "s_A", [P, TPC, GROUPS, WIN5])
        MY = sb(nc, st, "s_MY", [P, 3, TPC, GK])
        PR = sb(nc, st, "s_PR", [P, 3, 3, TPC, GK])
        rest = sb(nc, st, "s_rest", [P, TPC, 5, GROUPS * 5])
        parts = sb(nc, st, "s_parts", [P, TPC, 5, 3, GROUPS * 5], BF16)
        AT = [sb(nc, st, f"s_AT{j}", [ROWS, 5, CH], BF16) for j in range(2)]
        prod_pe = [sb(nc, st, f"s_pp{i}", [P, CH]) for i in range(3)]
        prod_pool = [sb(nc, st, f"s_pq{i}", [P, CH]) for i in range(3)]
        acc = [sb(nc, st, f"s_acc{j}", [P, CH]) for j in range(2)]
        NB = 4
        p_bc = [ps(nc, st, f"s_pbc{i}") for i in range(NB)]
        p_out = [ps(nc, st, f"s_pout{j}") for j in range(2)]
        p_tr = [ps(nc, st, f"s_ptr{j}", (P, 2, CH), BF16) for j in range(2)]

        zero = sb(nc, st, "s_zero", [P, 1])

        w_in = sem(nc, st, "s_w_in")
        zeroed = sem(nc, st, "s_zeroed")
        cast = sem(nc, st, "s_cast")
        cleared = sem(nc, st, "s_cleared")
        step = sem(nc, st, "s_step")
        coef = sem(nc, st, "s_coef")
        high = sem(nc, st, "s_high")
        left = sem(nc, st, "s_left")
        mid = sem(nc, st, "s_mid")
        low = sem(nc, st, "s_low")
        turned = sem(nc, st, "s_turned")
        stored = sem(nc, st, "s_stored")
        bc = sem(nc, st, "s_bc")
        mul = sem(nc, st, "s_mul")
        summed = sem(nc, st, "s_summed")
        opm = sem(nc, st, "s_opm")
        outp = sem(nc, st, "s_outp")
        resid = sem(nc, st, "s_resid")
        NPE, NPO = (WIN5 + 1) // 2, WIN5 // 2
        STEPS = 5

        with nc.Block() as block:
            @block.sync
            def _(sp):
                sp.dma_start(identf[:], d["c_ident"]).then_inc(w_in, 16)
                sp.dma_start(opT[:], d["op_wT"]).then_inc(w_in, 16)
                sp.dma_start(self32[:], d["c_select"]).then_inc(w_in, 16)

            @block.gpsimd
            def _(pool):
                nc.gpsimd.memset(zero[:], 0.0).then_inc(zeroed, 1)
                nc.gpsimd.memset(A[:], 0.0).then_inc(cleared, 1)

                def chunk(c, j, first):
                    for m in range(1, NPO):
                        pool.wait_ge(mul, c * WIN5 + 2 * m + 2)
                        src = prod_pool[m % 3][:]
                        if m == 1:
                            if not first:
                                pool.wait_ge(outp, c - 1)
                            before = prod_pool[0][:]
                        else:
                            pool.wait_ge(summed, c * (NPO - 1) + m - 1)
                            before = acc[j][:]
                        nc.gpsimd.tensor_tensor(acc[j][:], before, src, ALU.add).then_inc(summed, 1)

                chunk(0, 0, True)
                chunk(1, 1, True)
                with pool.Fori(1, IMAGES) as n:
                    chunk(n * 2, 0, False)
                    chunk(n * 2 + 1, 1, False)

            @block.scalar
            def _(act):
                act.wait_ge(w_in, 48)
                act.wait_ge(zeroed, 1)
                act.activation(ident[:], identf[:], ACT.Copy).then_inc(cast, 1)
                act.activation(sel[:], self32[:], ACT.Copy).then_inc(cast, 1)

                def chunk(c, j, first):
                    act.wait_ge(coef, c * 9 + 9)
                    if not (isinstance(c, int) and c == 0):
                        act.wait_ge(turned, c * 3)
                    for t in range(TPC):
                        act.activation(parts[:, t, :, 0].rearrange("p q (g b) -> p q g b", b=5),
                                       A[:, t].rearrange("p g (q b) -> p q g b", b=5),
                                       ACT.Copy).then_inc(high, 1)
                    act.wait_ge(left, c * TPC + TPC)
                    act.activation(parts[:, :, :, 1], rest[:], ACT.Copy).then_inc(mid, 1)
                    act.activation(A[:].rearrange("p t g w -> p (t g w)"),
                                   zero[:].to_broadcast([P, TPC * GROUPS * WIN5]), ACT.Copy)\
                       .then_inc(cleared, 1)
                    if not first:
                        act.wait_ge(bc, (c - 1) * WIN5)
                    for q in range(0, 5, 2):
                        act.wait_ge(turned, c * 3 + q // 2 + 1)
                        w = min(2, 5 - q)
                        act.activation(AT[j][:, q:q + w], p_tr[(q // 2) % 2][0:ROWS, 0:w], ACT.Copy)\
                           .then_inc(stored, 1)

                chunk(0, 0, True)
                chunk(1, 1, True)
                with act.Fori(1, IMAGES) as n:
                    chunk(n * 2, 0, False)
                    chunk(n * 2 + 1, 1, False)

            @block.vector
            def _(dve):
                def weights(c, first):
                    om = OM[:, bass.ds(c * TPC, TPC), :]
                    oy, ox, m = om[:, :, 0:GK], om[:, :, GK:2 * GK], om[:, :, 2 * GK:3 * GK]
                    b = c * STEPS
                    dve.scalar_tensor_tensor(MY[:, 2], oy, 0.0, m, ALU.max, ALU.mult)
                    dve.scalar_tensor_tensor(MY[:, 0], oy, 0.0, m, ALU.min, ALU.mult).then_inc(step, 1)
                    dve.wait_ge(step, b + 1)
                    dve.tensor_tensor(MY[:, 1], m, MY[:, 2], ALU.subtract).then_inc(step, 1)
                    dve.wait_ge(step, b + 2)
                    dve.tensor_tensor(MY[:, 1], MY[:, 1], MY[:, 0], ALU.add).then_inc(step, 1)
                    dve.wait_ge(step, b + 3)
                    for r in range(3):
                        dve.scalar_tensor_tensor(PR[:, r, 2], ox, 0.0, MY[:, r], ALU.max, ALU.mult)
                    for r in range(3):
                        ins = dve.scalar_tensor_tensor(PR[:, r, 0], ox, 0.0, MY[:, r], ALU.min, ALU.mult)
                    ins.then_inc(step, 1)
                    dve.wait_ge(step, b + 4)
                    flat = "p r t k -> p r (t k)"
                    dve.tensor_tensor(PR[:, :, 1].rearrange(flat), MY[:].rearrange(flat),
                                      PR[:, :, 2].rearrange(flat), ALU.subtract).then_inc(step, 1)
                    dve.wait_ge(step, b + 5)
                    dve.tensor_tensor(PR[:, :, 1].rearrange(flat), PR[:, :, 1].rearrange(flat),
                                      PR[:, :, 0].rearrange(flat), ALU.add)
                    dve.wait_ge(cleared, c + 1)
                    win = A[:].rearrange("p t g (a b) -> p (t g) a b", a=5)
                    n = 0
                    for q in (0, 2, 1):
                        for r in range(3):
                            v = win[:, :, r:r + 3, q:q + 3]
                            w = PR[:, r, q].rearrange("p t (g a b) -> p (t g) a b", a=3, b=3)
                            if n:
                                dve.wait_ge(coef, c * 9 + n)
                            dve.tensor_tensor(v, v, w, ALU.subtract if (r == 0) != (q == 0) else ALU.add)\
                               .then_inc(coef, 1)
                            n += 1

                def split_rest(c):
                    for t in range(TPC):
                        dve.wait_ge(high, c * TPC + t + 1)
                        dve.tensor_tensor(rest[:, t].rearrange("p q (g b) -> p q g b", b=5),
                                          A[:, t].rearrange("p g (q b) -> p q g b", b=5),
                                          parts[:, t, :, 0].rearrange("p q (g b) -> p q g b", b=5),
                                          ALU.subtract).then_inc(left, 1)

                def split_low(c):
                    dve.wait_ge(mid, c + 1)
                    dve.tensor_tensor(parts[:, :, :, 2], rest[:], parts[:, :, :, 1], ALU.subtract)\
                       .then_inc(low, 1)

                def multiply(c, n, h, taps):
                    for t in taps:
                        dve.wait_ge(bc, c * WIN5 + t + 1)
                        m = t // 2
                        if t % 2 == 0:
                            out = prod_pe[m % 3]
                            if m >= 3 or m == 0:
                                dve.wait_ge(opm, c * NPE + max(m - 2, 0))
                        else:
                            out = prod_pool[m % 3]
                            if m >= 3 or m == 0:
                                dve.wait_ge(summed, c * (NPO - 1) + max(m - 3, min(m, 1)))
                        y, x = t // 5, t % 5
                        dve.tensor_tensor(
                            out[:].rearrange("p (a b) -> p a b", a=HALF),
                            p_bc[t % NB][:].rearrange("p (a b) -> p a b", a=HALF),
                            VP[:, bass.ds(n, 1), h * HALF + y:h * HALF + y + HALF, x:x + SIDE]
                            .rearrange("p o a b -> p (o a) b"),
                            ALU.mult).then_inc(mul, 1)

                def residual(c, j):
                    dve.wait_ge(outp, c + 1)
                    cols = X[:, bass.ds(c * CH, CH)]
                    dve.tensor_tensor(cols, cols, p_out[j][:], ALU.add).then_inc(resid, 1)

                weights(0, True)
                split_rest(0)
                split_low(0)
                with dve.Fori(0, IMAGES - 1) as n:
                    for h in range(2):
                        c = n * 2 + h
                        multiply(c, n, h, range(0, 12))
                        weights(c + 1, False)
                        multiply(c, n, h, range(12, 15))
                        split_rest(c + 1)
                        multiply(c, n, h, range(15, 17))
                        split_low(c + 1)
                        multiply(c, n, h, range(17, WIN5))
                        residual(c, h)
                n, c = IMAGES - 1, NCH - 2
                multiply(c, n, 0, range(0, 12))
                weights(c + 1, False)
                multiply(c, n, 0, range(12, 15))
                split_rest(c + 1)
                multiply(c, n, 0, range(15, 17))
                split_low(c + 1)
                multiply(c, n, 0, range(17, WIN5))
                residual(c, 0)
                multiply(c + 1, n, 1, range(WIN5))
                residual(c + 1, 1)

            @block.tensor
            def _(pe):
                pe.wait_ge(cast, 2)
                LAG = 3

                def turn(c):
                    pe.wait_ge(low, c + 1)
                    for q in range(5):
                        if q == 4 :
                            pe.wait_ge(stored, c * 3 + 1)
                        if q == 0 and not (isinstance(c, int) and c == 0):
                            pe.wait_ge(stored, c * 3)
                        for t in range(TPC):
                            last = pe.transpose(p_tr[(q // 2) % 2][0:ROWS, q % 2, t * P:(t + 1) * P],
                                                parts[:, t, q].rearrange("p a b -> p (a b)"), ident[:])
                        if q % 2 or q == 4:
                            last.then_inc(turned, 1)

                def spread(c, j, t):
                    if t % 10 == 0:
                        pe.wait_ge(stored, c * 3 + t // 10 + 1)
                    if not (isinstance(c, int) and c * WIN5 + t < NB):
                        pe.wait_ge(mul, c * WIN5 + t - (NB - 1))
                    pe.matmul(p_bc[t % NB][:], sel[:, t % 5, :], AT[j][:, t // 5, :],
                              start=True, stop=True).then_inc(bc, 1)

                def project(c, j, m):
                    pe.wait_ge(mul, c * WIN5 + 2 * m + 1)
                    pe.matmul(p_out[j][:], opT[:], prod_pe[m % 3][:], start=(m == 0), stop=False)\
                      .then_inc(opm, 1)

                def chunk(c, j, first, last):
                    if not first:
                        pe.wait_ge(resid, c - 1)
                    for t in range(WIN5 + LAG):
                        if t < WIN5:
                            spread(c, j, t)
                        if t == WIN5 - 2 and not last:
                            turn(c + 1)
                        if t >= LAG and (t - LAG) % 2 == 0:
                            project(c, j, (t - LAG) // 2)
                    pe.wait_ge(summed, (c + 1) * (NPO - 1))
                    pe.matmul(p_out[j][:], opT[:], acc[j][:], start=False, stop=True).then_inc(outp, 1)

                turn(0)
                chunk(0, 0, True, False)
                chunk(1, 1, True, False)
                with pe.Fori(1, IMAGES - 1) as n:
                    chunk(n * 2, 0, False, False)
                    chunk(n * 2 + 1, 1, False, False)
                chunk(NCH - 2, 0, False, False)
                chunk(NCH - 1, 1, False, True)


def sample_general(nc, d, X, VP, OM, flag):
    TPI = PIX // P
    with ExitStack() as st:
        ident = sb(nc, st, "g_ident", [P, P])
        opT = sb(nc, st, "g_opT", [P, P])
        line = sb(nc, st, "g_line", [P, SIDE])
        pix = sb(nc, st, "g_pix", [P, TPI, 2])
        kern = sb(nc, st, "g_kern", [P, 2, GK])
        pos = sb(nc, st, "g_pos", [P, 2, GK])
        W = [sb(nc, st, f"g_W{a}", [P, GK, SIDE]) for a in range(2)]
        outer = sb(nc, st, "g_outer", [P, SIDE, SIDE])
        AG = sb(nc, st, "g_AG", [P, PIX])
        AGT = sb(nc, st, "g_AGT", [P, TPI, P])
        VC = sb(nc, st, "g_VC", [P, PIX])
        VT = sb(nc, st, "g_VT", [P, TPI, P])
        S = sb(nc, st, "g_S", [P, P])
        ST = sb(nc, st, "g_ST", [P, P])
        p_tr = [ps(nc, st, f"g_ptr{i}") for i in range(2)]
        p_s = ps(nc, st, "g_ps", (P, P))
        p_st = ps(nc, st, "g_pst", (P, P))
        p_o = ps(nc, st, "g_po", (P, P))
        w_in = sem(nc, st, "g_w_in")
        image = sem(nc, st, "g_image")
        vturn = sem(nc, st, "g_vturn")
        vout = sem(nc, st, "g_vout")
        step = sem(nc, st, "g_step")
        dist = sem(nc, st, "g_dist")
        tent = sem(nc, st, "g_tent")
        part = sem(nc, st, "g_part")
        wsum = sem(nc, st, "g_wsum")
        turned = sem(nc, st, "g_turned")
        moved = sem(nc, st, "g_moved")
        applied = sem(nc, st, "g_applied")
        sout = sem(nc, st, "g_sout")
        sturn = sem(nc, st, "g_sturn")
        stout = sem(nc, st, "g_stout")
        projected = sem(nc, st, "g_projected")
        added = sem(nc, st, "g_added")

        with nc.Block() as block:
            @block.sync
            def _(sp):
                far = sp.value_load(flag[0:1, 0:1])
                with sp.If(far > 0):
                    for n in range(IMAGES):
                        sp.dma_start(X[:, n * PIX:(n + 1) * PIX], d["x"][n]).then_inc(w_in, 16)
                    for dst, src in ((ident, "c_ident"), (opT, "op_wT"), (pix, "c_pixel"), (kern, "c_kernel"),
                                     (line, "c_line")):
                        sp.dma_start(dst[:], d[src]).then_inc(w_in, 16)
                sp.nop()

            @block.vector
            def _(dve):
                far = dve.value_load(flag[0:1, 0:1])
                with dve.If(far > 0):
                    dve.wait_ge(w_in, 16 * (IMAGES + 5))
                    with dve.Fori(0, IMAGES) as n:
                        dve.wait_ge(vturn, n)
                        dve.tensor_copy(VC[:].rearrange("p (a b) -> p a b", a=SIDE),
                                        VP[:, bass.ds(n, 1), 2:2 + SIDE, 2:2 + SIDE]
                                        .rearrange("p o a b -> p (o a) b")).then_inc(image, 1)
                        with dve.Fori(0, TPI) as t:
                            c = n * TPI + t
                            for a in range(2):
                                dve.scalar_tensor_tensor(
                                    pos[:, a], OM[:, bass.ds(c, 1), a * GK:(a + 1) * GK]
                                    .rearrange("p o k -> p (o k)"), pix[:, bass.ds(t, 1), a]
                                    , kern[:, a], ALU.add, ALU.add).then_inc(step, 1)
                            dve.wait_ge(step, c * 2 + 2)
                            for a in range(2):
                                dve.tensor_tensor(
                                    W[a][:], pos[:, a].rearrange("p (k o) -> p k o", o=1)
                                    .to_broadcast([P, GK, SIDE]),
                                    line[:].rearrange("p (o s) -> p o s", o=1).to_broadcast([P, GK, SIDE]),
                                    ALU.subtract).then_inc(dist, 1)
                            dve.wait_ge(tent, c * 2 + 2)
                            dve.tensor_tensor(
                                W[0][:], W[0][:], OM[:, bass.ds(c, 1), 2 * GK:3 * GK]
                                .rearrange("p o k -> p k o").to_broadcast([P, GK, SIDE]),
                                ALU.mult).then_inc(part, 1)
                            with dve.Fori(0, GROUPS) as g:
                                cg = c * GROUPS + g
                                dve.wait_ge(turned, cg * 2)
                                for k in range(K):
                                    wy = W[0][:, bass.ds(g * K + k, 1), :].rearrange("p o s -> p s o")\
                                        .to_broadcast([P, SIDE, SIDE])
                                    wx = W[1][:, bass.ds(g * K + k, 1), :].to_broadcast([P, SIDE, SIDE])
                                    dve.wait_ge(part, (c + 1) + cg * 17 + max(2 * k - 1, 0))
                                    out = AG[:].rearrange("p (a b) -> p a b", a=SIDE) if k == 0 else outer[:]
                                    dve.tensor_tensor(out, wy, wx, ALU.mult).then_inc(part, 1)
                                    if k:
                                        dve.wait_ge(part, (c + 1) + cg * 17 + 2 * k)
                                        dve.tensor_tensor(AG[:], AG[:], outer[:].rearrange("p a b -> p (a b)"),
                                                          ALU.add).then_inc(part, 1)
                                dve.wait_ge(part, (c + 1) + cg * 17 + 17)
                                dve.tensor_copy(pos[0:1, 0, 0:1], pos[0:1, 0, 0:1]).then_inc(wsum, 1)
                            dve.wait_ge(applied, c * GROUPS + GROUPS)
                            dve.tensor_copy(S[:], p_s[:]).then_inc(sout, 1)
                            dve.wait_ge(sturn, c + 1)
                            dve.tensor_copy(ST[:], p_st[:]).then_inc(stout, 1)
                            dve.wait_ge(projected, c + 1)
                            cols = X[:, bass.ds(c * P, P)]
                            dve.tensor_tensor(cols, cols, p_o[:], ALU.add).then_inc(added, 1)
                dve.engine_nop()

            @block.scalar
            def _(act):
                far = act.value_load(flag[0:1, 0:1])
                with act.If(far > 0):
                    with act.Fori(0, IMAGES) as n:
                        for h in range(2):
                            act.wait_ge(vturn, n + 1)
                            act.activation(VT[:, h * 4:h * 4 + 4].rearrange("p m c -> p (m c)"), p_tr[h][:],
                                           ACT.Copy).then_inc(vout, 1)
                        with act.Fori(0, TPI) as t:
                            c = n * TPI + t
                            for a in range(2):
                                act.wait_ge(dist, c * 2 + a + 1)
                                act.activation(W[a][:], W[a][:], ACT.Abs).then_inc(moved, 1)
                                act.wait_ge(moved, c * (2 + 2 * GROUPS) + a + 1)
                                act.activation(W[a][:], W[a][:], ACT.Relu, bias=1.0, scale=-1.0)\
                                   .then_inc(tent, 1)
                            with act.Fori(0, GROUPS) as g:
                                cg = c * GROUPS + g
                                act.wait_ge(applied, cg)
                                for h in range(2):
                                    act.wait_ge(turned, cg * 2 + h + 1)
                                    act.activation(AGT[:, h * 4:h * 4 + 4].rearrange("p m c -> p (m c)"),
                                                   p_tr[h][:], ACT.Copy).then_inc(moved, 1)
                act.nop()

            @block.tensor
            def _(pe):
                far = pe.value_load(flag[0:1, 0:1])
                with pe.If(far > 0):
                    pe.wait_ge(w_in, 16 * (IMAGES + 5))
                    with pe.Fori(0, IMAGES) as n:
                        pe.wait_ge(image, n + 1)
                        pe.wait_ge(moved, n * (TPI * (2 + 2 * GROUPS)))
                        for m in range(TPI):
                            last = pe.transpose(p_tr[m // 4][:, (m % 4) * P:(m % 4 + 1) * P],
                                                VC[:, m * P:(m + 1) * P], ident[:])
                        last.then_inc(vturn, 1)
                        with pe.Fori(0, TPI) as t:
                            c = n * TPI + t
                            with pe.Fori(0, GROUPS) as g:
                                cg = c * GROUPS + g
                                pe.wait_ge(vout, n * 2 + 2)
                                pe.wait_ge(sout, c)
                                pe.wait_ge(wsum, cg + 1)
                                for m in range(TPI):
                                    last = pe.transpose(p_tr[m // 4][:, (m % 4) * P:(m % 4 + 1) * P],
                                                        AG[:, m * P:(m + 1) * P], ident[:])
                                    if m % 4 == 3:
                                        last.then_inc(turned, 1)
                                pe.wait_ge(moved, c * (2 + 2 * GROUPS) + 2 + 2 * g + 2)
                                for m in range(TPI):
                                    last = pe.matmul(p_s[:, bass.ds(g * CG, CG)], AGT[:, m, :],
                                                     VT[:, m, bass.ds(g * CG, CG)],
                                                     start=(m == 0), stop=(m == TPI - 1))
                                last.then_inc(applied, 1)
                            pe.wait_ge(sout, c + 1)
                            pe.transpose(p_st[:], S[:], ident[:]).then_inc(sturn, 1)
                            pe.wait_ge(stout, c + 1)
                            pe.wait_ge(added, c)
                            pe.matmul(p_o[:], opT[:], ST[:], start=True, stop=True).then_inc(projected, 1)
                pe.nop()


def token_norm(nc, d, X, XA):
    with ExitStack() as st:
        center = sb(nc, st, "n_center", [P, P])
        ones = sb(nc, st, "n_ones", [P, P])
        eps = sb(nc, st, "n_eps", [P, 1])
        sq = [sb(nc, st, f"n_sq{k}", [P, CH]) for k in range(4)]
        p_c = [ps(nc, st, f"n_pc{k}") for k in range(4)]
        p_v = [ps(nc, st, f"n_pv{k}") for k in range(4)]
        w_in = sem(nc, st, "n_w_in")
        cleared = sem(nc, st, "n_cleared")
        centered = sem(nc, st, "n_centered")
        squared = sem(nc, st, "n_squared")
        varied = sem(nc, st, "n_varied")
        rooted = sem(nc, st, "n_rooted")
        inverted = sem(nc, st, "n_inverted")
        written = sem(nc, st, "n_written")

        with nc.Block() as block:
            @block.sync
            def _(sp):
                sp.dma_start(center[:], d["c_center"]).then_inc(w_in, 16)
                sp.dma_start(ones[:], d["c_ones"]).then_inc(w_in, 16)

            @block.gpsimd
            def _(pool):
                nc.gpsimd.memset(eps[:], EPS).then_inc(cleared, 1)
                nc.gpsimd.memset(XA[:, :, 0:REACH], 0.0).then_inc(cleared, 1)
                nc.gpsimd.memset(XA[:, :, REACH + PIX:], 0.0).then_inc(cleared, 1)

            @block.tensor
            def _(pe):
                pe.wait_ge(w_in, 32)
                with pe.Fori(0, NCH // 4) as i:
                    pe.wait_ge(written, i * 4)
                    for k in range(4):
                        pe.matmul(p_c[k][:], center[:], X[:, bass.ds((i * 4 + k) * CH, CH)],
                                  start=True, stop=True).then_inc(centered, 1)
                    for k in range(4):
                        pe.wait_ge(squared, i * 4 + k + 1)
                        pe.matmul(p_v[k][:], ones[:], sq[k][:], start=True, stop=True).then_inc(varied, 1)

            @block.scalar
            def _(act):
                act.wait_ge(cleared, 3)
                with act.Fori(0, NCH // 4) as i:
                    for k in range(4):
                        act.wait_ge(centered, i * 4 + k + 1)
                        act.activation(sq[k][:], p_c[k][:], ACT.Square).then_inc(squared, 1)
                    for k in range(4):
                        act.wait_ge(varied, i * 4 + k + 1)
                        act.activation(sq[k][:], p_v[k][:], ACT.Sqrt, bias=eps[:]).then_inc(rooted, 1)

            @block.vector
            def _(dve):
                with dve.Fori(0, NCH // 4) as i:
                    for k in range(4):
                        c = i * 4 + k
                        dve.wait_ge(rooted, c + 1)
                        dve.reciprocal(sq[k][:], sq[k][:]).then_inc(inverted, 1)
                    for k in range(4):
                        c = i * 4 + k
                        dve.wait_ge(inverted, c + 1)
                        off = REACH + (k % 2) * CH
                        dve.tensor_tensor(XA[:, bass.ds(i * 2 + k // 2, 1), off:off + CH]
                                          .rearrange("p o w -> p (o w)"), p_c[k][:], sq[k][:],
                                          ALU.mult).then_inc(written, 1)


def attention(nc, d, XA):
    PADA = PIX + 2 * REACH
    NBLK = PIX // QB
    VW = DV + 1
    with ExitStack() as st:
        ident = sb(nc, st, "a_ident", [P, P])
        wq = sb(nc, st, "a_wq", [P, 2, P])
        wk = sb(nc, st, "a_wk", [P, 2, P])
        wv = sb(nc, st, "a_wv", [P, P])
        wo = sb(nc, st, "a_wo", [P, P])
        bq = sb(nc, st, "a_bq", [P, 2])
        bk = sb(nc, st, "a_bk", [P, 2])
        bv = sb(nc, st, "a_bv", [P, P])
        bo = sb(nc, st, "a_bo", [P, 1])
        bias = [sb(nc, st, f"a_bias{v}", [P, 4, 2, P]) for v in range(3)]
        XS = [sb(nc, st, f"a_XS{j}", [P, PADA]) for j in range(2)]
        QT = [sb(nc, st, f"a_QT{j}", [P, 2, PIX]) for j in range(2)]
        KT = [sb(nc, st, f"a_KT{j}", [P, 2, PADA]) for j in range(2)]
        V = [sb(nc, st, f"a_V{j}", [P, NBLK, HEADS, VW]) for j in range(2)]
        E = [sb(nc, st, f"a_E{b}", [P, HEADS, P]) for b in range(2)]
        PT = [sb(nc, st, f"a_PT{b}", [P, HEADS, P]) for b in range(2)]
        nm = sb(nc, st, "a_nm", [P, 2, HEADS])
        rsum = sb(nc, st, "a_rsum", [P, 2, HEADS])
        O = [sb(nc, st, f"a_O{b}", [P, P]) for b in range(2)]
        OT = [sb(nc, st, f"a_OT{j}", [P, PIX]) for j in range(2)]
        p_s = ps(nc, st, "a_ps", (P, 4, 4, P))
        p_t = ps(nc, st, "a_pt", (P, 2, 4, P))
        p_m = ps(nc, st, "a_pm")
        p_o = ps(nc, st, "a_po")

        w_in = sem(nc, st, "a_w_in")
        rel_in = sem(nc, st, "a_rel_in")
        masked = sem(nc, st, "a_masked")
        cleared = sem(nc, st, "a_cleared")
        staged = sem(nc, st, "a_staged")
        proj = sem(nc, st, "a_proj")
        proj_out = sem(nc, st, "a_proj_out")
        scored = sem(nc, st, "a_scored")
        biased = sem(nc, st, "a_biased")
        maxed = sem(nc, st, "a_maxed")
        powered = sem(nc, st, "a_powered")
        turned = sem(nc, st, "a_turned")
        pt_dve = sem(nc, st, "a_pt_dve")
        pt_act = sem(nc, st, "a_pt_act")
        mixed = sem(nc, st, "a_mixed")
        summed = sem(nc, st, "a_summed")
        scaled = sem(nc, st, "a_scaled")
        oturned = sem(nc, st, "a_oturned")
        ostored = sem(nc, st, "a_ostored")
        wo_done = sem(nc, st, "a_wo_done")
        written = sem(nc, st, "a_written")
        NPM = 14
        VHEAD = {r * 2 + hh: hh * 4 + r for r in range(4) for hh in range(2)}
        U2 = 2 * UNITS

        with nc.Block() as block:
            @block.sync
            def _(sp):
                for dst, src in ((ident, "c_ident"), (wq, "wq"), (wk, "wk"), (wv, "wv"), (wo, "wo"), (bq, "bq"),
                                 (bk, "bk"), (bo, "bo")):
                    sp.dma_start(dst[:], d[src]).then_inc(w_in, 16)
                sp.dma_start(bv[:], d["bv"].partition_broadcast(P)).then_inc(w_in, 16)
                sp.wait_ge(masked, 1)
                rel = d["rel_bias"].rearrange("(o hh r) w -> o r hh w", o=1, hh=2)
                for half in range(2):
                    for i in range(QB):
                        row = half * QB + i
                        sp.dma_start(bias[1][row:row + 1, :, :, i:i + 2 * REACH + 1], rel).then_inc(rel_in, 16)

            @block.gpsimd
            def _(pool):
                nc.gpsimd.memset(bias[1][:], NEG).then_inc(masked, 1)
                for j in range(2):
                    nc.gpsimd.memset(KT[j][:, :, 0:REACH], 0.0).then_inc(cleared, 1)
                    nc.gpsimd.memset(KT[j][:, :, REACH + PIX:], 0.0).then_inc(cleared, 1)
                    nc.gpsimd.memset(V[j][:, :, :, DV:VW], 1.0).then_inc(cleared, 1)

                def stage(n, j):
                    nc.gpsimd.tensor_copy(XS[j][:], XA[:, bass.ds(n, 1), :].rearrange("p o w -> p (o w)"))\
                      .then_inc(staged, 1)

                stage(0, 0)
                stage(1, 1)
                pool.wait_ge(rel_in, 16 * 2 * QB)
                for v in (0, 2):
                    nc.gpsimd.tensor_copy(bias[v][:], bias[1][:]).then_inc(masked, 1)
                pool.wait_ge(masked, 3)
                nc.gpsimd.memset(bias[0][0:QB, :, :, 0:REACH], NEG).then_inc(masked, 1)
                nc.gpsimd.memset(bias[2][QB:P, :, :, P - REACH:P], NEG).then_inc(masked, 1)
                with pool.Fori(1, IMAGES // 2) as i:
                    for j in range(2):
                        pool.wait_ge(written, (i * 2 + j - 1) * 2)
                        stage(i * 2 + j, j)

            @block.tensor
            def _(pe):
                pe.wait_ge(w_in, 16 * 9)
                pe.wait_ge(cleared, 6)

                def project(n, j, base):
                    pe.wait_ge(staged, n + 1)
                    k = 0
                    for w in (wq, wk):
                        for m in range(2):
                            for h in range(2):
                                pe.wait_ge(proj_out, base + k)
                                pe.matmul(p_m[:], w[:, m, :], XS[j][:, REACH + h * CH:REACH + (h + 1) * CH],
                                          start=True, stop=True).then_inc(proj, 1)
                                k += 1
                    for q in range(4):
                        pe.wait_ge(proj_out, base + k)
                        for b in range(4):
                            at = (q * 4 + b) * QB
                            last = pe.matmul(p_m[:, b * P:(b + 1) * P], XS[j][:, at:at + P], wv[:],
                                             start=True, stop=True)
                        last.then_inc(proj, 1)
                        k += 1

                def scores(g, u):
                    j, v = u // UNITS, u % UNITS
                    pe.wait_ge(biased, g + u)
                    for r in range(4):
                        for hh in range(2):
                            for half in range(2):
                                q0 = (2 * v + half) * QB
                                last = pe.matmul(p_s[half * QB:(half + 1) * QB, r, hh, :],
                                                 QT[j][r * DK:(r + 1) * DK, hh, q0:q0 + QB],
                                                 KT[j][r * DK:(r + 1) * DK, hh, q0:q0 + P],
                                                 start=True, stop=True)
                    last.then_inc(scored, 1)

                def turn(g, u):
                    for b in range(2):
                        for k in range(4):
                            o = b * 4 + k
                            pe.wait_ge(powered, (g + u) * HEADS + o + 1)
                            if k == 0:
                                pe.wait_ge((pt_dve, pt_act)[b], g + u)
                            last = pe.transpose(p_t[:, b, k, :], E[u % 2][:, o, :], ident[:])
                        last.then_inc(turned, 1)

                def mix(g, u):
                    j, v = u // UNITS, u % UNITS
                    pe.wait_ge(pt_dve, g + u + 1)
                    pe.wait_ge(pt_act, g + u + 1)
                    pe.wait_ge(scaled, g + u)
                    pe.wait_ge(ostored, g + u)
                    for o in range(HEADS):
                        hd = VHEAD[o]
                        for half in range(2):
                            last = pe.matmul(p_o[half * QB:(half + 1) * QB,
                                                 hd * VW:(hd + 1) * VW],
                                             PT[u % 2][:, o, half * QB:(half + 1) * QB],
                                             V[j][:, 2 * v + half, hd, :], start=True, stop=True)
                    last.then_inc(mixed, 1)

                def turn_out(g, u):
                    pe.wait_ge(scaled, g + u + 1)
                    pe.wait_ge(ostored, g + u)
                    pe.transpose(p_o[:, HEADS * VW:HEADS * VW + P], O[u % 2][:], ident[:])\
                      .then_inc(oturned, 1)

                def output(n, j, base):
                    pe.wait_ge(ostored, n * UNITS + UNITS)
                    for h in range(2):
                        if h:
                            pe.wait_ge(written, n * 2 + 1)
                        else:
                            pe.wait_ge(proj_out, base)
                            pe.wait_ge(written, n * 2)
                        pe.matmul(p_m[:], wo[:], OT[j][:, h * CH:(h + 1) * CH], start=True, stop=True)\
                          .then_inc(wo_done, 1)

                with pe.Fori(0, IMAGES // 2) as i:
                    n, g = i * 2, i * U2
                    pe.wait_ge(written, n * 2)
                    project(n, 0, n * 12)
                    pe.wait_ge(proj_out, n * 12 + 12)
                    scores(g, 0)
                    for u in range(U2 + 2):
                        if u == 3:
                            project(n + 1, 1, n * 12 + 12)
                        if u + 1 == UNITS:
                            pe.wait_ge(proj_out, n * 12 + 24)
                        if u >= 2:
                            turn_out(g, u - 2)
                        if u + 1 < U2:
                            scores(g, u + 1)
                        if u < U2:
                            turn(g, u)
                        if 1 <= u <= U2:
                            mix(g, u - 1)
                        if u - 2 == UNITS - 1:
                            output(n, 0, n * 12 + 24)
                    output(n + 1, 1, n * 12 + 24)

            @block.scalar
            def _(act):
                act.wait_ge(w_in, 16 * 9)

                def project(n, j, base):
                    k = 0
                    for dst, off, b in ((QT, 0, bq), (KT, REACH, bk)):
                        for m in range(2):
                            for h in range(2):
                                act.wait_ge(proj, base + k + 1)
                                act.activation(dst[j][:, m, off + h * CH:off + (h + 1) * CH], p_m[:],
                                               ACT.Identity, bias=b[:, m:m + 1]).then_inc(proj_out, 1)
                                k += 1

                def exps(g, u):
                    act.wait_ge(maxed, g + u + 1)
                    for o in range(HEADS):
                        act.activation(E[u % 2][:, o, :], E[u % 2][:, o, :], ACT.Exp,
                                       bias=nm[:, u % 2, o:o + 1]).then_inc(powered, 1)

                def copy_pt(g, u):
                    act.wait_ge(turned, (g + u) * 2 + 2)
                    if u >= 2:
                        act.wait_ge(mixed, g + u - 1)
                    act.activation(PT[u % 2][:, 4:8, :], p_t[:, 1], ACT.Copy).then_inc(pt_act, 1)

                def copy_out(g, u):
                    act.wait_ge(oturned, g + u + 1)
                    act.activation(OT[u // UNITS][:, (u % UNITS) * P:(u % UNITS + 1) * P],
                                   p_o[:, HEADS * VW:HEADS * VW + P], ACT.Copy).then_inc(ostored, 1)

                with act.Fori(0, IMAGES // 2) as i:
                    n, g = i * 2, i * U2
                    act.wait_ge(wo_done, n * 2)
                    act.wait_ge(mixed, g)
                    project(n, 0, n * 12)
                    exps(g, 0)
                    for u in range(U2 + 2):
                        if u == 3:
                            project(n + 1, 1, n * 12 + 12)
                        if u >= 2:
                            copy_out(g, u - 2)
                        if u + 1 < U2:
                            exps(g, u + 1)
                        if u < U2:
                            copy_pt(g, u)

            @block.vector
            def _(dve):
                dve.wait_ge(w_in, 16 * 9)
                dve.wait_ge(cleared, 6)
                dve.wait_ge(masked, 5)

                def values(n, j, base):
                    for q in range(4):
                        dve.wait_ge(proj, base + 8 + q + 1)
                        dve.tensor_tensor(V[j][:, q * 4:(q + 1) * 4, :, 0:DV],
                                          p_m[:].rearrange("p (b h w) -> p b h w", b=4, h=HEADS),
                                          bv[:].rearrange("p (o h w) -> p o h w", o=1, h=HEADS)
                                          .to_broadcast([P, 4, HEADS, DV]), ALU.add).then_inc(proj_out, 1)

                def soft(g, u):
                    v = u % UNITS
                    which = 0 if v == 0 else 2 if v == UNITS - 1 else 1
                    dve.wait_ge(scored, g + u + 1)
                    if u >= 2:
                        dve.wait_ge(turned, (g + u - 1) * 2)
                    dve.scalar_tensor_tensor(
                        E[u % 2][:].rearrange("p (r h) w -> p r (h w)", r=4),
                        p_s[:, :, 0:2].rearrange("p r h w -> p r (h w)"), float(DK) ** -0.5,
                        bias[which][:].rearrange("p r h w -> p r (h w)"), ALU.mult, ALU.add)\
                       .then_inc(biased, 1)
                    dve.wait_ge(biased, g + u + 1)
                    dve.tensor_reduce(nm[:, u % 2, :], E[u % 2][:], AX.X, ALU.max, negate=True)\
                       .then_inc(maxed, 1)

                def copy_pt(g, u):
                    dve.wait_ge(turned, (g + u) * 2 + 1)
                    if u >= 2:
                        dve.wait_ge(mixed, g + u - 1)
                    dve.tensor_copy(PT[u % 2][:, 0:4, :], p_t[:, 0]).then_inc(pt_dve, 1)

                def scale(g, u):
                    dve.wait_ge(mixed, g + u + 1)
                    if u >= 2:
                        dve.wait_ge(oturned, g + u - 1)
                    po = p_o[:, 0:HEADS * VW].rearrange("p (h w) -> p h w", h=HEADS)
                    dve.reciprocal(rsum[:, u % 2, :], po[:, :, DV]).then_inc(summed, 1)
                    dve.wait_ge(summed, g + u + 1)
                    dve.tensor_tensor(O[u % 2][:].rearrange("p (h w) -> p h w", h=HEADS), po[:, :, 0:DV],
                                      rsum[:, u % 2, :].rearrange("p (h o) -> p h o", o=1)
                                      .to_broadcast([P, HEADS, DV]), ALU.mult).then_inc(scaled, 1)

                def output(n, j):
                    for h in range(2):
                        dve.wait_ge(wo_done, n * 2 + h + 1)
                        cols = slice(REACH + h * CH, REACH + (h + 1) * CH)
                        dve.scalar_tensor_tensor(XA[:, bass.ds(n, 1), cols].rearrange("p o w -> p (o w)"),
                                                 p_m[:], bo[:], XS[j][:, cols], ALU.add, ALU.add)\
                           .then_inc(written, 1)

                with dve.Fori(0, IMAGES // 2) as i:
                    n, g = i * 2, i * U2
                    dve.wait_ge(mixed, g)
                    dve.wait_ge(turned, g * 2)
                    values(n, 0, n * 12)
                    soft(g, 0)
                    for u in range(U2 + 2):
                        if u == 3:
                            values(n + 1, 1, n * 12 + 12)
                        if u + 1 < U2:
                            soft(g, u + 1)
                        if u < U2:
                            copy_pt(g, u)
                        if 1 <= u <= U2:
                            scale(g, u - 1)
                        if u - 2 == UNITS - 1:
                            output(n, 0)
                    output(n + 1, 1)


def middle(nc, d, X, XA, H, XN):
    W4 = 4
    NPE, NACT, NDVE = 9, 10, 10
    with ExitStack() as st:
        center = sb(nc, st, "m_center", [P, P])
        ones = sb(nc, st, "m_ones", [P, P])
        lin = sb(nc, st, "m_lin", [P, P])
        vec = sb(nc, st, "m_vec", [P, 5])
        g1, b1, bl, g2, b2 = (vec[:, k:k + 1] for k in range(5))
        eps = sb(nc, st, "m_eps", [P, 1])
        sq = [sb(nc, st, f"m_sq{k}", [P, CH]) for k in range(W4)]
        xs = [sb(nc, st, f"m_xs{k}", [P, CH]) for k in range(W4)]
        y = [sb(nc, st, f"m_y{k}", [P, CH]) for k in range(W4)]
        p_a = [ps(nc, st, f"m_pa{k}") for k in range(W4)]
        p_v = [ps(nc, st, f"m_pv{k}") for k in range(W4)]
        w_in = sem(nc, st, "m_w_in")
        cleared = sem(nc, st, "m_cleared")
        pe_stage = sem(nc, st, "m_pe_stage")
        act_stage = sem(nc, st, "m_act_stage")
        dve_stage = sem(nc, st, "m_dve_stage")

        def pe_at(i, s, k):
            return i * (NPE * W4) + s * W4 + k + 1

        def act_at(i, s, k):
            return i * (NACT * W4) + s * W4 + k + 1

        def dve_at(i, s, k):
            return i * (NDVE * W4) + s * W4 + k + 1

        def cols(buf, i, k):
            return buf[:, bass.ds((i * W4 + k) * CH, CH)]

        with nc.Block() as block:
            @block.sync
            def _(sp):
                for dst, src in ((center, "c_center"), (ones, "c_ones"), (lin, "w_lin"), (vec, "mid_vec")):
                    sp.dma_start(dst[:], d[src]).then_inc(w_in, 16)

            @block.gpsimd
            def _(pool):
                nc.gpsimd.memset(eps[:], EPS).then_inc(cleared, 1)

            @block.tensor
            def _(pe):
                pe.wait_ge(w_in, 64)
                with pe.Fori(0, NCH // W4) as i:
                    pe.wait_ge(dve_stage, i * (NDVE * W4))
                    for s in range(NPE):
                        for k in range(W4):
                            off = REACH + (k % 2) * CH
                            if s == 0:
                                w, x, o = center, XA[:, bass.ds(i * 2 + k // 2, 1), off:off + CH]\
                                    .rearrange("p o w -> p (o w)"), p_a
                            elif s == 1:
                                pe.wait_ge(act_stage, act_at(i, 0, k))
                                w, x, o = ones, sq[k][:], p_v
                            elif s == 2:
                                pe.wait_ge(act_stage, act_at(i, 2, k))
                                w, x, o = lin, xs[k][:], p_a
                            elif s == 3:
                                pe.wait_ge(dve_stage, dve_at(i, 2, k))
                                w, x, o = center, y[k][:], p_a
                            elif s == 4:
                                pe.wait_ge(act_stage, act_at(i, 4, k))
                                w, x, o = ones, sq[k][:], p_v
                            elif s == 5:
                                pe.wait_ge(dve_stage, dve_at(i, 5, k))
                                w, x, o = center, cols(X, i, k), p_a
                            elif s == 6:
                                pe.wait_ge(act_stage, act_at(i, 6, k))
                                w, x, o = ones, sq[k][:], p_v
                            elif s == 7:
                                pe.wait_ge(dve_stage, dve_at(i, 7, k))
                                w, x, o = center, cols(H, i, k), p_a
                            else:
                                pe.wait_ge(act_stage, act_at(i, 8, k))
                                w, x, o = ones, sq[k][:], p_v
                            pe.matmul(o[k][:], w[:], x, start=True, stop=True).then_inc(pe_stage, 1)

            @block.scalar
            def _(act):
                act.wait_ge(cleared, 1)
                act.wait_ge(w_in, 64)
                with act.Fori(0, NCH // W4) as i:
                    for s in range(NACT):
                        for k in range(W4):
                            if s == 2:
                                act.wait_ge(dve_stage, dve_at(i, 1, k))
                                ins = act.activation(xs[k][:], xs[k][:], ACT.Identity, bias=b1)
                            elif s == 3:
                                act.wait_ge(pe_stage, pe_at(i, 2, k))
                                ins = act.activation(y[k][:], p_a[k][:], ACT.Relu, bias=bl)
                            elif s in (0, 4, 6, 8):
                                act.wait_ge(pe_stage, pe_at(i, {0: 0, 4: 3, 6: 5, 8: 7}[s], k))
                                ins = act.activation(sq[k][:], p_a[k][:], ACT.Square)
                            else:
                                act.wait_ge(pe_stage, pe_at(i, {1: 1, 5: 4, 7: 6, 9: 8}[s], k))
                                ins = act.activation(sq[k][:], p_v[k][:], ACT.Sqrt, bias=eps[:])
                            ins.then_inc(act_stage, 1)

            @block.vector
            def _(dve):
                dve.wait_ge(w_in, 64)
                with dve.Fori(0, NCH // W4) as i:
                    for s in range(NDVE):
                        for k in range(W4):
                            if s in (0, 3, 6, 8):
                                dve.wait_ge(act_stage, act_at(i, {0: 1, 3: 5, 6: 7, 8: 9}[s], k))
                                ins = dve.reciprocal(sq[k][:], sq[k][:])
                            elif s == 2:
                                dve.wait_ge(act_stage, act_at(i, 3, k))
                                ins = dve.tensor_tensor(y[k][:], xs[k][:], y[k][:], ALU.add)
                            else:
                                dve.wait_ge(dve_stage, dve_at(i, s - 1, k))
                                if s == 1:
                                    ins = dve.scalar_tensor_tensor(xs[k][:], p_a[k][:], g1, sq[k][:],
                                                                   ALU.mult, ALU.mult)
                                elif s == 4:
                                    ins = dve.scalar_tensor_tensor(y[k][:], p_a[k][:], g2, sq[k][:],
                                                                   ALU.mult, ALU.mult)
                                elif s == 5:
                                    ins = dve.scalar_tensor_tensor(cols(X, i, k), y[k][:], b2, cols(X, i, k),
                                                                   ALU.add, ALU.add)
                                else:
                                    ins = dve.tensor_tensor(cols(H if s == 7 else XN, i, k), p_a[k][:],
                                                            sq[k][:], ALU.mult)
                            ins.then_inc(dve_stage, 1)


def experts_dense(nc, d, X, H, XN):
    with ExitStack() as st:
        ident = sb(nc, st, "e_ident", [P, P])
        w1 = sb(nc, st, "e_w1", [P, EXPERTS, HID])
        w2 = sb(nc, st, "e_w2", [P, EXPERTS, HC, P])
        wr = sb(nc, st, "e_wr", [P, EXPERTS])
        br = sb(nc, st, "e_br", [EXPERTS, 1])
        lng = sb(nc, st, "e_lng", [P, EXPERTS])
        lnb = sb(nc, st, "e_lnb", [P, EXPERTS])
        b1 = sb(nc, st, "e_b1", [P, EXPERTS, HC])
        b2 = sb(nc, st, "e_b2", [P, EXPERTS])
        num = sb(nc, st, "e_num", [P, EXPERTS])
        LG = sb(nc, st, "e_LG", [P, CH])
        LT = sb(nc, st, "e_LT", [P, TPC, EXPERTS])
        top = sb(nc, st, "e_top", [P, TPC, 8])
        idx = sb(nc, st, "e_idx", [P, TPC, 8], U32)
        fidx = sb(nc, st, "e_fidx", [P, TPC, 8])
        dif = sb(nc, st, "e_dif", [P, TPC])
        ex = sb(nc, st, "e_ex", [P, TPC])
        sm = sb(nc, st, "e_sm", [P, TPC])
        wt = sb(nc, st, "e_wt", [P, 2, TPC])
        gate = sb(nc, st, "e_gate", [P, 2, TPC, EXPERTS])
        G = sb(nc, st, "e_G", [P, TPC, EXPERTS])
        NH = 4
        hs = [sb(nc, st, f"e_hs{i}", [P, CH]) for i in range(NH)]
        gs = [sb(nc, st, f"e_gs{i}", [P, CH]) for i in range(2)]
        wy = [sb(nc, st, f"e_wy{i}", [P, CH]) for i in range(2)]
        p_h = [ps(nc, st, f"e_ph{i}") for i in range(3)]
        p_y = [ps(nc, st, f"e_py{i}") for i in range(2)]
        p_g = [ps(nc, st, f"e_pg{i}") for i in range(2)]
        p_r = ps(nc, st, "e_pr")
        w_in = sem(nc, st, "e_w_in")
        cleared = sem(nc, st, "e_cleared")
        folded = sem(nc, st, "e_folded")
        bsum = sem(nc, st, "e_bsum")
        logit = sem(nc, st, "e_logit")
        lout = sem(nc, st, "e_lout")
        lturn = sem(nc, st, "e_lturn")
        rstep = sem(nc, st, "e_rstep")
        lmax = sem(nc, st, "e_lmax")
        lidx = sem(nc, st, "e_lidx")
        half = sem(nc, st, "e_half")
        power = sem(nc, st, "e_power")
        gated = sem(nc, st, "e_gated")
        gturn = sem(nc, st, "e_gturn")
        gout = sem(nc, st, "e_gout")
        hid = sem(nc, st, "e_hid")
        gelu = sem(nc, st, "e_gelu")
        down = sem(nc, st, "e_down")
        ydone = sem(nc, st, "e_ydone")
        weighted = sem(nc, st, "e_weighted")
        addx = sem(nc, st, "e_addx")
        NW = 10
        PER = EXPERTS * HC
        RS = 6

        with nc.Block() as block:
            @block.sync
            def _(sp):
                for dst, src in ((ident, "c_ident"), (w1, "w1"), (w2, "w2"), (wr, "wr"), (br, "br"), (lng, "ln_g"),
                                 (lnb, "ln_b"), (b1, "b1"), (b2, "b2"), (num, "c_number")):
                    sp.dma_start(dst[:], d[src]).then_inc(w_in, 16)

            @block.gpsimd
            def _(pool):
                nc.gpsimd.memset(LG[:], 0.0).then_inc(cleared, 1)

            @block.tensor
            def _(pe):
                pe.wait_ge(w_in, 16 * NW)
                for e in range(EXPERTS):
                    for q in range(HC):
                        last = pe.matmul(p_r[:, e * HC + q:e * HC + q + 1], w1[:, e, q * P:(q + 1) * P],
                                         lnb[:, e:e + 1], start=True, stop=True)
                last.then_inc(bsum, 1)
                pe.wait_ge(folded, EXPERTS + 1)
                with pe.Fori(0, NCH) as c:
                    pe.wait_ge(rstep, c * RS)
                    pe.matmul(p_r[0:EXPERTS, :], wr[:], H[:, bass.ds(c * CH, CH)], start=True, stop=True)\
                      .then_inc(logit, 1)
                    pe.wait_ge(lout, c + 1)
                    for t in range(TPC):
                        last = pe.transpose(p_r[:, t * P:(t + 1) * P], LG[:, t * P:(t + 1) * P], ident[:])
                    last.then_inc(lturn, 1)
                    pe.wait_ge(gated, c + 1)

                    def up(m):
                        e, q = m // HC, m % HC
                        if m % HC == 0:
                            if e >= 2:
                                pe.wait_ge(gout, c * EXPERTS + e - 1)
                            for t in range(TPC):
                                last = pe.transpose(p_g[e % 2][:, t * P:(t + 1) * P],
                                                    G[:, t, e:e + 1].to_broadcast([P, P]), ident[:])
                            last.then_inc(gturn, 1)
                        if m >= 3:
                            pe.wait_ge(gelu, c * PER + m - 2)
                        else:
                            pe.wait_ge(gelu, c * PER)
                        pe.matmul(p_h[m % 3][:], w1[:, e, q * P:(q + 1) * P], XN[:, bass.ds(c * CH, CH)],
                                  start=True, stop=True).then_inc(hid, 1)

                    def dn(m):
                        e, q = m // HC, m % HC
                        pe.wait_ge(gelu, c * PER + m + 1)
                        if q == 0:
                            pe.wait_ge(weighted, c * EXPERTS + max(e - 1, 0))
                        ins = pe.matmul(p_y[e % 2][:], w2[:, e, q, :], hs[m % NH][:],
                                        start=(q == 0), stop=(q == HC - 1))
                        ins.then_inc(down, 1)

                    for m in range(PER + 2):
                        if m < PER:
                            up(m)
                        if m >= 2:
                            dn(m - 2)

            @block.scalar
            def _(act):
                act.wait_ge(w_in, 16 * NW)
                act.wait_ge(folded, EXPERTS + 1)
                act.wait_ge(cleared, 1)
                with act.Fori(0, NCH) as c:
                    act.wait_ge(logit, c + 1)
                    act.activation(LG[0:EXPERTS, :], p_r[0:EXPERTS, :], ACT.Identity, bias=br[:]).then_inc(lout, 1)
                    act.wait_ge(rstep, c * RS + 2)
                    act.activation(ex[:], dif[:], ACT.Exp).then_inc(power, 1)
                    for m in range(PER):
                        e, q = m // HC, m % HC
                        if q == 0:
                            act.wait_ge(gturn, c * EXPERTS + e + 1)
                            act.wait_ge(weighted, c * EXPERTS + max(e - 1, 0))
                            act.activation(gs[e % 2][:], p_g[e % 2][:], ACT.Copy).then_inc(gout, 1)
                        act.wait_ge(hid, c * PER + m + 1)
                        act.wait_ge(down, c * PER + max(m - NH + 1, 0))
                        act.activation(hs[m % NH][:], p_h[m % 3][:], ACT.Gelu, bias=b1[:, e, q:q + 1])\
                           .then_inc(gelu, 1)

            @block.vector
            def _(dve):
                dve.wait_ge(w_in, 16 * NW)
                dve.wait_ge(bsum, 1)
                for e in range(EXPERTS):
                    dve.tensor_scalar(w1[:, e, :], w1[:, e, :], lng[:, e:e + 1], None, ALU.mult).then_inc(folded, 1)
                dve.tensor_tensor(b1[:].rearrange("p e q -> p (e q)"), b1[:].rearrange("p e q -> p (e q)"),
                                  p_r[:, 0:PER], ALU.add).then_inc(folded, 1)
                with dve.Fori(0, NCH) as c:
                    dve.wait_ge(lturn, c + 1)
                    dve.tensor_copy(LT[:], p_r[:].rearrange("p (t e) -> p t e", t=TPC)[:, :, 0:EXPERTS]).then_inc(rstep, 1)
                    dve.wait_ge(rstep, c * RS + 1)
                    dve.tensor_copy(sm[:, 0:1], LT[:, 0, 0:1])
                    for t in range(TPC):
                        dve.max(top[:, t, :], LT[:, t, :]).then_inc(lmax, 1)
                    dve.wait_ge(lmax, c * TPC + TPC)
                    dve.tensor_tensor(dif[:], top[:, :, 1], top[:, :, 0], ALU.subtract).then_inc(rstep, 1)
                    for t in range(TPC):
                        ins = dve.max_index(idx[:, t, :], top[:, t, :], LT[:, t, :])
                    ins.then_inc(lidx, 1)
                    dve.wait_ge(lidx, c + 1)
                    dve.tensor_copy(fidx[:], idx[:]).then_inc(rstep, 1)
                    dve.wait_ge(power, c + 1)
                    dve.tensor_scalar(sm[:], ex[:], 1.0, None, ALU.add).then_inc(rstep, 1)
                    dve.wait_ge(rstep, c * RS + 4)
                    dve.reciprocal(wt[:, 0, :], sm[:]).then_inc(rstep, 1)
                    dve.wait_ge(rstep, c * RS + 5)
                    dve.tensor_tensor(wt[:, 1, :], ex[:], wt[:, 0, :], ALU.mult).then_inc(rstep, 1)
                    dve.wait_ge(rstep, c * RS + 6)
                    for s in range(2):
                        for t in range(TPC):
                            ins = dve.tensor_scalar(gate[:, s, t, :], num[:], fidx[:, t, s:s + 1],
                                                    wt[:, s, t:t + 1], ALU.is_equal, ALU.mult)
                    ins.then_inc(half, 1)
                    dve.wait_ge(half, c + 1)
                    dve.wait_ge(gturn, c * EXPERTS)
                    dve.tensor_tensor(G[:], gate[:, 0], gate[:, 1], ALU.add).then_inc(gated, 1)
                    cols = X[:, bass.ds(c * CH, CH)]
                    for e in range(EXPERTS):
                        dve.wait_ge(down, c * PER + (e + 1) * HC)
                        dve.wait_ge(gout, c * EXPERTS + e + 1)
                        dve.scalar_tensor_tensor(wy[e % 2][:], p_y[e % 2][:], b2[:, e:e + 1], gs[e % 2][:],
                                                 ALU.add, ALU.mult).then_inc(weighted, 1)
                        dve.wait_ge(weighted, c * EXPERTS + e + 1)
                        dve.wait_ge(addx, c * EXPERTS + e)
                        dve.tensor_tensor(cols, cols, wy[e % 2][:], ALU.add).then_inc(addx, 1)


def store(nc, X, out):
    with ExitStack() as st:
        done = sem(nc, st, "out_done")
        with nc.Block() as block:
            @block.sync
            def _(sp):
                for n in range(IMAGES):
                    sp.dma_start(out[n], X[:, n * PIX:(n + 1) * PIX]).then_inc(done, 16)
                sp.wait_ge(done, 16 * IMAGES)


def program(nc, d, out, dbg=None):
    with ExitStack() as st:
        X = sb(nc, st, "X", [P, TOK])
        with ExitStack() as st1:
            VP = sb(nc, st1, "VP", [P, IMAGES, PAD5, PAD5])
            OM = sb(nc, st1, "OM", [P, TOK // P, 3 * GK])
            flag = sb(nc, st1, "flag", [1, 1], I32)
            front(nc, d, X, VP, OM, flag)
            if dbg: dbg("front", dict(VP=VP, OM=OM, flag=flag))
            sample_fast(nc, d, X, VP, OM)
            sample_general(nc, d, X, VP, OM, flag)
            if dbg: dbg("fast", dict(X=X))
        H = sb(nc, st, "H", [P, TOK])
        with ExitStack() as st1:
            XA = sb(nc, st1, "XA", [P, IMAGES, PIX + 2 * REACH])
            token_norm(nc, d, X, XA)
            if dbg: dbg("ln", dict(XA=XA))
            attention(nc, d, XA)
            if dbg: dbg("attn", dict(XA=XA))
            with ExitStack() as st2:
                XN = sb(nc, st2, "XN", [P, TOK])
                middle(nc, d, X, XA, H, XN)
                if dbg: dbg("mid", dict(X=X, H=H, XN=XN))
                experts_dense(nc, d, X, H, XN)
                if dbg: dbg("end", dict(X=X))
        if out is not None:
            store(nc, X, out)


def arrays_of(inp):
    import numpy as np

    n = {}
    n["x"] = np.ascontiguousarray(inp["x"]).reshape(IMAGES, P, PIX)
    g = lambda k: np.ascontiguousarray(inp[k])
    n["dw_w"] = g("L0_conv_dw_w").reshape(P, K)
    n["dw_b"] = g("L0_conv_dw_b").reshape(P, 1)
    om = g("L0_conv_om_w").reshape(GROUPS, 3 * K, P)
    ob = g("L0_conv_om_b").reshape(GROUPS, 3 * K)
    parts = [slice(0, 2 * K, 2), slice(1, 2 * K, 2), slice(2 * K, 3 * K)]
    n["om_wT"] = np.ascontiguousarray(np.concatenate([om[:, s].reshape(GK, P) for s in parts]).T)
    n["om_b"] = np.concatenate([ob[:, s].reshape(GK) for s in parts])
    n["vp_wT"] = np.ascontiguousarray(g("L0_conv_vp_w").T)
    n["vp_b"] = g("L0_conv_vp_b").reshape(P, 1)
    n["op_wT"] = np.ascontiguousarray(g("L0_conv_op_w").T)
    n["c_ident"] = np.eye(P, dtype=np.float32)
    n["c_group4"] = np.kron(np.eye(P // 4), np.full((4, 4), 0.25)).astype(np.float32)
    sel = np.zeros((3, GROUPS, 5, 5, P), np.float32)
    for g_ in range(GROUPS):
        for b in range(5):
            sel[:, g_, b, b, g_ * CG:(g_ + 1) * CG] = 1
    n["c_select"] = sel.reshape(3 * GROUPS * 5, 5, P)
    n["c_center"] = (np.eye(P) - np.full((P, P), 1 / P)).astype(np.float32)
    n["c_ones"] = np.full((P, P), 1 / P, np.float32)
    n["wq"] = g("L1_attn_Wq").reshape(P, 2, P)
    n["wk"] = g("L1_attn_Wk").reshape(P, 2, P)
    n["wv"], n["wo"] = g("L1_attn_Wv"), g("L1_attn_Wo")
    n["bq"] = np.ascontiguousarray(g("L1_attn_bq").reshape(2, P).T)
    n["bk"] = np.ascontiguousarray(g("L1_attn_bk").reshape(2, P).T)
    n["bv"], n["bo"] = g("L1_attn_bv"), g("L1_attn_bo").reshape(P, 1)
    n["rel_bias"] = g("L1_attn_rel_bias")
    n["w_lin"] = g("L1_attn_W_lin")
    n["mid_vec"] = np.stack([g("L1_attn_" + k) for k in ("ln1_g", "ln1_b", "b_lin", "ln2_g", "ln2_b")], -1)
    n["w1"] = np.ascontiguousarray(g("L1_ffn_W1").transpose(1, 0, 2))
    n["w2"] = np.ascontiguousarray(g("L1_ffn_W2").reshape(EXPERTS, HC, P, P).transpose(2, 0, 1, 3))
    n["wr"], n["br"] = g("L1_ffn_Wr"), g("L1_ffn_br").reshape(EXPERTS, 1)
    n["ln_g"] = np.ascontiguousarray(g("L1_ffn_ln_g").T)
    n["ln_b"] = np.ascontiguousarray(g("L1_ffn_ln_b").T)
    n["b1"] = np.ascontiguousarray(g("L1_ffn_b1").reshape(EXPERTS, HC, P).transpose(2, 0, 1))
    n["b2"] = np.ascontiguousarray(g("L1_ffn_b2").T)
    n["c_number"] = np.broadcast_to(np.arange(EXPERTS, dtype=np.float32), (P, EXPERTS)).copy()
    n["c_line"] = np.broadcast_to(np.arange(SIDE, dtype=np.float32), (P, SIDE)).copy()
    tok = np.arange(PIX).reshape(PIX // P, P).T
    n["c_pixel"] = np.stack([tok // SIDE, tok % SIDE], -1).astype(np.float32)
    point = np.tile(np.arange(K), GROUPS)
    kern = np.stack([point // 3 - 1, point % 3 - 1]).astype(np.float32)
    n["c_kernel"] = np.broadcast_to(kern, (P, 2, GK)).copy()
    return n


def kernel(**inputs):
    import numpy as np
    import concourse.bacc as bacc
    from concourse.bass_utils import run_bass_kernel_spmd

    nc = bacc.Bacc("TRN2", target_bir_lowering=False, num_devices=1)
    arrays = arrays_of(inputs)
    d = {k: nc.dram_tensor("in_" + k, list(a.shape), mybir.dt.from_np(a.dtype), kind="ExternalInput").ap()
         for k, a in arrays.items()}
    out = nc.dram_tensor("out", [IMAGES, P, PIX], F32, kind="ExternalOutput").ap()
    program(nc, d, out)
    r = run_bass_kernel_spmd(nc, [{"in_" + k: a for k, a in arrays.items()}], core_ids=[0])
    return r.results[0]["out"].reshape(IMAGES, P, SIDE, SIDE)
```

```python
from contextlib import ExitStack

import concourse.bass as bass
from concourse import mybir

ALU = mybir.AluOpType
ACT = mybir.ActivationFunctionType
AX = mybir.AxisListType
F32 = mybir.dt.float32
I32 = mybir.dt.int32
BF16 = mybir.dt.bfloat16
U32 = mybir.dt.uint32

P = 128
IMAGES, SIDE = 8, 32
PIX = SIDE * SIDE
TOK = IMAGES * PIX
CH = 512
HALF = SIDE // 2
NCH = TOK // CH
TPC = CH // P
GROUPS, CG, K = 8, 16, 9
GK = GROUPS * K
WIN5 = 25
PAD3, PAD5 = SIDE + 2, SIDE + 4
HEADS, DK, DV = 8, 32, 16
REACH = 32
QB = 64
UNITS = PIX // (2 * QB)
EXPERTS, HID = 8, 512
HC = HID // P
NEG = -1e9
REGION = TOK + P
BLOCKS = 2 * TOK // P + EXPERTS
SPARE = EXPERTS
SLOTS = EXPERTS * REGION + SPARE * P
PADS = EXPERTS + SPARE
ROW = P + 4
EPS = 1e-5


class Ctx:

    def __init__(self, nc):
        self.nc = nc
        self.outer = ExitStack()

    def scope(self):
        return ExitStack()


def sb(nc, st, name, shape, dt=F32):
    return st.enter_context(nc.sbuf_tensor(name, shape, dt))


def ps(nc, st, name, shape=(P, CH), dt=F32):
    return st.enter_context(nc.psum_tensor(name, list(shape), dt))


def sem(nc, st, name):
    return st.enter_context(nc.semaphore(name))


def front(nc, d, X, VP, OM, flag):
    with ExitStack() as st:
        ident = sb(nc, st, "f_ident", [P, P])
        g4 = sb(nc, st, "f_g4", [P, P])
        vpT = sb(nc, st, "f_vpT", [P, P])
        omT = sb(nc, st, "f_omT", [P, 3 * GK])
        omb = sb(nc, st, "f_omb", [P, 3 * GK])
        dww = sb(nc, st, "f_dww", [P, K])
        dwb = sb(nc, st, "f_dwb", [P, 1])
        vpb = sb(nc, st, "f_vpb", [P, 1])
        stats = sb(nc, st, "f_stats", [P, IMAGES, 2, 6])
        mv = sb(nc, st, "f_mv", [P, IMAGES, 2])
        dev = sb(nc, st, "f_dev", [P, IMAGES])
        gmean = sb(nc, st, "f_gmean", [P, IMAGES])
        var = sb(nc, st, "f_var", [P, IMAGES])
        sd = sb(nc, st, "f_sd", [P, IMAGES])
        rs = sb(nc, st, "f_rs", [P, IMAGES])
        nb = sb(nc, st, "f_nb", [P, IMAGES])
        eps = sb(nc, st, "f_eps", [P, 1])
        xnp = [sb(nc, st, f"f_xnp{j}", [P, PAD3, PAD3]) for j in range(2)]
        omin = [sb(nc, st, f"f_omin{j}", [P, PIX]) for j in range(2)]
        fmax = sb(nc, st, "f_fmax", [P, IMAGES])
        fone = sb(nc, st, "f_fone", [P, 1])
        ftop = sb(nc, st, "f_ftop", [1, 1])

        p_stat = ps(nc, st, "f_pstat")
        p_val = [ps(nc, st, f"f_pval{h}") for h in range(2)]
        p_om = [ps(nc, st, f"f_pom{h}") for h in range(4)]

        x_in = [sem(nc, st, f"x_in{n}") for n in range(IMAGES)]
        w_in = sem(nc, st, "w_in")
        cleared = sem(nc, st, "f_cleared")
        stat = sem(nc, st, "f_stat")
        avg = sem(nc, st, "f_avg")
        rooted = sem(nc, st, "f_rooted")
        normed = sem(nc, st, "f_normed")
        val_done = sem(nc, st, "f_val_done")
        val_out = sem(nc, st, "f_val_out")
        tap_done = sem(nc, st, "f_tap_done")
        om_done = sem(nc, st, "f_om_done")
        om_out = sem(nc, st, "f_om_out")
        folded = sem(nc, st, "f_folded")

        with nc.Block() as block:
            @block.sync
            def _(sp):
                for n in range(IMAGES):
                    sp.dma_start(X[:, n * PIX:(n + 1) * PIX], d["x"][n]).then_inc(x_in[n], 16)
                for dst, src in ((ident, "c_ident"), (g4, "c_group4"), (vpT, "vp_wT"), (omT, "om_wT"),
                                 (dww, "dw_w"), (dwb, "dw_b"), (vpb, "vp_b")):
                    sp.dma_start(dst[:], d[src]).then_inc(w_in, 16)
                sp.dma_start(omb[:], d["om_b"].partition_broadcast(P)).then_inc(w_in, 16)

            @block.gpsimd
            def _(pool):
                for b in xnp:
                    nc.gpsimd.memset(b[:], 0.0).then_inc(cleared, 1)
                nc.gpsimd.memset(eps[:], EPS).then_inc(cleared, 1)
                nc.gpsimd.memset(VP[:], 0.0).then_inc(cleared, 1)

            @block.scalar
            def _(act):
                act.wait_ge(cleared, 4)
                act.wait_ge(avg, 2)
                act.activation(sd[:], p_stat[:, 8:16], ACT.Sqrt, bias=eps[:]).then_inc(rooted, 1)
                act.wait_ge(w_in, 16 * 8)
                act.wait_ge(stat, 5)
                def image(n, j, first):
                    if not first:
                        act.wait_ge(tap_done, (n - 1) * (2 * K))
                        act.wait_ge(val_done, (n - 1) * 2)
                    act.activation(xnp[j][:, 1:1 + SIDE, 1:1 + SIDE],
                                   X[:, bass.ds(n * PIX, PIX)].rearrange("p (a b) -> p a b", a=SIDE),
                                   ACT.Identity, bias=nb[:, bass.ds(n, 1)],
                                   scale=rs[:, bass.ds(n, 1)]).then_inc(normed, 1)
                    for h in range(2):
                        act.wait_ge(val_done, n * 2 + h + 1)
                        act.activation(
                            VP[:, bass.ds(n, 1), 2 + h * HALF:2 + (h + 1) * HALF, 2:2 + SIDE]
                            .rearrange("p o a b -> p (o a) b"),
                            p_val[h][:].rearrange("p (a b) -> p a b", a=HALF),
                            ACT.Identity, bias=vpb[:]).then_inc(val_out, 1)

                image(0, 0, True)
                image(1, 1, True)
                with act.Fori(1, IMAGES // 2) as i:
                    image(i * 2, 0, False)
                    image(i * 2 + 1, 1, False)

            @block.vector
            def _(dve):
                for n in range(IMAGES):
                    dve.wait_ge(x_in[n], 16)
                    for h in range(2):
                        last = dve.bn_stats(stats[:, n, h, :], X[:, n * PIX + h * CH:n * PIX + (h + 1) * CH])
                    last.then_inc(folded, 1)
                for n in range(IMAGES):
                    dve.wait_ge(folded, n + 1)
                    last = dve.bn_aggr(mv[:, n, :], stats[:, n, :, :])
                last.then_inc(stat, 1)
                dve.wait_ge(stat, 1)
                dve.wait_ge(avg, 1)
                dve.tensor_tensor(dev[:], mv[:, :, 0], p_stat[:, 0:8], ALU.subtract).then_inc(stat, 1)
                dve.tensor_copy(gmean[:], p_stat[:, 0:8]).then_inc(folded, 1)
                dve.wait_ge(stat, 2)
                dve.tensor_tensor(var[:], dev[:], dev[:], ALU.mult).then_inc(folded, 1)
                dve.wait_ge(folded, IMAGES + 2)
                dve.tensor_tensor(var[:], var[:], mv[:, :, 1], ALU.add).then_inc(stat, 1)
                dve.wait_ge(rooted, 1)
                dve.reciprocal(rs[:], sd[:]).then_inc(stat, 1)
                dve.wait_ge(stat, 4)
                dve.scalar_tensor_tensor(nb[:], gmean[:], -1.0, rs[:], ALU.mult, ALU.mult).then_inc(stat, 1)
                dve.wait_ge(w_in, 16 * 8)
                with dve.Fori(0, IMAGES // 2) as i:
                    for j in range(2):
                        n = i * 2 + j
                        dve.wait_ge(normed, n + 1)
                        dve.wait_ge(om_done, n * 4)
                        for k in range(K):
                            for h in range(2):
                                out = omin[j][:, h * CH:(h + 1) * CH].rearrange("p (a b) -> p a b", a=HALF)
                                src = xnp[j][:, k // 3 + h * HALF:k // 3 + (h + 1) * HALF, k % 3:k % 3 + SIDE]
                                if k == 0:
                                    ins = dve.tensor_scalar(out, src, dww[:, 0:1], dwb[:], ALU.mult, ALU.add)
                                else:
                                    dve.wait_ge(tap_done, n * (2 * K) + 2 * (k - 1) + h + 1)
                                    ins = dve.scalar_tensor_tensor(out, src, dww[:, k:k + 1], out,
                                                                   ALU.mult, ALU.add)
                                ins.then_inc(tap_done, 1)
                        for q in range(4):
                            dve.wait_ge(om_done, n * 4 + q + 1)
                            dve.tensor_tensor(
                                OM[:, bass.ds(n * 8 + 2 * q, 2), :],
                                p_om[q][:, 0:6 * GK].rearrange("p (t c) -> p t c", t=2),
                                omb[:].rearrange("p (t c) -> p t c", t=1).to_broadcast([P, 2, 3 * GK]),
                                ALU.add).then_inc(om_out, 1)
                        dve.wait_ge(om_out, n * 4 + 4)
                        dve.tensor_reduce(fmax[:, bass.ds(n, 1)], OM[:, bass.ds(n * 8, 8), 0:2 * GK],
                                          AX.XY, ALU.max, apply_absolute_value=True).then_inc(folded, 1)
                dve.wait_ge(folded, 2 * IMAGES + 2)
                dve.tensor_reduce(fone[:], fmax[:], AX.X, ALU.max).then_inc(stat, 1)
                dve.wait_ge(avg, 3)
                dve.tensor_reduce(ftop[:], p_stat[0:1, 0:P], AX.X, ALU.max).then_inc(stat, 1)
                dve.wait_ge(stat, 7)
                dve.tensor_scalar(flag[:], ftop[:], 1.0, None, ALU.is_gt).then_inc(stat, 1)

            @block.tensor
            def _(pe):
                pe.wait_ge(w_in, 16 * 8)
                pe.wait_ge(stat, 1)
                pe.matmul(p_stat[:, 0:8], g4[:], mv[:, :, 0], start=True, stop=True).then_inc(avg, 1)
                pe.wait_ge(stat, 3)
                pe.matmul(p_stat[:, 8:16], g4[:], var[:], start=True, stop=True).then_inc(avg, 1)
                with pe.Fori(0, IMAGES // 2) as i:
                    for j in range(2):
                        n = i * 2 + j
                        pe.wait_ge(normed, n + 1)
                        pe.wait_ge(val_out, n * 2)
                        for h in range(2):
                            pe.matmul(p_val[h][:], vpT[:],
                                      xnp[j][:, 1 + h * HALF:1 + (h + 1) * HALF, 1:1 + SIDE],
                                      start=True, stop=True).then_inc(val_done, 1)
                        pe.wait_ge(om_out, n * 4)
                        for q in range(4):
                            pe.wait_ge(tap_done, n * (2 * K) + 2 * (K - 1) + q // 2 + 1)
                            for t in range(2):
                                last = pe.matmul(p_om[q][:, t * 3 * GK:(t + 1) * 3 * GK],
                                                 omin[j][:, (2 * q + t) * P:(2 * q + t + 1) * P], omT[:],
                                                 start=True, stop=True)
                            last.then_inc(om_done, 1)
                pe.wait_ge(stat, 6)
                pe.transpose(p_stat[0:1, 0:P], fone[:], ident[:]).then_inc(avg, 1)


def sample_fast(nc, d, X, VP, OM):
    ROWS = 3 * GROUPS * 5
    with ExitStack() as st:
        identf = sb(nc, st, "s_identf", [P, P])
        ident = sb(nc, st, "s_ident", [P, P], BF16)
        sel = sb(nc, st, "s_sel", [ROWS, 5, P], BF16)
        self32 = sb(nc, st, "s_self32", [ROWS, 5, P])
        opT = sb(nc, st, "s_opT", [P, P])
        A = sb(nc, st, "s_A", [P, TPC, GROUPS, WIN5])
        MY = sb(nc, st, "s_MY", [P, 3, TPC, GK])
        PR = sb(nc, st, "s_PR", [P, 3, 3, TPC, GK])
        rest = sb(nc, st, "s_rest", [P, TPC, 5, GROUPS * 5])
        parts = sb(nc, st, "s_parts", [P, TPC, 5, 3, GROUPS * 5], BF16)
        AT = [sb(nc, st, f"s_AT{j}", [ROWS, 5, CH], BF16) for j in range(2)]
        prod_pe = [sb(nc, st, f"s_pp{i}", [P, CH]) for i in range(3)]
        prod_pool = [sb(nc, st, f"s_pq{i}", [P, CH]) for i in range(3)]
        acc = [sb(nc, st, f"s_acc{j}", [P, CH]) for j in range(2)]
        NB = 4
        p_bc = [ps(nc, st, f"s_pbc{i}") for i in range(NB)]
        p_out = [ps(nc, st, f"s_pout{j}") for j in range(2)]
        p_tr = [ps(nc, st, f"s_ptr{j}", (P, 2, CH), BF16) for j in range(2)]

        zero = sb(nc, st, "s_zero", [P, 1])

        w_in = sem(nc, st, "s_w_in")
        zeroed = sem(nc, st, "s_zeroed")
        cast = sem(nc, st, "s_cast")
        cleared = sem(nc, st, "s_cleared")
        step = sem(nc, st, "s_step")
        coef = sem(nc, st, "s_coef")
        high = sem(nc, st, "s_high")
        left = sem(nc, st, "s_left")
        mid = sem(nc, st, "s_mid")
        low = sem(nc, st, "s_low")
        turned = sem(nc, st, "s_turned")
        stored = sem(nc, st, "s_stored")
        bc = sem(nc, st, "s_bc")
        mul = sem(nc, st, "s_mul")
        summed = sem(nc, st, "s_summed")
        opm = sem(nc, st, "s_opm")
        outp = sem(nc, st, "s_outp")
        resid = sem(nc, st, "s_resid")
        NPE, NPO = (WIN5 + 1) // 2, WIN5 // 2
        STEPS = 5

        with nc.Block() as block:
            @block.sync
            def _(sp):
                sp.dma_start(identf[:], d["c_ident"]).then_inc(w_in, 16)
                sp.dma_start(opT[:], d["op_wT"]).then_inc(w_in, 16)
                sp.dma_start(self32[:], d["c_select"]).then_inc(w_in, 16)

            @block.gpsimd
            def _(pool):
                nc.gpsimd.memset(zero[:], 0.0).then_inc(zeroed, 1)
                nc.gpsimd.memset(A[:], 0.0).then_inc(cleared, 1)

                def chunk(c, j, first):
                    for m in range(1, NPO):
                        pool.wait_ge(mul, c * WIN5 + 2 * m + 2)
                        src = prod_pool[m % 3][:]
                        if m == 1:
                            if not first:
                                pool.wait_ge(outp, c - 1)
                            before = prod_pool[0][:]
                        else:
                            pool.wait_ge(summed, c * (NPO - 1) + m - 1)
                            before = acc[j][:]
                        nc.gpsimd.tensor_tensor(acc[j][:], before, src, ALU.add).then_inc(summed, 1)

                chunk(0, 0, True)
                chunk(1, 1, True)
                with pool.Fori(1, IMAGES) as n:
                    chunk(n * 2, 0, False)
                    chunk(n * 2 + 1, 1, False)

            @block.scalar
            def _(act):
                act.wait_ge(w_in, 48)
                act.wait_ge(zeroed, 1)
                act.activation(ident[:], identf[:], ACT.Copy).then_inc(cast, 1)
                act.activation(sel[:], self32[:], ACT.Copy).then_inc(cast, 1)

                def chunk(c, j, first):
                    act.wait_ge(coef, c * 9 + 9)
                    if not (isinstance(c, int) and c == 0):
                        act.wait_ge(turned, c * 3)
                    for t in range(TPC):
                        act.activation(parts[:, t, :, 0].rearrange("p q (g b) -> p q g b", b=5),
                                       A[:, t].rearrange("p g (q b) -> p q g b", b=5),
                                       ACT.Copy).then_inc(high, 1)
                    act.wait_ge(left, c * TPC + TPC)
                    act.activation(parts[:, :, :, 1], rest[:], ACT.Copy).then_inc(mid, 1)
                    act.activation(A[:].rearrange("p t g w -> p (t g w)"),
                                   zero[:].to_broadcast([P, TPC * GROUPS * WIN5]), ACT.Copy)\
                       .then_inc(cleared, 1)
                    if not first:
                        act.wait_ge(bc, (c - 1) * WIN5)
                    for q in range(0, 5, 2):
                        act.wait_ge(turned, c * 3 + q // 2 + 1)
                        w = min(2, 5 - q)
                        act.activation(AT[j][:, q:q + w], p_tr[(q // 2) % 2][0:ROWS, 0:w], ACT.Copy)\
                           .then_inc(stored, 1)

                chunk(0, 0, True)
                chunk(1, 1, True)
                with act.Fori(1, IMAGES) as n:
                    chunk(n * 2, 0, False)
                    chunk(n * 2 + 1, 1, False)

            @block.vector
            def _(dve):
                def weights(c, first):
                    om = OM[:, bass.ds(c * TPC, TPC), :]
                    oy, ox, m = om[:, :, 0:GK], om[:, :, GK:2 * GK], om[:, :, 2 * GK:3 * GK]
                    b = c * STEPS
                    dve.scalar_tensor_tensor(MY[:, 2], oy, 0.0, m, ALU.max, ALU.mult)
                    dve.scalar_tensor_tensor(MY[:, 0], oy, 0.0, m, ALU.min, ALU.mult).then_inc(step, 1)
                    dve.wait_ge(step, b + 1)
                    dve.tensor_tensor(MY[:, 1], m, MY[:, 2], ALU.subtract).then_inc(step, 1)
                    dve.wait_ge(step, b + 2)
                    dve.tensor_tensor(MY[:, 1], MY[:, 1], MY[:, 0], ALU.add).then_inc(step, 1)
                    dve.wait_ge(step, b + 3)
                    for r in range(3):
                        dve.scalar_tensor_tensor(PR[:, r, 2], ox, 0.0, MY[:, r], ALU.max, ALU.mult)
                    for r in range(3):
                        ins = dve.scalar_tensor_tensor(PR[:, r, 0], ox, 0.0, MY[:, r], ALU.min, ALU.mult)
                    ins.then_inc(step, 1)
                    dve.wait_ge(step, b + 4)
                    flat = "p r t k -> p r (t k)"
                    dve.tensor_tensor(PR[:, :, 1].rearrange(flat), MY[:].rearrange(flat),
                                      PR[:, :, 2].rearrange(flat), ALU.subtract).then_inc(step, 1)
                    dve.wait_ge(step, b + 5)
                    dve.tensor_tensor(PR[:, :, 1].rearrange(flat), PR[:, :, 1].rearrange(flat),
                                      PR[:, :, 0].rearrange(flat), ALU.add)
                    dve.wait_ge(cleared, c + 1)
                    win = A[:].rearrange("p t g (a b) -> p (t g) a b", a=5)
                    n = 0
                    for q in (0, 2, 1):
                        for r in range(3):
                            v = win[:, :, r:r + 3, q:q + 3]
                            w = PR[:, r, q].rearrange("p t (g a b) -> p (t g) a b", a=3, b=3)
                            if n:
                                dve.wait_ge(coef, c * 9 + n)
                            dve.tensor_tensor(v, v, w, ALU.subtract if (r == 0) != (q == 0) else ALU.add)\
                               .then_inc(coef, 1)
                            n += 1

                def split_rest(c):
                    for t in range(TPC):
                        dve.wait_ge(high, c * TPC + t + 1)
                        dve.tensor_tensor(rest[:, t].rearrange("p q (g b) -> p q g b", b=5),
                                          A[:, t].rearrange("p g (q b) -> p q g b", b=5),
                                          parts[:, t, :, 0].rearrange("p q (g b) -> p q g b", b=5),
                                          ALU.subtract).then_inc(left, 1)

                def split_low(c):
                    dve.wait_ge(mid, c + 1)
                    dve.tensor_tensor(parts[:, :, :, 2], rest[:], parts[:, :, :, 1], ALU.subtract)\
                       .then_inc(low, 1)

                def multiply(c, n, h, taps):
                    for t in taps:
                        dve.wait_ge(bc, c * WIN5 + t + 1)
                        m = t // 2
                        if t % 2 == 0:
                            out = prod_pe[m % 3]
                            if m >= 3 or m == 0:
                                dve.wait_ge(opm, c * NPE + max(m - 2, 0))
                        else:
                            out = prod_pool[m % 3]
                            if m >= 3 or m == 0:
                                dve.wait_ge(summed, c * (NPO - 1) + max(m - 3, min(m, 1)))
                        y, x = t // 5, t % 5
                        dve.tensor_tensor(
                            out[:].rearrange("p (a b) -> p a b", a=HALF),
                            p_bc[t % NB][:].rearrange("p (a b) -> p a b", a=HALF),
                            VP[:, bass.ds(n, 1), h * HALF + y:h * HALF + y + HALF, x:x + SIDE]
                            .rearrange("p o a b -> p (o a) b"),
                            ALU.mult).then_inc(mul, 1)

                def residual(c, j):
                    dve.wait_ge(outp, c + 1)
                    cols = X[:, bass.ds(c * CH, CH)]
                    dve.tensor_tensor(cols, cols, p_out[j][:], ALU.add).then_inc(resid, 1)

                weights(0, True)
                split_rest(0)
                split_low(0)
                with dve.Fori(0, IMAGES - 1) as n:
                    for h in range(2):
                        c = n * 2 + h
                        multiply(c, n, h, range(0, 12))
                        weights(c + 1, False)
                        multiply(c, n, h, range(12, 15))
                        split_rest(c + 1)
                        multiply(c, n, h, range(15, 17))
                        split_low(c + 1)
                        multiply(c, n, h, range(17, WIN5))
                        residual(c, h)
                n, c = IMAGES - 1, NCH - 2
                multiply(c, n, 0, range(0, 12))
                weights(c + 1, False)
                multiply(c, n, 0, range(12, 15))
                split_rest(c + 1)
                multiply(c, n, 0, range(15, 17))
                split_low(c + 1)
                multiply(c, n, 0, range(17, WIN5))
                residual(c, 0)
                multiply(c + 1, n, 1, range(WIN5))
                residual(c + 1, 1)

            @block.tensor
            def _(pe):
                pe.wait_ge(cast, 2)
                LAG = 3

                def turn(c):
                    pe.wait_ge(low, c + 1)
                    for q in range(5):
                        if q == 4 :
                            pe.wait_ge(stored, c * 3 + 1)
                        if q == 0 and not (isinstance(c, int) and c == 0):
                            pe.wait_ge(stored, c * 3)
                        for t in range(TPC):
                            last = pe.transpose(p_tr[(q // 2) % 2][0:ROWS, q % 2, t * P:(t + 1) * P],
                                                parts[:, t, q].rearrange("p a b -> p (a b)"), ident[:])
                        if q % 2 or q == 4:
                            last.then_inc(turned, 1)

                def spread(c, j, t):
                    if t % 10 == 0:
                        pe.wait_ge(stored, c * 3 + t // 10 + 1)
                    if not (isinstance(c, int) and c * WIN5 + t < NB):
                        pe.wait_ge(mul, c * WIN5 + t - (NB - 1))
                    pe.matmul(p_bc[t % NB][:], sel[:, t % 5, :], AT[j][:, t // 5, :],
                              start=True, stop=True).then_inc(bc, 1)

                def project(c, j, m):
                    pe.wait_ge(mul, c * WIN5 + 2 * m + 1)
                    pe.matmul(p_out[j][:], opT[:], prod_pe[m % 3][:], start=(m == 0), stop=False)\
                      .then_inc(opm, 1)

                def chunk(c, j, first, last):
                    if not first:
                        pe.wait_ge(resid, c - 1)
                    for t in range(WIN5 + LAG):
                        if t < WIN5:
                            spread(c, j, t)
                        if t == WIN5 - 2 and not last:
                            turn(c + 1)
                        if t >= LAG and (t - LAG) % 2 == 0:
                            project(c, j, (t - LAG) // 2)
                    pe.wait_ge(summed, (c + 1) * (NPO - 1))
                    pe.matmul(p_out[j][:], opT[:], acc[j][:], start=False, stop=True).then_inc(outp, 1)

                turn(0)
                chunk(0, 0, True, False)
                chunk(1, 1, True, False)
                with pe.Fori(1, IMAGES - 1) as n:
                    chunk(n * 2, 0, False, False)
                    chunk(n * 2 + 1, 1, False, False)
                chunk(NCH - 2, 0, False, False)
                chunk(NCH - 1, 1, False, True)


def sample_general(nc, d, X, VP, OM, flag):
    TPI = PIX // P
    with ExitStack() as st:
        ident = sb(nc, st, "g_ident", [P, P])
        opT = sb(nc, st, "g_opT", [P, P])
        line = sb(nc, st, "g_line", [P, SIDE])
        pix = sb(nc, st, "g_pix", [P, TPI, 2])
        kern = sb(nc, st, "g_kern", [P, 2, GK])
        pos = sb(nc, st, "g_pos", [P, 2, GK])
        W = [sb(nc, st, f"g_W{a}", [P, GK, SIDE]) for a in range(2)]
        outer = sb(nc, st, "g_outer", [P, SIDE, SIDE])
        AG = sb(nc, st, "g_AG", [P, PIX])
        AGT = sb(nc, st, "g_AGT", [P, TPI, P])
        VC = sb(nc, st, "g_VC", [P, PIX])
        VT = sb(nc, st, "g_VT", [P, TPI, P])
        S = sb(nc, st, "g_S", [P, P])
        ST = sb(nc, st, "g_ST", [P, P])
        p_tr = [ps(nc, st, f"g_ptr{i}") for i in range(2)]
        p_s = ps(nc, st, "g_ps", (P, P))
        p_st = ps(nc, st, "g_pst", (P, P))
        p_o = ps(nc, st, "g_po", (P, P))
        w_in = sem(nc, st, "g_w_in")
        image = sem(nc, st, "g_image")
        vturn = sem(nc, st, "g_vturn")
        vout = sem(nc, st, "g_vout")
        step = sem(nc, st, "g_step")
        dist = sem(nc, st, "g_dist")
        tent = sem(nc, st, "g_tent")
        part = sem(nc, st, "g_part")
        wsum = sem(nc, st, "g_wsum")
        turned = sem(nc, st, "g_turned")
        moved = sem(nc, st, "g_moved")
        applied = sem(nc, st, "g_applied")
        sout = sem(nc, st, "g_sout")
        sturn = sem(nc, st, "g_sturn")
        stout = sem(nc, st, "g_stout")
        projected = sem(nc, st, "g_projected")
        added = sem(nc, st, "g_added")

        with nc.Block() as block:
            @block.sync
            def _(sp):
                far = sp.value_load(flag[0:1, 0:1])
                with sp.If(far > 0):
                    for n in range(IMAGES):
                        sp.dma_start(X[:, n * PIX:(n + 1) * PIX], d["x"][n]).then_inc(w_in, 16)
                    for dst, src in ((ident, "c_ident"), (opT, "op_wT"), (pix, "c_pixel"), (kern, "c_kernel"),
                                     (line, "c_line")):
                        sp.dma_start(dst[:], d[src]).then_inc(w_in, 16)
                sp.nop()

            @block.vector
            def _(dve):
                far = dve.value_load(flag[0:1, 0:1])
                with dve.If(far > 0):
                    dve.wait_ge(w_in, 16 * (IMAGES + 5))
                    with dve.Fori(0, IMAGES) as n:
                        dve.wait_ge(vturn, n)
                        dve.tensor_copy(VC[:].rearrange("p (a b) -> p a b", a=SIDE),
                                        VP[:, bass.ds(n, 1), 2:2 + SIDE, 2:2 + SIDE]
                                        .rearrange("p o a b -> p (o a) b")).then_inc(image, 1)
                        with dve.Fori(0, TPI) as t:
                            c = n * TPI + t
                            for a in range(2):
                                dve.scalar_tensor_tensor(
                                    pos[:, a], OM[:, bass.ds(c, 1), a * GK:(a + 1) * GK]
                                    .rearrange("p o k -> p (o k)"), pix[:, bass.ds(t, 1), a]
                                    , kern[:, a], ALU.add, ALU.add).then_inc(step, 1)
                            dve.wait_ge(step, c * 2 + 2)
                            for a in range(2):
                                dve.tensor_tensor(
                                    W[a][:], pos[:, a].rearrange("p (k o) -> p k o", o=1)
                                    .to_broadcast([P, GK, SIDE]),
                                    line[:].rearrange("p (o s) -> p o s", o=1).to_broadcast([P, GK, SIDE]),
                                    ALU.subtract).then_inc(dist, 1)
                            dve.wait_ge(tent, c * 2 + 2)
                            dve.tensor_tensor(
                                W[0][:], W[0][:], OM[:, bass.ds(c, 1), 2 * GK:3 * GK]
                                .rearrange("p o k -> p k o").to_broadcast([P, GK, SIDE]),
                                ALU.mult).then_inc(part, 1)
                            with dve.Fori(0, GROUPS) as g:
                                cg = c * GROUPS + g
                                dve.wait_ge(turned, cg * 2)
                                for k in range(K):
                                    wy = W[0][:, bass.ds(g * K + k, 1), :].rearrange("p o s -> p s o")\
                                        .to_broadcast([P, SIDE, SIDE])
                                    wx = W[1][:, bass.ds(g * K + k, 1), :].to_broadcast([P, SIDE, SIDE])
                                    dve.wait_ge(part, (c + 1) + cg * 17 + max(2 * k - 1, 0))
                                    out = AG[:].rearrange("p (a b) -> p a b", a=SIDE) if k == 0 else outer[:]
                                    dve.tensor_tensor(out, wy, wx, ALU.mult).then_inc(part, 1)
                                    if k:
                                        dve.wait_ge(part, (c + 1) + cg * 17 + 2 * k)
                                        dve.tensor_tensor(AG[:], AG[:], outer[:].rearrange("p a b -> p (a b)"),
                                                          ALU.add).then_inc(part, 1)
                                dve.wait_ge(part, (c + 1) + cg * 17 + 17)
                                dve.tensor_copy(pos[0:1, 0, 0:1], pos[0:1, 0, 0:1]).then_inc(wsum, 1)
                            dve.wait_ge(applied, c * GROUPS + GROUPS)
                            dve.tensor_copy(S[:], p_s[:]).then_inc(sout, 1)
                            dve.wait_ge(sturn, c + 1)
                            dve.tensor_copy(ST[:], p_st[:]).then_inc(stout, 1)
                            dve.wait_ge(projected, c + 1)
                            cols = X[:, bass.ds(c * P, P)]
                            dve.tensor_tensor(cols, cols, p_o[:], ALU.add).then_inc(added, 1)
                dve.engine_nop()

            @block.scalar
            def _(act):
                far = act.value_load(flag[0:1, 0:1])
                with act.If(far > 0):
                    with act.Fori(0, IMAGES) as n:
                        for h in range(2):
                            act.wait_ge(vturn, n + 1)
                            act.activation(VT[:, h * 4:h * 4 + 4].rearrange("p m c -> p (m c)"), p_tr[h][:],
                                           ACT.Copy).then_inc(vout, 1)
                        with act.Fori(0, TPI) as t:
                            c = n * TPI + t
                            for a in range(2):
                                act.wait_ge(dist, c * 2 + a + 1)
                                act.activation(W[a][:], W[a][:], ACT.Abs).then_inc(moved, 1)
                                act.wait_ge(moved, c * (2 + 2 * GROUPS) + a + 1)
                                act.activation(W[a][:], W[a][:], ACT.Relu, bias=1.0, scale=-1.0)\
                                   .then_inc(tent, 1)
                            with act.Fori(0, GROUPS) as g:
                                cg = c * GROUPS + g
                                act.wait_ge(applied, cg)
                                for h in range(2):
                                    act.wait_ge(turned, cg * 2 + h + 1)
                                    act.activation(AGT[:, h * 4:h * 4 + 4].rearrange("p m c -> p (m c)"),
                                                   p_tr[h][:], ACT.Copy).then_inc(moved, 1)
                act.nop()

            @block.tensor
            def _(pe):
                far = pe.value_load(flag[0:1, 0:1])
                with pe.If(far > 0):
                    pe.wait_ge(w_in, 16 * (IMAGES + 5))
                    with pe.Fori(0, IMAGES) as n:
                        pe.wait_ge(image, n + 1)
                        pe.wait_ge(moved, n * (TPI * (2 + 2 * GROUPS)))
                        for m in range(TPI):
                            last = pe.transpose(p_tr[m // 4][:, (m % 4) * P:(m % 4 + 1) * P],
                                                VC[:, m * P:(m + 1) * P], ident[:])
                        last.then_inc(vturn, 1)
                        with pe.Fori(0, TPI) as t:
                            c = n * TPI + t
                            with pe.Fori(0, GROUPS) as g:
                                cg = c * GROUPS + g
                                pe.wait_ge(vout, n * 2 + 2)
                                pe.wait_ge(sout, c)
                                pe.wait_ge(wsum, cg + 1)
                                for m in range(TPI):
                                    last = pe.transpose(p_tr[m // 4][:, (m % 4) * P:(m % 4 + 1) * P],
                                                        AG[:, m * P:(m + 1) * P], ident[:])
                                    if m % 4 == 3:
                                        last.then_inc(turned, 1)
                                pe.wait_ge(moved, c * (2 + 2 * GROUPS) + 2 + 2 * g + 2)
                                for m in range(TPI):
                                    last = pe.matmul(p_s[:, bass.ds(g * CG, CG)], AGT[:, m, :],
                                                     VT[:, m, bass.ds(g * CG, CG)],
                                                     start=(m == 0), stop=(m == TPI - 1))
                                last.then_inc(applied, 1)
                            pe.wait_ge(sout, c + 1)
                            pe.transpose(p_st[:], S[:], ident[:]).then_inc(sturn, 1)
                            pe.wait_ge(stout, c + 1)
                            pe.wait_ge(added, c)
                            pe.matmul(p_o[:], opT[:], ST[:], start=True, stop=True).then_inc(projected, 1)
                pe.nop()


def token_norm(nc, d, X, XA):
    with ExitStack() as st:
        center = sb(nc, st, "n_center", [P, P])
        ones = sb(nc, st, "n_ones", [P, P])
        eps = sb(nc, st, "n_eps", [P, 1])
        sq = [sb(nc, st, f"n_sq{k}", [P, CH]) for k in range(4)]
        p_c = [ps(nc, st, f"n_pc{k}") for k in range(4)]
        p_v = [ps(nc, st, f"n_pv{k}") for k in range(4)]
        w_in = sem(nc, st, "n_w_in")
        cleared = sem(nc, st, "n_cleared")
        centered = sem(nc, st, "n_centered")
        squared = sem(nc, st, "n_squared")
        varied = sem(nc, st, "n_varied")
        logged = sem(nc, st, "n_logged")
        inverted = sem(nc, st, "n_inverted")
        written = sem(nc, st, "n_written")

        with nc.Block() as block:
            @block.sync
            def _(sp):
                sp.dma_start(center[:], d["c_center"]).then_inc(w_in, 16)
                sp.dma_start(ones[:], d["c_ones"]).then_inc(w_in, 16)

            @block.gpsimd
            def _(pool):
                nc.gpsimd.memset(eps[:], EPS).then_inc(cleared, 1)
                nc.gpsimd.memset(XA[:, :, 0:REACH], 0.0).then_inc(cleared, 1)
                nc.gpsimd.memset(XA[:, :, REACH + PIX:], 0.0).then_inc(cleared, 1)

            @block.tensor
            def _(pe):
                pe.wait_ge(w_in, 32)
                with pe.Fori(0, NCH // 4) as i:
                    pe.wait_ge(written, i * 4)
                    for k in range(4):
                        pe.matmul(p_c[k][:], center[:], X[:, bass.ds((i * 4 + k) * CH, CH)],
                                  start=True, stop=True).then_inc(centered, 1)
                    for k in range(4):
                        pe.wait_ge(squared, i * 4 + k + 1)
                        pe.matmul(p_v[k][:], ones[:], sq[k][:], start=True, stop=True).then_inc(varied, 1)

            @block.scalar
            def _(act):
                act.preload_act_table_set("natural_log_exp_and_others")
                act.wait_ge(cleared, 3)
                with act.Fori(0, NCH // 4) as i:
                    for k in range(4):
                        act.wait_ge(centered, i * 4 + k + 1)
                        act.activation(sq[k][:], p_c[k][:], ACT.Square).then_inc(squared, 1)
                    for k in range(4):
                        act.wait_ge(varied, i * 4 + k + 1)
                        act.activation(sq[k][:], p_v[k][:], ACT.Ln, bias=eps[:]).then_inc(logged, 1)
                    for k in range(4):
                        act.wait_ge(logged, i * 4 + k + 1)
                        act.activation(sq[k][:], sq[k][:], ACT.Exp, scale=-0.5).then_inc(inverted, 1)

            @block.vector
            def _(dve):
                with dve.Fori(0, NCH // 4) as i:
                    for k in range(4):
                        c = i * 4 + k
                        dve.wait_ge(inverted, c + 1)
                        off = REACH + (k % 2) * CH
                        dve.tensor_tensor(XA[:, bass.ds(i * 2 + k // 2, 1), off:off + CH]
                                          .rearrange("p o w -> p (o w)"), p_c[k][:], sq[k][:],
                                          ALU.mult).then_inc(written, 1)


def attention(nc, d, XA):
    PADA = PIX + 2 * REACH
    NBLK = PIX // QB
    VW = DV + 1
    with ExitStack() as st:
        ident = sb(nc, st, "a_ident", [P, P])
        wq = sb(nc, st, "a_wq", [P, 2, P])
        wk = sb(nc, st, "a_wk", [P, 2, P])
        wv = sb(nc, st, "a_wv", [P, P])
        wo = sb(nc, st, "a_wo", [P, P])
        bq = sb(nc, st, "a_bq", [P, 2])
        bk = sb(nc, st, "a_bk", [P, 2])
        bv = sb(nc, st, "a_bv", [P, P])
        bo = sb(nc, st, "a_bo", [P, 1])
        bias = [sb(nc, st, f"a_bias{v}", [P, 4, 2, P]) for v in range(3)]
        XS = [sb(nc, st, f"a_XS{j}", [P, PADA]) for j in range(2)]
        QT = [sb(nc, st, f"a_QT{j}", [P, 2, PIX]) for j in range(2)]
        KT = [sb(nc, st, f"a_KT{j}", [P, 2, PADA]) for j in range(2)]
        V = [sb(nc, st, f"a_V{j}", [P, NBLK, HEADS, VW]) for j in range(2)]
        E = [sb(nc, st, f"a_E{b}", [P, HEADS, P]) for b in range(2)]
        PT = [sb(nc, st, f"a_PT{b}", [P, HEADS, P]) for b in range(2)]
        nm = sb(nc, st, "a_nm", [P, 2, HEADS])
        rsum = sb(nc, st, "a_rsum", [P, 2, HEADS])
        O = [sb(nc, st, f"a_O{b}", [P, P]) for b in range(2)]
        OT = [sb(nc, st, f"a_OT{j}", [P, PIX]) for j in range(2)]
        p_s = ps(nc, st, "a_ps", (P, 4, 4, P))
        p_t = ps(nc, st, "a_pt", (P, 2, 4, P))
        p_m = ps(nc, st, "a_pm")
        p_o = ps(nc, st, "a_po")

        w_in = sem(nc, st, "a_w_in")
        rel_in = sem(nc, st, "a_rel_in")
        masked = sem(nc, st, "a_masked")
        cleared = sem(nc, st, "a_cleared")
        staged = sem(nc, st, "a_staged")
        proj = sem(nc, st, "a_proj")
        proj_out = sem(nc, st, "a_proj_out")
        scored = sem(nc, st, "a_scored")
        biased = sem(nc, st, "a_biased")
        maxed = sem(nc, st, "a_maxed")
        powered = sem(nc, st, "a_powered")
        turned = sem(nc, st, "a_turned")
        pt_dve = sem(nc, st, "a_pt_dve")
        pt_act = sem(nc, st, "a_pt_act")
        mixed = sem(nc, st, "a_mixed")
        summed = sem(nc, st, "a_summed")
        scaled = sem(nc, st, "a_scaled")
        oturned = sem(nc, st, "a_oturned")
        ostored = sem(nc, st, "a_ostored")
        wo_done = sem(nc, st, "a_wo_done")
        written = sem(nc, st, "a_written")
        NPM = 14
        VHEAD = {r * 2 + hh: hh * 4 + r for r in range(4) for hh in range(2)}
        U2 = 2 * UNITS

        with nc.Block() as block:
            @block.sync
            def _(sp):
                for dst, src in ((ident, "c_ident"), (wq, "wq"), (wk, "wk"), (wv, "wv"), (wo, "wo"), (bq, "bq"),
                                 (bk, "bk"), (bo, "bo")):
                    sp.dma_start(dst[:], d[src]).then_inc(w_in, 16)
                sp.dma_start(bv[:], d["bv"].partition_broadcast(P)).then_inc(w_in, 16)
                sp.wait_ge(masked, 1)
                rel = d["rel_bias"].rearrange("(o hh r) w -> o r hh w", o=1, hh=2)
                for half in range(2):
                    for i in range(QB):
                        row = half * QB + i
                        sp.dma_start(bias[1][row:row + 1, :, :, i:i + 2 * REACH + 1], rel).then_inc(rel_in, 16)

            @block.gpsimd
            def _(pool):
                nc.gpsimd.memset(bias[1][:], NEG).then_inc(masked, 1)
                for j in range(2):
                    nc.gpsimd.memset(KT[j][:, :, 0:REACH], 0.0).then_inc(cleared, 1)
                    nc.gpsimd.memset(KT[j][:, :, REACH + PIX:], 0.0).then_inc(cleared, 1)
                    nc.gpsimd.memset(V[j][:, :, :, DV:VW], 1.0).then_inc(cleared, 1)

                def stage(n, j):
                    nc.gpsimd.tensor_copy(XS[j][:], XA[:, bass.ds(n, 1), :].rearrange("p o w -> p (o w)"))\
                      .then_inc(staged, 1)

                stage(0, 0)
                stage(1, 1)
                pool.wait_ge(rel_in, 16 * 2 * QB)
                for v in (0, 2):
                    nc.gpsimd.tensor_copy(bias[v][:], bias[1][:]).then_inc(masked, 1)
                pool.wait_ge(masked, 3)
                nc.gpsimd.memset(bias[0][0:QB, :, :, 0:REACH], NEG).then_inc(masked, 1)
                nc.gpsimd.memset(bias[2][QB:P, :, :, P - REACH:P], NEG).then_inc(masked, 1)
                with pool.Fori(1, IMAGES // 2) as i:
                    for j in range(2):
                        pool.wait_ge(written, (i * 2 + j - 1) * 2)
                        stage(i * 2 + j, j)

            @block.tensor
            def _(pe):
                pe.wait_ge(w_in, 16 * 9)
                pe.wait_ge(cleared, 6)

                def project(n, j, base):
                    pe.wait_ge(staged, n + 1)
                    k = 0
                    for w in (wq, wk):
                        for m in range(2):
                            for h in range(2):
                                pe.wait_ge(proj_out, base + k)
                                pe.matmul(p_m[:], w[:, m, :], XS[j][:, REACH + h * CH:REACH + (h + 1) * CH],
                                          start=True, stop=True).then_inc(proj, 1)
                                k += 1
                    for q in range(4):
                        pe.wait_ge(proj_out, base + k)
                        for b in range(4):
                            at = (q * 4 + b) * QB
                            last = pe.matmul(p_m[:, b * P:(b + 1) * P], XS[j][:, at:at + P], wv[:],
                                             start=True, stop=True)
                        last.then_inc(proj, 1)
                        k += 1

                def scores(g, u):
                    j, v = u // UNITS, u % UNITS
                    pe.wait_ge(biased, g + u)
                    for r in range(4):
                        for hh in range(2):
                            for half in range(2):
                                q0 = (2 * v + half) * QB
                                last = pe.matmul(p_s[half * QB:(half + 1) * QB, r, hh, :],
                                                 QT[j][r * DK:(r + 1) * DK, hh, q0:q0 + QB],
                                                 KT[j][r * DK:(r + 1) * DK, hh, q0:q0 + P],
                                                 start=True, stop=True)
                    last.then_inc(scored, 1)

                def turn(g, u):
                    for b in range(2):
                        for k in range(4):
                            o = b * 4 + k
                            pe.wait_ge(powered, (g + u) * HEADS + o + 1)
                            if k == 0:
                                pe.wait_ge((pt_dve, pt_act)[b], g + u)
                            last = pe.transpose(p_t[:, b, k, :], E[u % 2][:, o, :], ident[:])
                        last.then_inc(turned, 1)

                def mix(g, u):
                    j, v = u // UNITS, u % UNITS
                    pe.wait_ge(pt_dve, g + u + 1)
                    pe.wait_ge(pt_act, g + u + 1)
                    pe.wait_ge(scaled, g + u)
                    pe.wait_ge(ostored, g + u)
                    for o in range(HEADS):
                        hd = VHEAD[o]
                        for half in range(2):
                            last = pe.matmul(p_o[half * QB:(half + 1) * QB,
                                                 hd * VW:(hd + 1) * VW],
                                             PT[u % 2][:, o, half * QB:(half + 1) * QB],
                                             V[j][:, 2 * v + half, hd, :], start=True, stop=True)
                    last.then_inc(mixed, 1)

                def turn_out(g, u):
                    pe.wait_ge(scaled, g + u + 1)
                    pe.wait_ge(ostored, g + u)
                    pe.transpose(p_o[:, HEADS * VW:HEADS * VW + P], O[u % 2][:], ident[:])\
                      .then_inc(oturned, 1)

                def output(n, j, base):
                    pe.wait_ge(ostored, n * UNITS + UNITS)
                    for h in range(2):
                        if h:
                            pe.wait_ge(written, n * 2 + 1)
                        else:
                            pe.wait_ge(proj_out, base)
                            pe.wait_ge(written, n * 2)
                        pe.matmul(p_m[:], wo[:], OT[j][:, h * CH:(h + 1) * CH], start=True, stop=True)\
                          .then_inc(wo_done, 1)

                with pe.Fori(0, IMAGES // 2) as i:
                    n, g = i * 2, i * U2
                    pe.wait_ge(written, n * 2)
                    project(n, 0, n * 12)
                    pe.wait_ge(proj_out, n * 12 + 12)
                    scores(g, 0)
                    for u in range(U2 + 2):
                        if u == 3:
                            project(n + 1, 1, n * 12 + 12)
                        if u + 1 == UNITS:
                            pe.wait_ge(proj_out, n * 12 + 24)
                        if u >= 2:
                            turn_out(g, u - 2)
                        if u + 1 < U2:
                            scores(g, u + 1)
                        if u < U2:
                            turn(g, u)
                        if 1 <= u <= U2:
                            mix(g, u - 1)
                        if u - 2 == UNITS - 1:
                            output(n, 0, n * 12 + 24)
                    output(n + 1, 1, n * 12 + 24)

            @block.scalar
            def _(act):
                act.wait_ge(w_in, 16 * 9)

                def project(n, j, base):
                    k = 0
                    for dst, off, b in ((QT, 0, bq), (KT, REACH, bk)):
                        for m in range(2):
                            for h in range(2):
                                act.wait_ge(proj, base + k + 1)
                                act.activation(dst[j][:, m, off + h * CH:off + (h + 1) * CH], p_m[:],
                                               ACT.Identity, bias=b[:, m:m + 1]).then_inc(proj_out, 1)
                                k += 1

                def exps(g, u):
                    act.wait_ge(maxed, g + u + 1)
                    for o in range(HEADS):
                        act.activation(E[u % 2][:, o, :], E[u % 2][:, o, :], ACT.Exp,
                                       bias=nm[:, u % 2, o:o + 1]).then_inc(powered, 1)

                def copy_pt(g, u):
                    act.wait_ge(turned, (g + u) * 2 + 2)
                    if u >= 2:
                        act.wait_ge(mixed, g + u - 1)
                    act.activation(PT[u % 2][:, 4:8, :], p_t[:, 1], ACT.Copy).then_inc(pt_act, 1)

                def copy_out(g, u):
                    act.wait_ge(oturned, g + u + 1)
                    act.activation(OT[u // UNITS][:, (u % UNITS) * P:(u % UNITS + 1) * P],
                                   p_o[:, HEADS * VW:HEADS * VW + P], ACT.Copy).then_inc(ostored, 1)

                with act.Fori(0, IMAGES // 2) as i:
                    n, g = i * 2, i * U2
                    act.wait_ge(wo_done, n * 2)
                    act.wait_ge(mixed, g)
                    project(n, 0, n * 12)
                    exps(g, 0)
                    for u in range(U2 + 2):
                        if u == 3:
                            project(n + 1, 1, n * 12 + 12)
                        if u >= 2:
                            copy_out(g, u - 2)
                        if u + 1 < U2:
                            exps(g, u + 1)
                        if u < U2:
                            copy_pt(g, u)

            @block.vector
            def _(dve):
                dve.wait_ge(w_in, 16 * 9)
                dve.wait_ge(cleared, 6)
                dve.wait_ge(masked, 5)

                def values(n, j, base):
                    for q in range(4):
                        dve.wait_ge(proj, base + 8 + q + 1)
                        dve.tensor_tensor(V[j][:, q * 4:(q + 1) * 4, :, 0:DV],
                                          p_m[:].rearrange("p (b h w) -> p b h w", b=4, h=HEADS),
                                          bv[:].rearrange("p (o h w) -> p o h w", o=1, h=HEADS)
                                          .to_broadcast([P, 4, HEADS, DV]), ALU.add).then_inc(proj_out, 1)

                def soft(g, u):
                    v = u % UNITS
                    which = 0 if v == 0 else 2 if v == UNITS - 1 else 1
                    dve.wait_ge(scored, g + u + 1)
                    if u >= 2:
                        dve.wait_ge(turned, (g + u - 1) * 2)
                    dve.scalar_tensor_tensor(
                        E[u % 2][:].rearrange("p (r h) w -> p r (h w)", r=4),
                        p_s[:, :, 0:2].rearrange("p r h w -> p r (h w)"), float(DK) ** -0.5,
                        bias[which][:].rearrange("p r h w -> p r (h w)"), ALU.mult, ALU.add)\
                       .then_inc(biased, 1)
                    dve.wait_ge(biased, g + u + 1)
                    dve.tensor_reduce(nm[:, u % 2, :], E[u % 2][:], AX.X, ALU.max, negate=True)\
                       .then_inc(maxed, 1)

                def copy_pt(g, u):
                    dve.wait_ge(turned, (g + u) * 2 + 1)
                    if u >= 2:
                        dve.wait_ge(mixed, g + u - 1)
                    dve.tensor_copy(PT[u % 2][:, 0:4, :], p_t[:, 0]).then_inc(pt_dve, 1)

                def scale(g, u):
                    dve.wait_ge(mixed, g + u + 1)
                    if u >= 2:
                        dve.wait_ge(oturned, g + u - 1)
                    po = p_o[:, 0:HEADS * VW].rearrange("p (h w) -> p h w", h=HEADS)
                    dve.reciprocal(rsum[:, u % 2, :], po[:, :, DV]).then_inc(summed, 1)
                    dve.wait_ge(summed, g + u + 1)
                    dve.tensor_tensor(O[u % 2][:].rearrange("p (h w) -> p h w", h=HEADS), po[:, :, 0:DV],
                                      rsum[:, u % 2, :].rearrange("p (h o) -> p h o", o=1)
                                      .to_broadcast([P, HEADS, DV]), ALU.mult).then_inc(scaled, 1)

                def output(n, j):
                    for h in range(2):
                        dve.wait_ge(wo_done, n * 2 + h + 1)
                        cols = slice(REACH + h * CH, REACH + (h + 1) * CH)
                        dve.scalar_tensor_tensor(XA[:, bass.ds(n, 1), cols].rearrange("p o w -> p (o w)"),
                                                 p_m[:], bo[:], XS[j][:, cols], ALU.add, ALU.add)\
                           .then_inc(written, 1)

                with dve.Fori(0, IMAGES // 2) as i:
                    n, g = i * 2, i * U2
                    dve.wait_ge(mixed, g)
                    dve.wait_ge(turned, g * 2)
                    values(n, 0, n * 12)
                    soft(g, 0)
                    for u in range(U2 + 2):
                        if u == 3:
                            values(n + 1, 1, n * 12 + 12)
                        if u + 1 < U2:
                            soft(g, u + 1)
                        if u < U2:
                            copy_pt(g, u)
                        if 1 <= u <= U2:
                            scale(g, u - 1)
                        if u - 2 == UNITS - 1:
                            output(n, 0)
                    output(n + 1, 1)


def middle(nc, d, X, XA, table, slots):
    W4 = 4
    NT = W4 * TPC
    GRP = NCH // W4
    NPE, NACT, NDVE = 12, 17, 7
    with ExitStack() as st:
        ident = sb(nc, st, "m_ident", [P, P])
        center = sb(nc, st, "m_center", [P, P])
        ones = sb(nc, st, "m_ones", [P, P])
        lin = sb(nc, st, "m_lin", [P, P])
        vec = sb(nc, st, "m_vec", [P, 5])
        g1, b1, bl, g2, b2 = (vec[:, k:k + 1] for k in range(5))
        upper = sb(nc, st, "m_upper", [P, P])
        full = sb(nc, st, "m_full", [P, P])
        wr = sb(nc, st, "m_wr", [P, EXPERTS])
        br = sb(nc, st, "m_br", [EXPERTS, 1])
        num = sb(nc, st, "m_num", [P, EXPERTS])
        region = sb(nc, st, "m_region", [P, EXPERTS])
        dest = sb(nc, st, "m_dest", [P, GRP, 2, NT], I32)
        pad = sb(nc, st, "m_pad", [P, PADS, ROW], I32)
        part = sb(nc, st, "m_part", [P, 1])
        blk = sb(nc, st, "m_blk", [P, BLOCKS])
        eps = sb(nc, st, "m_eps", [P, 1])
        sq = [sb(nc, st, f"m_sq{k}", [P, CH]) for k in range(W4)]
        xs = [sb(nc, st, f"m_xs{k}", [P, CH]) for k in range(W4)]
        y = [sb(nc, st, f"m_y{k}", [P, CH]) for k in range(W4)]
        LG = [sb(nc, st, f"m_LG{k}", [P, CH]) for k in range(W4)]
        pay = [sb(nc, st, f"m_pay{c}", [P, NT, ROW]) for c in range(2)]
        LT = sb(nc, st, "m_LT", [P, NT, EXPERTS])
        top = sb(nc, st, "m_top", [P, NT, 8])
        idx = sb(nc, st, "m_idx", [P, NT, 8], U32)
        fidx = sb(nc, st, "m_fidx", [P, NT, 2])
        dif = sb(nc, st, "m_dif", [P, NT])
        ex = sb(nc, st, "m_ex", [P, NT])
        sm = sb(nc, st, "m_sm", [P, NT])
        hot = sb(nc, st, "m_hot", [P, 2, NT, EXPERTS])
        both = sb(nc, st, "m_both", [P, NT, EXPERTS])
        scan = [sb(nc, st, f"m_scan{k}", [P, NT, EXPERTS]) for k in range(2)]
        at = sb(nc, st, "m_at", [P, NT, EXPERTS])
        wpos = sb(nc, st, "m_wpos", [P, NT, EXPERTS])
        total = sb(nc, st, "m_total", [P, EXPERTS])
        fpos = sb(nc, st, "m_fpos", [P, 2, NT])
        pos = sb(nc, st, "m_pos", [P, 2, NT], I32)
        fend = sb(nc, st, "m_fend", [P, PADS])
        spare = sb(nc, st, "m_spare", [P, SPARE])
        end = sb(nc, st, "m_end", [P, PADS], I32)
        nblk = sb(nc, st, "m_nblk", [P, 3, EXPERTS])
        iblk = sb(nc, st, "m_iblk", [P, EXPERTS], I32)
        past = sb(nc, st, "m_past", [P, BLOCKS])
        etab = sb(nc, st, "m_etab", [P, BLOCKS])
        rtab = sb(nc, st, "m_rtab", [P, BLOCKS])
        p_a = [ps(nc, st, f"m_pa{k}") for k in range(W4)]
        p_v = [ps(nc, st, f"m_pv{k}") for k in range(W4)]
        w_in = sem(nc, st, "m_w_in")
        cleared = sem(nc, st, "m_cleared")
        pe_stage = sem(nc, st, "m_pe_stage")
        act_stage = sem(nc, st, "m_act_stage")
        dve_stage = sem(nc, st, "m_dve_stage")
        logits = sem(nc, st, "m_logits")
        tops = sem(nc, st, "m_tops")
        found = sem(nc, st, "m_found")
        power = sem(nc, st, "m_power")
        route = sem(nc, st, "m_route")
        counted = sem(nc, st, "m_counted")
        packed = sem(nc, st, "m_packed")
        doubled = sem(nc, st, "m_doubled")
        labelled = sem(nc, st, "m_labelled")
        sent = sem(nc, st, "m_sent")
        final = sem(nc, st, "m_final")
        ticked = sem(nc, st, "m_ticked")
        padded = sem(nc, st, "m_padded")
        NW = 16
        NR = 19

        def pe_at(i, s, k):
            return i * (NPE * W4) + s * W4 + k + 1

        def act_at(i, s, k):
            return i * (NACT * W4) + s * W4 + k + 1

        def dve_at(i, s, k):
            return i * (NDVE * W4) + s * W4 + k + 1

        def cols(buf, i, k):
            return buf[:, bass.ds((i * W4 + k) * CH, CH)]

        with nc.Block() as block:
            @block.sync
            def _(sp):
                for dst, src in ((center, "c_center"), (ones, "c_ones"), (lin, "w_lin"), (vec, "mid_vec"),
                                 (ident, "c_ident"), (upper, "c_upper"), (full, "c_full"), (wr, "wr"), (br, "br"),
                                 (num, "c_number"), (region, "c_region"), (dest, "c_dest"), (pad, "c_pad"),
                                 (part, "c_partition"), (blk, "c_block"),
                                 (spare, "c_spare")):
                    sp.dma_start(dst[:], d[src]).then_inc(w_in, 16)

            @block.gpsimd
            def _(pool):
                nc.gpsimd.memset(eps[:], EPS).then_inc(cleared, 1)
                for k in range(W4):
                    nc.gpsimd.memset(LG[k][:], 0.0).then_inc(cleared, 1)
                nc.gpsimd.memset(total[:], 0.0).then_inc(cleared, 1)
                for c in range(2):
                    nc.gpsimd.memset(pay[c][:, :, P:ROW], 0.0).then_inc(cleared, 1)
                tick = sb(nc, st, "m_tick", [1, 2])
                nc.gpsimd.memset(tick[:], 0.0).then_inc(cleared, 1)
                pool.wait_ge(cleared, 9)
                with pool.Fori(0, GRP) as i:
                    pool.wait_ge(ticked, i)
                    pool.wait_ge(labelled, i * 2 + 2)
                    nc.gpsimd.tensor_tensor(tick[:, 1:2], tick[:, 0:1], tick[:, 0:1], ALU.add)\
                      .then_inc(ticked, 1)
                    for c in range(2):
                        for t in range(NT):
                            nc.gpsimd.indirect_dma_start(
                                out=slots, out_offset=bass.IndirectOffsetOnAxis(
                                    ap=pos[:, c, t:t + 1].bitcast(U32), axis=0),
                                in_=pay[c][:, t, :], in_offset=None).then_inc(sent, 16)
                pool.wait_ge(final, 1)
                pool.wait_ge(w_in, 16 * NW)
                for e in range(PADS):
                    nc.gpsimd.indirect_dma_start(
                        out=slots, out_offset=bass.IndirectOffsetOnAxis(ap=end[:, e:e + 1].bitcast(U32), axis=0),
                        in_=pad[:, e, :].bitcast(F32), in_offset=None).then_inc(padded, 16)
                pool.wait_ge(sent, 16 * 2 * NT * GRP)
                pool.wait_ge(padded, 16 * PADS)

            @block.tensor
            def _(pe):
                pe.wait_ge(w_in, 16 * NW)
                pe.wait_ge(cleared, 5)
                with pe.Fori(0, GRP) as i:
                    pe.wait_ge(act_stage, i * (NACT * W4))
                    pe.wait_ge(route, i * NR)
                    for s in range(NPE):
                        for k in range(W4):
                            off = REACH + (k % 2) * CH
                            if s == 0:
                                w, x, o = center, XA[:, bass.ds(i * 2 + k // 2, 1), off:off + CH]\
                                    .rearrange("p o w -> p (o w)"), p_a
                            elif s in (1, 4, 6, 8):
                                pe.wait_ge(act_stage, act_at(i, {1: 0, 4: 5, 6: 8, 8: 11}[s], k))
                                w, x, o = ones, sq[k][:], p_v
                            elif s == 2:
                                pe.wait_ge(act_stage, act_at(i, 3, k))
                                w, x, o = lin, xs[k][:], p_a
                            elif s == 3:
                                pe.wait_ge(dve_stage, dve_at(i, 1, k))
                                w, x, o = center, y[k][:], p_a
                            elif s == 5:
                                pe.wait_ge(dve_stage, dve_at(i, 3, k))
                                w, x, o = center, cols(X, i, k), p_a
                            elif s == 7:
                                pe.wait_ge(dve_stage, dve_at(i, 4, k))
                                w, x, o = center, y[k][:], p_a
                            elif s == 9:
                                pe.wait_ge(dve_stage, dve_at(i, 5, k))
                                pe.matmul(p_a[k][0:EXPERTS, :], wr[:], y[k][:], start=True, stop=True)\
                                  .then_inc(pe_stage, 1)
                                continue
                            elif s == 10:
                                pe.wait_ge(act_stage, act_at(i, 14, k))
                                for t in range(TPC):
                                    last = pe.transpose(p_v[k][:, t * P:(t + 1) * P],
                                                        LG[k][:, t * P:(t + 1) * P], ident[:])
                                last.then_inc(pe_stage, 1)
                                continue
                            else:
                                for t in range(TPC):
                                    last = pe.transpose(p_a[k][:, t * P:(t + 1) * P],
                                                        xs[k][:, t * P:(t + 1) * P], ident[:])
                                last.then_inc(pe_stage, 1)
                                continue
                            pe.matmul(o[k][:], w[:], x, start=True, stop=True).then_inc(pe_stage, 1)
                    pe.wait_ge(route, i * NR + 6)
                    bothf = both[:].rearrange("p t e -> p (t e)")
                    pe.matmul(p_v[0][:, 0:NT * EXPERTS], upper[:], bothf, start=True, stop=True)
                    pe.matmul(p_v[1][:, 0:NT * EXPERTS], full[:], bothf, start=True, stop=True)\
                      .then_inc(counted, 1)

            @block.scalar
            def _(act):
                act.preload_act_table_set("natural_log_exp_and_others")
                act.wait_ge(cleared, 9)
                act.wait_ge(w_in, 16 * NW)
                with act.Fori(0, GRP) as i:
                    for s in range(NACT):
                        for k in range(W4):
                            if s == 3:
                                act.wait_ge(dve_stage, dve_at(i, 0, k))
                                ins = act.activation(xs[k][:], xs[k][:], ACT.Identity, bias=b1)
                            elif s == 4:
                                act.wait_ge(pe_stage, pe_at(i, 2, k))
                                ins = act.activation(y[k][:], p_a[k][:], ACT.Relu, bias=bl)
                            elif s in (0, 5, 8, 11):
                                act.wait_ge(pe_stage, pe_at(i, {0: 0, 5: 3, 8: 5, 11: 7}[s], k))
                                ins = act.activation(sq[k][:], p_a[k][:], ACT.Square)
                            elif s in (1, 6, 9, 12):
                                act.wait_ge(pe_stage, pe_at(i, {1: 1, 6: 4, 9: 6, 12: 8}[s], k))
                                ins = act.activation(sq[k][:], p_v[k][:], ACT.Ln, bias=eps[:])
                            elif s in (2, 7, 10, 13):
                                act.wait_ge(act_stage, act_at(i, s - 1, k))
                                ins = act.activation(sq[k][:], sq[k][:], ACT.Exp, scale=-0.5)
                            elif s == 14:
                                act.wait_ge(pe_stage, pe_at(i, 9, k))
                                ins = act.activation(LG[k][0:EXPERTS, :], p_a[k][0:EXPERTS, :], ACT.Identity,
                                                     bias=br[:])
                            elif s == 15:
                                if k == 0:
                                    act.wait_ge(tops, i + 1)
                                    act.activation(ex[:], dif[:], ACT.Exp).then_inc(power, 1)
                                act.wait_ge(sent, i * (16 * 2 * NT))
                                act.wait_ge(pe_stage, pe_at(i, 11, k))
                                ins = act.activation(pay[0][:, k * TPC:(k + 1) * TPC, 0:P],
                                                     p_a[k][:].rearrange("p (t c) -> p t c", t=TPC), ACT.Copy)
                            else:
                                ins = act.activation(pay[1][:, k * TPC:(k + 1) * TPC, 0:P],
                                                     p_a[k][:].rearrange("p (t c) -> p t c", t=TPC), ACT.Copy)
                            ins.then_inc(act_stage, 1)

            @block.vector
            def _(dve):
                dve.wait_ge(w_in, 16 * NW)
                dve.wait_ge(cleared, 9)
                with dve.Fori(0, GRP) as i:
                    for s in range(NDVE - 1):
                        for k in range(W4):
                            if s == 1:
                                dve.wait_ge(act_stage, act_at(i, 4, k))
                                ins = dve.tensor_tensor(y[k][:], xs[k][:], y[k][:], ALU.add)
                            elif s == 0:
                                dve.wait_ge(act_stage, act_at(i, 2, k))
                                ins = dve.scalar_tensor_tensor(xs[k][:], p_a[k][:], g1, sq[k][:],
                                                               ALU.mult, ALU.mult)
                            elif s == 2:
                                dve.wait_ge(act_stage, act_at(i, 7, k))
                                ins = dve.scalar_tensor_tensor(y[k][:], p_a[k][:], g2, sq[k][:],
                                                               ALU.mult, ALU.mult)
                            elif s == 3:
                                dve.wait_ge(dve_stage, dve_at(i, 2, k))
                                ins = dve.scalar_tensor_tensor(cols(X, i, k), y[k][:], b2, cols(X, i, k),
                                                               ALU.add, ALU.add)
                            else:
                                dve.wait_ge(act_stage, act_at(i, 10 if s == 4 else 13, k))
                                ins = dve.tensor_tensor((y if s == 4 else xs)[k][:], p_a[k][:], sq[k][:],
                                                        ALU.mult)
                            ins.then_inc(dve_stage, 1)
                    for k in range(W4):
                        dve.wait_ge(pe_stage, pe_at(i, 10, k))
                        dve.tensor_copy(LT[:, k * TPC:(k + 1) * TPC, :],
                                        p_v[k][:].rearrange("p (t e) -> p t e", t=TPC)[:, :, 0:EXPERTS])\
                           .then_inc(dve_stage, 1)
                    r = i * NR
                    dve.wait_ge(dve_stage, dve_at(i, 6, W4 - 1))
                    dve.tensor_copy(sm[:, 0:1], LT[:, 0, 0:1])
                    for t in range(NT):
                        ins = dve.max(top[:, t, :], LT[:, t, :])
                    ins.then_inc(found, 1)
                    dve.wait_ge(found, i * 2 + 1)
                    dve.tensor_tensor(dif[:], top[:, :, 1], top[:, :, 0], ALU.subtract).then_inc(tops, 1)
                    for t in range(NT):
                        ins = dve.max_index(idx[:, t, :], top[:, t, :], LT[:, t, :])
                    ins.then_inc(found, 1)
                    dve.wait_ge(found, i * 2 + 2)
                    dve.tensor_copy(fidx[:], idx[:, :, 0:2]).then_inc(route, 1)
                    dve.wait_ge(power, i + 1)
                    dve.tensor_scalar(sm[:], ex[:], 1.0, None, ALU.add).then_inc(route, 1)
                    dve.wait_ge(route, r + 2)
                    dve.reciprocal(sm[:], sm[:]).then_inc(route, 1)
                    numb = num[:].rearrange("p (o e) -> p o e", o=1).to_broadcast([P, NT, EXPERTS])
                    for c in range(2):
                        dve.tensor_tensor(hot[:, c], numb, fidx[:, :, c:c + 1].to_broadcast([P, NT, EXPERTS]),
                                          ALU.is_equal).then_inc(route, 1)
                    dve.wait_ge(route, r + 5)
                    dve.tensor_tensor(both[:], hot[:, 0], hot[:, 1], ALU.add).then_inc(route, 1)
                    dve.wait_ge(counted, i + 1)
                    tot = p_v[1][:, 0:NT * EXPERTS].rearrange("p (t e) -> p t e", t=NT)
                    dve.tensor_copy(scan[0][:], tot).then_inc(route, 1)
                    shift, n = 1, 7
                    src, dst = 0, 1
                    while shift < NT:
                        dve.wait_ge(route, r + n)
                        dve.tensor_copy(scan[dst][:, 0:shift], scan[src][:, 0:shift])
                        dve.tensor_tensor(scan[dst][:, shift:], scan[src][:, shift:], scan[src][:, :NT - shift],
                                          ALU.add).then_inc(route, 1)
                        src, dst, shift, n = dst, src, shift * 2, n + 1
                    dve.wait_ge(route, r + n)
                    dve.tensor_tensor(at[:], scan[src][:], tot, ALU.subtract).then_inc(route, 1)
                    dve.tensor_tensor(scan[dst][:, 0, :], total[:], region[:], ALU.add).then_inc(route, 1)
                    dve.wait_ge(route, r + 13)
                    dve.tensor_tensor(at[:], at[:], scan[dst][:, 0:1, :].to_broadcast([P, NT, EXPERTS]), ALU.add)\
                       .then_inc(route, 1)
                    dve.tensor_tensor(total[:], total[:], scan[src][:, NT - 1, :], ALU.add).then_inc(route, 1)
                    dve.wait_ge(route, r + 15)
                    dve.tensor_tensor(at[:], at[:], p_v[0][:, 0:NT * EXPERTS]
                                      .rearrange("p (t e) -> p t e", t=NT), ALU.add).then_inc(route, 1)
                    for c in range(2):
                        dve.wait_ge(route, r + 16 + c)
                        dve.tensor_tensor(wpos[:], at[:], hot[:, c], ALU.mult).then_inc(packed, 1)
                        dve.wait_ge(packed, i * 2 + c + 1)
                        dve.tensor_reduce(fpos[:, c, :], wpos[:], AX.X, ALU.add).then_inc(route, 1)
                    dve.wait_ge(act_stage, act_at(i, 16, W4 - 1))
                    dve.tensor_copy(pay[0][:, :, P:P + 1].bitcast(I32), dest[:, bass.ds(i, 1), 0, :]
                                    .rearrange("p o t -> p t o"))
                    dve.tensor_copy(pay[1][:, :, P:P + 1].bitcast(I32), dest[:, bass.ds(i, 1), 1, :]
                                    .rearrange("p o t -> p t o"))
                    dve.tensor_copy(pay[0][:, :, P + 1:P + 2], sm[:].rearrange("p (t o) -> p t o", o=1))
                    dve.tensor_tensor(pay[1][:, :, P + 1:P + 2], sm[:].rearrange("p (t o) -> p t o", o=1),
                                      ex[:].rearrange("p (t o) -> p t o", o=1), ALU.mult).then_inc(labelled, 1)
                    dve.wait_ge(route, r + 18)
                    dve.tensor_copy(pos[:], fpos[:]).then_inc(labelled, 1)
                    dve.wait_ge(labelled, i * 2 + 2)
                    dve.tensor_copy(dif[:, 0:1], sm[:, 0:1]).then_inc(route, 1)
                dve.tensor_tensor(fend[:, 0:EXPERTS], total[:], region[:], ALU.add).then_inc(doubled, 1)
                dve.tensor_copy(fend[:, EXPERTS:], spare[:]).then_inc(doubled, 1)
                dve.tensor_scalar(iblk[:], total[:], float(P - 1), None, ALU.add).then_inc(doubled, 1)
                dve.wait_ge(doubled, 3)
                dve.tensor_scalar(end[:], fend[:], part[:], None, ALU.add).then_inc(final, 1)
                dve.tensor_scalar(iblk[:], iblk[:], 7, None, ALU.arith_shift_right).then_inc(doubled, 1)
                dve.wait_ge(doubled, 4)
                dve.tensor_copy(nblk[:, 0, :], iblk[:]).then_inc(doubled, 1)
                dve.memset(etab[:], 0.0).then_inc(doubled, 1)
                dve.tensor_scalar(rtab[:], blk[:], float(P), None, ALU.mult).then_inc(doubled, 1)
                dve.wait_ge(doubled, 7)
                dve.tensor_scalar(nblk[:, 2, :], nblk[:, 0, :], -float(P), float(REGION), ALU.mult, ALU.add)
                dve.tensor_copy(nblk[:, 1, 0:1], nblk[:, 0, 0:1]).then_inc(doubled, 1)
                for e in range(1, EXPERTS):
                    dve.wait_ge(doubled, 7 + e)
                    dve.tensor_tensor(nblk[:, 1, e:e + 1], nblk[:, 1, e - 1:e], nblk[:, 0, e:e + 1], ALU.add)\
                       .then_inc(doubled, 1)
                n = 7 + EXPERTS
                for e in range(EXPERTS):
                    dve.wait_ge(doubled, n)
                    dve.tensor_scalar(past[:], blk[:], nblk[:, 1, e:e + 1], None, ALU.is_ge).then_inc(doubled, 1)
                    dve.wait_ge(doubled, n + 1)
                    dve.tensor_tensor(etab[:], etab[:], past[:], ALU.add)
                    dve.scalar_tensor_tensor(rtab[:], past[:], nblk[:, 2, e:e + 1], rtab[:], ALU.mult, ALU.add)\
                       .then_inc(doubled, 1)
                    n += 2
                dve.wait_ge(doubled, n)
                dve.tensor_copy(table[:, 0, :], rtab[0:1, :]).then_inc(final, 1)
                dve.tensor_scalar(table[:, 1, :], etab[0:1, :], float(EXPERTS - 1), None, ALU.min)\
                   .then_inc(final, 1)


def experts(nc, d, table, slots, picks):
    with ExitStack() as st:
        ident = sb(nc, st, "e_ident", [P, P])
        w1 = sb(nc, st, "e_w1", [P, EXPERTS, HID])
        w2 = sb(nc, st, "e_w2", [P, EXPERTS, HC * P])
        lng = sb(nc, st, "e_lng", [P, EXPERTS])
        lnb = sb(nc, st, "e_lnb", [P, EXPERTS])
        b1 = sb(nc, st, "e_b1", [P, EXPERTS, HC])
        b2 = sb(nc, st, "e_b2", [P, EXPERTS, P])
        NBX = 8
        rows = [sb(nc, st, f"e_rows{j}", [P, ROW]) for j in range(NBX)]
        xT = [sb(nc, st, f"e_xT{j}", [P, P]) for j in range(2)]
        hp = [sb(nc, st, f"e_hp{j}", [P, HID]) for j in range(2)]
        hT = [sb(nc, st, f"e_hT{j}", [P, HC, P]) for j in range(2)]
        yb = [sb(nc, st, f"e_yb{j}", [P, P]) for j in range(NBX)]
        yw = [sb(nc, st, f"e_yw{j}", [P, P]) for j in range(NBX)]
        p_x = [ps(nc, st, f"e_px{j}") for j in range(2)]
        p_h = [ps(nc, st, f"e_ph{j}") for j in range(2)]
        p_t = [ps(nc, st, f"e_pt{j}") for j in range(2)]
        p_y = [ps(nc, st, f"e_py{j}") for j in range(2)]
        w_in = sem(nc, st, "e_w_in")
        folded = sem(nc, st, "e_folded")
        bsum = sem(nc, st, "e_bsum")
        rows_in = [sem(nc, st, f"e_rows_in{j}") for j in range(NBX)]
        x_turned = sem(nc, st, "e_x_turned")
        x_out = sem(nc, st, "e_x_out")
        up = sem(nc, st, "e_up")
        up_out = sem(nc, st, "e_up_out")
        h_turned = sem(nc, st, "e_h_turned")
        gelu = sem(nc, st, "e_gelu")
        down = sem(nc, st, "e_down")
        biased = sem(nc, st, "e_biased")
        weighted = sem(nc, st, "e_weighted")
        sent = [sem(nc, st, f"e_sent{j}") for j in range(NBX)]
        cleared = sem(nc, st, "e_cleared")
        ticked = sem(nc, st, "e_ticked")
        NW = 7

        with nc.Block() as block:
            @block.sync
            def _(sp):
                for dst, src in ((ident, "c_ident"), (w1, "w1"), (w2, "w2"), (lng, "ln_g"), (lnb, "ln_b"),
                                 (b1, "b1")):
                    sp.dma_start(dst[:], d[src]).then_inc(w_in, 16)
                sp.dma_start(b2[:].rearrange("p e c -> p (e c)"), d["b2_row"].partition_broadcast(P))\
                  .then_inc(w_in, 16)

                def load(b, j, first):
                    if not first:
                        sp.wait_ge(sent[j], (b // NBX if isinstance(b, int) else None or 0) * 16)
                    row = sp.value_load(table[0:1, 0, bass.ds(b, 1)], min_val=0, max_val=SLOTS - P)
                    sp.dma_start(rows[j][:], slots[bass.ds(row, P), :]).then_inc(rows_in[j], 16)

                for b in range(NBX):
                    load(b, b, True)
                with sp.Fori(1, BLOCKS // NBX) as i:
                    for j in range(NBX):
                        sp.wait_ge(sent[j], i * 16)
                        load(i * NBX + j, j, True)

            @block.gpsimd
            def _(pool):
                tick = sb(nc, st, "e_tick", [1, 2])
                nc.gpsimd.memset(tick[:], 0.0).then_inc(cleared, 1)
                pool.wait_ge(cleared, 1)
                with pool.Fori(0, BLOCKS // NBX) as i:
                    for j in range(NBX):
                        pool.wait_ge(ticked, i * NBX + j)
                        pool.wait_ge(weighted, i * NBX + j + 1)
                        nc.gpsimd.tensor_tensor(tick[:, 1:2], tick[:, 0:1], tick[:, 0:1], ALU.add)\
                          .then_inc(ticked, 1)
                        nc.gpsimd.indirect_dma_start(
                            out=picks, out_offset=bass.IndirectOffsetOnAxis(
                                ap=rows[j][:, P:P + 1].bitcast(U32), axis=0),
                            in_=yw[j][:], in_offset=None).then_inc(sent[j], 16)
                for j in range(NBX):
                    pool.wait_ge(sent[j], 16 * (BLOCKS // NBX))

            @block.tensor
            def _(pe):
                pe.wait_ge(w_in, 16 * NW)
                for e in range(EXPERTS):
                    for q in range(HC):
                        last = pe.matmul(p_x[0][:, e * HC + q:e * HC + q + 1], w1[:, e, q * P:(q + 1) * P],
                                         lnb[:, e:e + 1], start=True, stop=True)
                last.then_inc(bsum, 1)
                pe.wait_ge(folded, EXPERTS + 1)

                def turn_x(b, j, i):
                    pe.wait_ge(rows_in[j], (i + 1) * 16)
                    pe.transpose(p_x[j % 2][:, 0:P], rows[j][:, 0:P], ident[:]).then_inc(x_turned, 1)

                def first(b, j):
                    e = pe.value_load(table[0:1, 1, bass.ds(b, 1)], min_val=0, max_val=EXPERTS - 1)
                    pe.wait_ge(x_out, b + 1)
                    pe.matmul(p_h[j % 2][:], xT[j % 2][:], w1[:, bass.ds(e, 1), :].rearrange("p o h -> p (o h)"),
                              start=True, stop=True).then_inc(up, 1)

                def turn_h(b, j):
                    pe.wait_ge(up_out, b + 1)
                    for q in range(HC):
                        last = pe.transpose(p_t[j % 2][:, q * P:(q + 1) * P], hp[j % 2][:, q * P:(q + 1) * P],
                                            ident[:])
                    last.then_inc(h_turned, 1)

                def second(b, j):
                    e = pe.value_load(table[0:1, 1, bass.ds(b, 1)], min_val=0, max_val=EXPERTS - 1)
                    pe.wait_ge(gelu, b + 1)
                    if not isinstance(b, int) or b >= 2:
                        pe.wait_ge(biased, b - 1)
                    for q in range(HC):
                        last = pe.matmul(p_y[j % 2][:, 0:P], hT[j % 2][:, q, :],
                                         w2[:, bass.ds(e, 1), q * P:(q + 1) * P].rearrange("p o h -> p (o h)"),
                                         start=(q == 0), stop=(q == HC - 1))
                    last.then_inc(down, 1)

                def step(s, j, i, lo=0, hi=BLOCKS):
                    if hi:
                        turn_x(s, j, i)
                    for back, stage in ((1, first), (2, turn_h), (3, second)):
                        if back >= lo and (not isinstance(s, int) or 0 <= s - back < BLOCKS):
                            stage(s - back, (j - back) % NBX)

                for s in range(NBX):
                    step(s, s, 0)
                with pe.Fori(1, BLOCKS // NBX) as i:
                    for j in range(NBX):
                        step(i * NBX + j, j, i)
                for s in range(BLOCKS, BLOCKS + 3):
                    step(s, s % NBX, 0, hi=0)

            @block.scalar
            def _(act):
                act.wait_ge(folded, EXPERTS + 1)

                def scale_out(b, j, first):
                    act.wait_ge(biased, b + 1)
                    act.activation(yw[j][:], yb[j][:], ACT.Copy, scale=rows[j][:, P + 1:P + 2])\
                       .then_inc(weighted, 1)

                def gelus(b, j):
                    e = act.value_load(table[0:1, 1, bass.ds(b, 1)], min_val=0, max_val=EXPERTS - 1)
                    act.wait_ge(h_turned, b + 1)
                    for q in range(HC):
                        ins = act.activation(hT[j % 2][:, q, :], p_t[j % 2][:, q * P:(q + 1) * P], ACT.Gelu,
                                             bias=b1[:, bass.ds(e, 1), q:q + 1].rearrange("p o h -> p (o h)"))
                    ins.then_inc(gelu, 1)

                def step(s, j):
                    if not isinstance(s, int) or s < BLOCKS:
                        gelus(s, j)
                    if not isinstance(s, int) or s >= 2:
                        scale_out(s - 2, (j - 2) % NBX, False)

                for s in range(NBX):
                    step(s, s)
                with act.Fori(1, BLOCKS // NBX) as i:
                    for j in range(NBX):
                        step(i * NBX + j, j)
                for s in range(BLOCKS, BLOCKS + 2):
                    step(s, s % NBX)

            @block.vector
            def _(dve):
                dve.wait_ge(w_in, 16 * NW)
                dve.wait_ge(bsum, 1)
                for e in range(EXPERTS):
                    dve.tensor_scalar(w1[:, e, :], w1[:, e, :], lng[:, e:e + 1], None, ALU.mult).then_inc(folded, 1)
                dve.tensor_tensor(b1[:].rearrange("p e q -> p (e q)"), b1[:].rearrange("p e q -> p (e q)"),
                                  p_x[0][:, 0:EXPERTS * HC], ALU.add).then_inc(folded, 1)

                def copy_x(b, j):
                    dve.wait_ge(x_turned, b + 1)
                    dve.tensor_copy(xT[j % 2][:], p_x[j % 2][:, 0:P]).then_inc(x_out, 1)

                def copy_h(b, j):
                    dve.wait_ge(up, b + 1)
                    dve.tensor_copy(hp[j % 2][:], p_h[j % 2][:]).then_inc(up_out, 1)

                def add_bias(b, j):
                    e = dve.value_load(table[0:1, 1, bass.ds(b, 1)], min_val=0, max_val=EXPERTS - 1)
                    dve.wait_ge(down, b + 1)
                    dve.tensor_tensor(yb[j][:], p_y[j % 2][:, 0:P],
                                      b2[:, bass.ds(e, 1), :].rearrange("p o c -> p (o c)"), ALU.add)\
                       .then_inc(biased, 1)

                def step(s, j):
                    for back, stage in ((0, copy_x), (1, copy_h), (3, add_bias)):
                        if not isinstance(s, int) or 0 <= s - back < BLOCKS:
                            stage(s - back, (j - back) % NBX)

                for s in range(NBX):
                    step(s, s)
                with dve.Fori(1, BLOCKS // NBX) as i:
                    for j in range(NBX):
                        step(i * NBX + j, j)
                for s in range(BLOCKS, BLOCKS + 3):
                    step(s, s % NBX)


def combine(nc, d, X, picks, out):
    NB = 3
    with ExitStack() as st:
        ident = sb(nc, st, "c_identity", [P, P])
        y = [[sb(nc, st, f"c_y{c}{j}", [P, TPC, P]) for j in range(NB)] for c in range(2)]
        o = [sb(nc, st, f"c_o{j}", [P, CH]) for j in range(NB)]
        p_t = [ps(nc, st, f"c_pt{j}") for j in range(NB)]
        w_in = sem(nc, st, "c_w_in")
        y_in = [sem(nc, st, f"c_y_in{j}") for j in range(NB)]
        both = sem(nc, st, "c_both")
        turned = sem(nc, st, "c_turned")
        added = sem(nc, st, "c_added")
        stored = [sem(nc, st, f"c_stored{j}") for j in range(NB)]
        with nc.Block() as block:
            @block.sync
            def _(sp):
                sp.dma_start(ident[:], d["c_ident"]).then_inc(w_in, 16)
                for c in range(NCH):
                    j = c % NB
                    if c >= NB:
                        sp.wait_ge(turned, c - NB + 1)
                    for k in range(2):
                        src = picks[k * TOK + c * CH:k * TOK + (c + 1) * CH, :]
                        sp.dma_start(y[k][j][:], src.rearrange("(t p) c -> p t c", p=P)).then_inc(y_in[j], 16)

            @block.vector
            def _(dve):
                for c in range(NCH + 1):
                    if c < NCH:
                        j = c % NB
                        dve.wait_ge(y_in[j], 32 * (c // NB + 1))
                        dve.tensor_tensor(y[0][j][:], y[0][j][:], y[1][j][:], ALU.add).then_inc(both, 1)
                    if c:
                        b = c - 1
                        dve.wait_ge(turned, b + 1)
                        if b >= NB:
                            dve.wait_ge(stored[b % NB], 16 * (b // NB))
                        dve.tensor_tensor(o[b % NB][:], p_t[b % NB][:], X[:, b * CH:(b + 1) * CH], ALU.add)\
                           .then_inc(added, 1)

            @block.tensor
            def _(pe):
                pe.wait_ge(w_in, 16)
                for c in range(NCH):
                    j = c % NB
                    pe.wait_ge(both, c + 1)
                    if c >= NB:
                        pe.wait_ge(added, c - NB + 1)
                    for t in range(TPC):
                        last = pe.transpose(p_t[j][:, t * P:(t + 1) * P], y[0][j][:, t, :], ident[:])
                    last.then_inc(turned, 1)

            @block.scalar
            def _(act):
                for c in range(NCH):
                    act.wait_ge(added, c + 1)
                    act.dma_start(out[c // 2, :, (c % 2) * CH:(c % 2 + 1) * CH], o[c % NB][:])\
                       .then_inc(stored[c % NB], 16)
                for j in range(NB):
                    act.wait_ge(stored[j], 16 * len(range(j, NCH, NB)))


def store(nc, X, out):
    with ExitStack() as st:
        done = sem(nc, st, "out_done")
        with nc.Block() as block:
            @block.sync
            def _(sp):
                for n in range(IMAGES):
                    sp.dma_start(out[n], X[:, n * PIX:(n + 1) * PIX]).then_inc(done, 16)
                sp.wait_ge(done, 16 * IMAGES)


def program(nc, d, out, dbg=None):
    with ExitStack() as st:
        X = sb(nc, st, "X", [P, TOK])
        with ExitStack() as st1:
            VP = sb(nc, st1, "VP", [P, IMAGES, PAD5, PAD5])
            OM = sb(nc, st1, "OM", [P, TOK // P, 3 * GK])
            flag = sb(nc, st1, "flag", [1, 1], I32)
            front(nc, d, X, VP, OM, flag)
            if dbg: dbg("front", dict(VP=VP, OM=OM, flag=flag))
            sample_fast(nc, d, X, VP, OM)
            sample_general(nc, d, X, VP, OM, flag)
            if dbg: dbg("fast", dict(X=X))
        table = sb(nc, st, "table", [1, 2, BLOCKS], I32)
        with ExitStack() as st1:
            XA = sb(nc, st1, "XA", [P, IMAGES, PIX + 2 * REACH])
            token_norm(nc, d, X, XA)
            if dbg: dbg("ln", dict(XA=XA))
            attention(nc, d, XA)
            if dbg: dbg("attn", dict(XA=XA))
            slots = nc.dram_tensor("slots", [SLOTS, ROW], F32, kind="Internal").ap()
            picks = nc.dram_tensor("picks", [2 * TOK + PADS * P, P], F32, kind="Internal").ap()
            middle(nc, d, X, XA, table, slots)
            if dbg: dbg("mid", dict(X=X, table=table))
        experts(nc, d, table, slots, picks)
        combine(nc, d, X, picks, out)


def arrays_of(inp):
    import numpy as np

    n = {}
    n["x"] = np.ascontiguousarray(inp["x"]).reshape(IMAGES, P, PIX)
    g = lambda k: np.ascontiguousarray(inp[k])
    n["dw_w"] = g("L0_conv_dw_w").reshape(P, K)
    n["dw_b"] = g("L0_conv_dw_b").reshape(P, 1)
    om = g("L0_conv_om_w").reshape(GROUPS, 3 * K, P)
    ob = g("L0_conv_om_b").reshape(GROUPS, 3 * K)
    parts = [slice(0, 2 * K, 2), slice(1, 2 * K, 2), slice(2 * K, 3 * K)]
    n["om_wT"] = np.ascontiguousarray(np.concatenate([om[:, s].reshape(GK, P) for s in parts]).T)
    n["om_b"] = np.concatenate([ob[:, s].reshape(GK) for s in parts])
    n["vp_wT"] = np.ascontiguousarray(g("L0_conv_vp_w").T)
    n["vp_b"] = g("L0_conv_vp_b").reshape(P, 1)
    n["op_wT"] = np.ascontiguousarray(g("L0_conv_op_w").T)
    n["c_ident"] = np.eye(P, dtype=np.float32)
    n["c_group4"] = np.kron(np.eye(P // 4), np.full((4, 4), 0.25)).astype(np.float32)
    sel = np.zeros((3, GROUPS, 5, 5, P), np.float32)
    for g_ in range(GROUPS):
        for b in range(5):
            sel[:, g_, b, b, g_ * CG:(g_ + 1) * CG] = 1
    n["c_select"] = sel.reshape(3 * GROUPS * 5, 5, P)
    n["c_center"] = (np.eye(P) - np.full((P, P), 1 / P)).astype(np.float32)
    n["c_ones"] = np.full((P, P), 1 / P, np.float32)
    n["wq"] = g("L1_attn_Wq").reshape(P, 2, P)
    n["wk"] = g("L1_attn_Wk").reshape(P, 2, P)
    n["wv"], n["wo"] = g("L1_attn_Wv"), g("L1_attn_Wo")
    n["bq"] = np.ascontiguousarray(g("L1_attn_bq").reshape(2, P).T)
    n["bk"] = np.ascontiguousarray(g("L1_attn_bk").reshape(2, P).T)
    n["bv"], n["bo"] = g("L1_attn_bv"), g("L1_attn_bo").reshape(P, 1)
    n["rel_bias"] = g("L1_attn_rel_bias")
    n["w_lin"] = g("L1_attn_W_lin")
    n["mid_vec"] = np.stack([g("L1_attn_" + k) for k in ("ln1_g", "ln1_b", "b_lin", "ln2_g", "ln2_b")], -1)
    n["w1"] = np.ascontiguousarray(g("L1_ffn_W1").transpose(1, 0, 2))
    n["w2"] = np.ascontiguousarray(g("L1_ffn_W2").reshape(EXPERTS, HC, P, P).transpose(2, 0, 1, 3))
    n["wr"], n["br"] = g("L1_ffn_Wr"), g("L1_ffn_br").reshape(EXPERTS, 1)
    n["ln_g"] = np.ascontiguousarray(g("L1_ffn_ln_g").T)
    n["ln_b"] = np.ascontiguousarray(g("L1_ffn_ln_b").T)
    n["b1"] = np.ascontiguousarray(g("L1_ffn_b1").reshape(EXPERTS, HC, P).transpose(2, 0, 1))
    n["b2"] = np.ascontiguousarray(g("L1_ffn_b2").T)
    n["b2_row"] = g("L1_ffn_b2").reshape(EXPERTS * P)
    n["c_upper"] = np.triu(np.ones((P, P), np.float32), 1)
    n["c_full"] = np.ones((P, P), np.float32)
    n["c_region"] = np.broadcast_to(np.arange(EXPERTS, dtype=np.float32) * REGION, (P, EXPERTS)).copy()
    n["c_dest"] = (np.arange(TOK, dtype=np.int32).reshape(NCH // 4, 4 * TPC, P).transpose(2, 0, 1)[:, :, None]
                   + np.array([0, TOK], np.int32)[:, None]).astype(np.int32)
    n["c_pad"] = np.zeros((P, PADS, ROW), np.int32)
    n["c_pad"][:, :, P] = 2 * TOK + np.arange(PADS) * P + np.arange(P)[:, None]
    n["c_spare"] = np.broadcast_to(EXPERTS * REGION + np.arange(SPARE, dtype=np.float32) * P, (P, SPARE)).copy()
    n["c_partition"] = np.arange(P, dtype=np.float32).reshape(P, 1)
    n["c_block"] = np.broadcast_to(np.arange(BLOCKS, dtype=np.float32), (P, BLOCKS)).copy()
    n["c_number"] = np.broadcast_to(np.arange(EXPERTS, dtype=np.float32), (P, EXPERTS)).copy()
    n["c_line"] = np.broadcast_to(np.arange(SIDE, dtype=np.float32), (P, SIDE)).copy()
    tok = np.arange(PIX).reshape(PIX // P, P).T
    n["c_pixel"] = np.stack([tok // SIDE, tok % SIDE], -1).astype(np.float32)
    point = np.tile(np.arange(K), GROUPS)
    kern = np.stack([point // 3 - 1, point % 3 - 1]).astype(np.float32)
    n["c_kernel"] = np.broadcast_to(kern, (P, 2, GK)).copy()
    return n


def kernel(**inputs):
    import numpy as np
    import concourse.bacc as bacc
    from concourse.bass_utils import run_bass_kernel_spmd

    nc = bacc.Bacc("TRN2", target_bir_lowering=False, num_devices=1)
    arrays = arrays_of(inputs)
    d = {k: nc.dram_tensor("in_" + k, list(a.shape), mybir.dt.from_np(a.dtype), kind="ExternalInput").ap()
         for k, a in arrays.items()}
    out = nc.dram_tensor("out", [IMAGES, P, PIX], F32, kind="ExternalOutput").ap()
    program(nc, d, out)
    r = run_bass_kernel_spmd(nc, [{"in_" + k: a for k, a in arrays.items()}], core_ids=[0])
    return r.results[0]["out"].reshape(IMAGES, P, SIDE, SIDE)
```

```python
from contextlib import ExitStack

import concourse.bass as bass
from concourse import mybir

ALU = mybir.AluOpType
ACT = mybir.ActivationFunctionType
AX = mybir.AxisListType
F32 = mybir.dt.float32
I32 = mybir.dt.int32
BF16 = mybir.dt.bfloat16
U32 = mybir.dt.uint32

P = 128
IMAGES, SIDE = 8, 32
PIX = SIDE * SIDE
TOK = IMAGES * PIX
CH = 512
HALF = SIDE // 2
NCH = TOK // CH
TPC = CH // P
GROUPS, CG, K = 8, 16, 9
GK = GROUPS * K
WIN5 = 25
PAD3, PAD5 = SIDE + 2, SIDE + 4
HEADS, DK, DV = 8, 32, 16
REACH = 32
QB = 32
QW = QB + 2 * REACH
UB = 4
EXPERTS, HID = 8, 512
HC = HID // P
NEG = -1e9
REGION = TOK + P
BLOCKS = 2 * TOK // P + EXPERTS
SPARE = EXPERTS
SLOTS = EXPERTS * REGION + SPARE * P
PADS = EXPERTS + SPARE
ROW = P + 4
NBX = 8
EPS = 1e-5


def sb(nc, st, name, shape, dt=F32):
    return st.enter_context(nc.sbuf_tensor(name, shape, dt))


def ps(nc, st, name, shape=(P, CH), dt=F32):
    return st.enter_context(nc.psum_tensor(name, list(shape), dt))


def sem(nc, st, name):
    return st.enter_context(nc.semaphore(name))


def front(nc, d, X, VP, OM, flag):
    with ExitStack() as st:
        ident = sb(nc, st, "f_ident", [P, P])
        g4 = sb(nc, st, "f_g4", [P, P])
        vpT = sb(nc, st, "f_vpT", [P, P])
        omT = sb(nc, st, "f_omT", [P, 3 * GK])
        omb = sb(nc, st, "f_omb", [P, 3 * GK])
        dww = sb(nc, st, "f_dww", [P, K])
        dwb = sb(nc, st, "f_dwb", [P, 1])
        vpb = sb(nc, st, "f_vpb", [P, 1])
        stats = sb(nc, st, "f_stats", [P, IMAGES, 2, 6])
        mv = sb(nc, st, "f_mv", [P, IMAGES, 2])
        dev = sb(nc, st, "f_dev", [P, IMAGES])
        gmean = sb(nc, st, "f_gmean", [P, IMAGES])
        var = sb(nc, st, "f_var", [P, IMAGES])
        sd = sb(nc, st, "f_sd", [P, IMAGES])
        rs = sb(nc, st, "f_rs", [P, IMAGES])
        nb = sb(nc, st, "f_nb", [P, IMAGES])
        eps = sb(nc, st, "f_eps", [P, 1])
        ahead = sb(nc, st, "f_ahead", [P, 1])
        xnp = [sb(nc, st, f"f_xnp{j}", [P, PAD3, PAD3]) for j in range(2)]
        omin = [sb(nc, st, f"f_omin{j}", [P, PIX]) for j in range(2)]
        fmax = sb(nc, st, "f_fmax", [P, IMAGES])
        fone = sb(nc, st, "f_fone", [P, 1])
        ftop = sb(nc, st, "f_ftop", [1, 1])

        PT = 3
        diag = [sb(nc, st, f"f_diag{k}", [P, P]) for k in range(PT)]
        dwbb = sb(nc, st, "f_dwbb", [P, P])
        p_dw = [ps(nc, st, f"f_pdw{h}") for h in range(2)]
        p_stat = p_dw[0]
        p_val = [ps(nc, st, f"f_pval{h}") for h in range(2)]
        p_om = [ps(nc, st, f"f_pom{h}") for h in range(4)]

        x_in = [sem(nc, st, f"x_in{n}") for n in range(IMAGES // 2)]
        w_in = sem(nc, st, "w_in")
        cleared = sem(nc, st, "f_cleared")
        stat = sem(nc, st, "f_stat")
        avg = sem(nc, st, "f_avg")
        rooted = sem(nc, st, "f_rooted")
        normed = sem(nc, st, "f_normed")
        val_done = sem(nc, st, "f_val_done")
        val_out = sem(nc, st, "f_val_out")
        tap_done = sem(nc, st, "f_tap_done")
        om_done = sem(nc, st, "f_om_done")
        om_out = sem(nc, st, "f_om_out")
        folded = sem(nc, st, "f_folded")
        shaped = sem(nc, st, "f_shaped")
        biased = sem(nc, st, "f_biased")
        dw_done = sem(nc, st, "f_dw_done")
        TD = 2 * (K - PT)

        def images(eng, body):
            body(0, 0)
            with eng.Fori(0, IMAGES // 2 - 1) as i:
                body(i * 2 + 1, 1)
                body(i * 2 + 2, 0)
            body(IMAGES - 1, 1)

        with nc.Block() as block:
            @block.sync
            def _(sp):
                for dst, src in ((ident, "c_ident"), (g4, "c_group4"), (vpT, "vp_wT"), (omT, "om_wT"),
                                 (dww, "dw_w"), (dwb, "dw_b"), (vpb, "vp_b")):
                    sp.dma_start(dst[:], d[src]).then_inc(w_in, 16)
                sp.dma_start(omb[:], d["om_b"].partition_broadcast(P)).then_inc(w_in, 16)
                for n in range(IMAGES):
                    sp.dma_start(X[:, n * PIX:(n + 1) * PIX], d["x"][n]).then_inc(x_in[n // 2], 16)

            @block.gpsimd
            def _(pool):
                for b in xnp:
                    nc.gpsimd.memset(b[:], 0.0).then_inc(cleared, 1)
                nc.gpsimd.memset(eps[:], EPS).then_inc(cleared, 1)
                nc.gpsimd.memset(VP[:], 0.0).then_inc(cleared, 1)

            @block.scalar
            def _(act):
                act.wait_ge(cleared, 4)
                act.activation(ahead[:], eps[:], ACT.Sqrt)
                act.wait_ge(avg, 2)
                act.activation(sd[:], p_stat[:, 8:16], ACT.Sqrt, bias=eps[:]).then_inc(rooted, 1)
                act.wait_ge(w_in, 16 * 8)
                act.wait_ge(stat, 5)
                def image(n, j):
                    if not isinstance(n, int) or n >= 2:
                        act.wait_ge(tap_done, n * TD - TD)
                        act.wait_ge(dw_done, n * 2 - 2)
                    act.activation(xnp[j][:, 1:1 + SIDE, 1:1 + SIDE],
                                   X[:, bass.ds(n * PIX, PIX)].rearrange("p (a b) -> p a b", a=SIDE),
                                   ACT.Identity, bias=nb[:, bass.ds(n, 1)],
                                   scale=rs[:, bass.ds(n, 1)]).then_inc(normed, 1)
                    for h in range(2):
                        act.wait_ge(val_done, n * 2 + h + 1)
                        act.activation(
                            VP[:, bass.ds(n, 1), 2 + h * HALF:2 + (h + 1) * HALF, 2:2 + SIDE]
                            .rearrange("p o a b -> p (o a) b"),
                            p_val[h][:].rearrange("p (a b) -> p a b", a=HALF),
                            ACT.Identity, bias=vpb[:]).then_inc(val_out, 1)

                images(act, image)

            @block.vector
            def _(dve):
                dve.wait_ge(w_in, 16 * 8)
                for k in range(PT):
                    dve.tensor_scalar(diag[k][:], ident[:], dww[:, k:k + 1], None, ALU.mult).then_inc(shaped, 1)
                dve.tensor_copy(dwbb[:], dwb[:].to_broadcast([P, P])).then_inc(shaped, 1)
                for n in range(IMAGES):
                    dve.wait_ge(x_in[n // 2], 32)
                    for h in range(2):
                        last = dve.bn_stats(stats[:, n, h, :], X[:, n * PIX + h * CH:n * PIX + (h + 1) * CH])
                    last.then_inc(folded, 1)
                for n in range(IMAGES):
                    dve.wait_ge(folded, n + 1)
                    last = dve.bn_aggr(mv[:, n, :], stats[:, n, :, :])
                last.then_inc(stat, 1)
                dve.wait_ge(stat, 1)
                dve.wait_ge(avg, 1)
                dve.tensor_tensor(dev[:], mv[:, :, 0], p_stat[:, 0:8], ALU.subtract).then_inc(stat, 1)
                dve.tensor_copy(gmean[:], p_stat[:, 0:8]).then_inc(folded, 1)
                dve.wait_ge(stat, 2)
                dve.tensor_tensor(var[:], dev[:], dev[:], ALU.mult).then_inc(folded, 1)
                dve.wait_ge(folded, IMAGES + 2)
                dve.tensor_tensor(var[:], var[:], mv[:, :, 1], ALU.add).then_inc(stat, 1)
                dve.wait_ge(rooted, 1)
                dve.reciprocal(rs[:], sd[:]).then_inc(stat, 1)
                dve.wait_ge(stat, 4)
                dve.scalar_tensor_tensor(nb[:], gmean[:], -1.0, rs[:], ALU.mult, ALU.mult).then_inc(stat, 1)
                dve.wait_ge(biased, 1)
                dve.tensor_tensor(omb[:], omb[:], p_val[1][:, 0:3 * GK], ALU.add).then_inc(folded, 1)

                def taps(n, j):
                    dve.wait_ge(normed, n + 1)
                    if not isinstance(n, int) or n >= 2:
                        dve.wait_ge(om_done, n * 4 - 4)
                    for k in range(PT, K):
                        for h in range(2):
                            out = omin[j][:, h * CH:(h + 1) * CH].rearrange("p (a b) -> p a b", a=HALF)
                            src = xnp[j][:, k // 3 + h * HALF:k // 3 + (h + 1) * HALF, k % 3:k % 3 + SIDE]
                            if k == PT:
                                dve.wait_ge(dw_done, n * 2 + h + 1)
                                before = p_dw[h][:].rearrange("p (a b) -> p a b", a=HALF)
                            else:
                                dve.wait_ge(tap_done, n * TD + 2 * (k - PT - 1) + h + 1)
                                before = out
                            dve.scalar_tensor_tensor(out, src, dww[:, k:k + 1], before, ALU.mult, ALU.add)\
                               .then_inc(tap_done, 1)

                def offsets(n, j):
                    for q in range(4):
                        dve.wait_ge(om_done, n * 4 + q + 1)
                        dve.tensor_tensor(
                            OM[:, bass.ds(n * 8 + 2 * q, 2), :],
                            p_om[q][:, 0:6 * GK].rearrange("p (t c) -> p t c", t=2),
                            omb[:].rearrange("p (t c) -> p t c", t=1).to_broadcast([P, 2, 3 * GK]),
                            ALU.add).then_inc(om_out, 1)
                    dve.wait_ge(om_out, n * 4 + 4)
                    dve.tensor_reduce(fmax[:, bass.ds(n, 1)], OM[:, bass.ds(n * 8, 8), 0:2 * GK],
                                      AX.XY, ALU.max, apply_absolute_value=True).then_inc(folded, 1)

                def image(n, j):
                    taps(n, j)
                    if not isinstance(n, int) or n:
                        offsets(n - 1, 1 - j)
                images(dve, image)
                offsets(IMAGES - 1, 1)
                dve.wait_ge(folded, 2 * IMAGES + 3)
                dve.tensor_reduce(fone[:], fmax[:], AX.X, ALU.max).then_inc(stat, 1)
                dve.wait_ge(avg, 3)
                dve.tensor_reduce(ftop[:], p_stat[0:1, 0:P], AX.X, ALU.max).then_inc(stat, 1)
                dve.wait_ge(stat, 7)
                dve.tensor_scalar(flag[:], ftop[:], 1.0, None, ALU.is_gt).then_inc(stat, 1)

            @block.tensor
            def _(pe):
                pe.wait_ge(w_in, 16 * 8)
                pe.wait_ge(shaped, PT + 1)
                pe.matmul(p_val[1][:, 0:3 * GK], dwbb[:], omT[:], start=True, stop=True).then_inc(biased, 1)
                pe.wait_ge(stat, 1)
                pe.matmul(p_stat[:, 0:8], g4[:], mv[:, :, 0], start=True, stop=True).then_inc(avg, 1)
                pe.wait_ge(stat, 3)
                pe.matmul(p_stat[:, 8:16], g4[:], var[:], start=True, stop=True).then_inc(avg, 1)
                pe.wait_ge(folded, IMAGES + 3)
                pe.wait_ge(rooted, 1)

                def offsets(n, j):
                    if not isinstance(n, int) or n:
                        pe.wait_ge(om_out, n * 4)
                    for q in range(4):
                        pe.wait_ge(tap_done, n * TD + (TD - 1 + q // 2))
                        for t in range(2):
                            last = pe.matmul(p_om[q][:, t * 3 * GK:(t + 1) * 3 * GK],
                                             omin[j][:, (2 * q + t) * P:(2 * q + t + 1) * P], omT[:],
                                             start=True, stop=True)
                        last.then_inc(om_done, 1)

                def image(n, j):
                    pe.wait_ge(normed, n + 1)
                    if not isinstance(n, int) or n:
                        pe.wait_ge(val_out, n * 2)
                    for h in range(2):
                        pe.matmul(p_val[h][:], vpT[:],
                                  xnp[j][:, 1 + h * HALF:1 + (h + 1) * HALF, 1:1 + SIDE],
                                  start=True, stop=True).then_inc(val_done, 1)
                    for h in range(2):
                        if not isinstance(n, int) or n:
                            pe.wait_ge(tap_done, n * TD - TD + h + 1)
                        for k in range(PT):
                            last = pe.matmul(p_dw[h][:], diag[k][:],
                                             xnp[j][:, k // 3 + h * HALF:k // 3 + (h + 1) * HALF,
                                                    k % 3:k % 3 + SIDE],
                                             start=(k == 0), stop=(k == PT - 1))
                        last.then_inc(dw_done, 1)
                    if not isinstance(n, int) or n:
                        offsets(n - 1, 1 - j)
                images(pe, image)
                offsets(IMAGES - 1, 1)
                pe.wait_ge(stat, 6)
                pe.transpose(p_stat[0:1, 0:P], fone[:], ident[:]).then_inc(avg, 1)


def sample_fast(nc, d, X, VP, OM):
    ROWS = 3 * GROUPS * 5
    pool_taps = (1, 5, 8, 12, 15, 19, 22)
    dve_taps = [t for t in range(WIN5) if t not in pool_taps]
    TAPS = dict(a=dve_taps[1::2], b=dve_taps[0::2], c=pool_taps)
    kind = {t: k for k in TAPS for t in TAPS[k]}
    NA, NBT, NC = (len(TAPS[k]) for k in "abc")
    ND = NA + NBT
    LAGS = dict(a=4, c=7)
    CLOSE, TAKE = 11, 14
    ROUNDS = (8, 12, 16)
    with ExitStack() as st:
        ident = sb(nc, st, "s_ident", [P, P], BF16)
        sel = sb(nc, st, "s_sel", [ROWS, 5, P], BF16)
        opT = sb(nc, st, "s_opT", [P, P])
        zero = sb(nc, st, "s_zero", [P, 1])
        A = sb(nc, st, "s_A", [P, TPC, GROUPS, WIN5])
        MY = sb(nc, st, "s_MY", [P, 3, TPC, GK])
        PR = sb(nc, st, "s_PR", [P, 3, 3, TPC, GK])
        rest = sb(nc, st, "s_rest", [P, TPC, 5, GROUPS * 5])
        parts = sb(nc, st, "s_parts", [P, TPC, 5, 3, GROUPS * 5], BF16)
        AT = [sb(nc, st, f"s_AT{j}", [ROWS, 5, CH], BF16) for j in range(2)]
        prod_a = [sb(nc, st, f"s_pa{i}", [P, CH]) for i in range(3)]
        prod_b = [sb(nc, st, f"s_pb{i}", [P, CH]) for i in range(3)]
        prod_c = [sb(nc, st, f"s_pc{i}", [P, CH]) for i in range(2)]
        wide = [sb(nc, st, f"s_wide{i}", [P, CH]) for i in range(2)]
        acc = [sb(nc, st, f"s_acc{j}", [P, CH]) for j in range(2)]
        NB = 5
        p_bc = [ps(nc, st, f"s_pbc{i}") for i in range(NB)]
        p_out = [ps(nc, st, f"s_pout{j}") for j in range(2)]
        p_tr = ps(nc, st, "s_ptr", (P, 2, CH), BF16)

        w_in = sem(nc, st, "s_w_in")
        zeroed = sem(nc, st, "s_zeroed")
        cast = sem(nc, st, "s_cast")
        cleared = sem(nc, st, "s_cleared")
        step = sem(nc, st, "s_step")
        coef = sem(nc, st, "s_coef")
        high = sem(nc, st, "s_high")
        left = sem(nc, st, "s_left")
        mid = sem(nc, st, "s_mid")
        low = sem(nc, st, "s_low")
        turned = sem(nc, st, "s_turned")
        stored = sem(nc, st, "s_stored")
        bc = sem(nc, st, "s_bc")
        mul = sem(nc, st, "s_mul")
        widened = sem(nc, st, "s_widened")
        mul_c = sem(nc, st, "s_mul_c")
        summed = sem(nc, st, "s_summed")
        sum_a = sem(nc, st, "s_sum_a")
        sum_c = sem(nc, st, "s_sum_c")
        outp = sem(nc, st, "s_outp")
        resid = sem(nc, st, "s_resid")
        STEPS = 5

        def known(c):
            return isinstance(c, int)

        def chunks(eng, chunk):
            chunk(0, 0, 0)
            chunk(1, 1, 0)
            with eng.Fori(1, IMAGES - 1) as n:
                chunk(n * 2, 0, n)
                chunk(n * 2 + 1, 1, n)
            chunk(NCH - 2, 0, IMAGES - 1)
            chunk(NCH - 1, 1, IMAGES - 1)

        def window(n, h, t):
            y, x = t // 5, t % 5
            return VP[:, bass.ds(n, 1), h * HALF + y:h * HALF + y + HALF, x:x + SIDE] \
                .rearrange("p o a b -> p (o a) b")

        with nc.Block() as block:
            @block.sync
            def _(sp):
                sp.dma_start(A[:].rearrange("p t g w -> p (t g w)")[:, 0:P], d["c_ident"]).then_inc(w_in, 16)
                sp.dma_start(opT[:], d["op_wT"]).then_inc(w_in, 16)
                sp.dma_start(PR[0:ROWS].rearrange("p a b t k -> p (a b t k)")[:, 0:5 * P],
                             d["c_select"].rearrange("r b c -> r (b c)")).then_inc(w_in, 16)

            @block.gpsimd
            def _(pool):
                nc.gpsimd.memset(zero[:], 0.0).then_inc(zeroed, 1)
                pool.wait_ge(cast, 2)
                nc.gpsimd.memset(A[:], 0.0).then_inc(cleared, 1)

                def chunk(c, j, n):
                    for t in range(WIN5):
                        if kind[t] == "b" and t != TAPS["b"][0]:
                            b = TAPS["b"].index(t)
                            pool.wait_ge(mul, c * ND + dve_taps.index(t) + 1)
                            if b == 1:
                                if not known(c) or c >= 2:
                                    pool.wait_ge(outp, c - 1)
                                before = prod_b[0][:]
                            else:
                                pool.wait_ge(summed, c * (NBT - 1) + b - 1)
                                before = acc[j][:]
                            nc.gpsimd.tensor_tensor(acc[j][:], before, prod_b[b % 3][:], ALU.add)\
                              .then_inc(summed, 1)
                        if kind[t] == "c":
                            i = TAPS["c"].index(t)
                            k = (j * NC + i) % 2
                            pool.wait_ge(widened, c * NC + i + 1)
                            if not known(c) or c * NC + i >= 2:
                                pool.wait_ge(sum_c, c * NC + i - 1)
                            nc.gpsimd.tensor_tensor(
                                prod_c[k][:].rearrange("p (a b) -> p a b", a=HALF),
                                wide[k][:].rearrange("p (a b) -> p a b", a=HALF),
                                window(n, j, t), ALU.mult).then_inc(mul_c, 1)
                chunks(pool, chunk)

            @block.scalar
            def _(act):
                act.wait_ge(w_in, 48)
                act.wait_ge(zeroed, 1)
                act.activation(ident[:], A[:].rearrange("p t g w -> p (t g w)")[:, 0:P], ACT.Copy)\
                   .then_inc(cast, 1)
                act.activation(sel[:].rearrange("p b c -> p (b c)"),
                               PR[0:ROWS].rearrange("p a b t k -> p (a b t k)")[:, 0:5 * P], ACT.Copy)\
                   .then_inc(cast, 1)

                def take_high(c):
                    act.wait_ge(coef, c * 9 + 9)
                    if not known(c) or c:
                        act.wait_ge(turned, c * 3)
                    for t in range(TPC):
                        act.activation(parts[:, t, :, 0].rearrange("p q (g b) -> p q g b", b=5),
                                       A[:, t].rearrange("p g (q b) -> p q g b", b=5),
                                       ACT.Copy).then_inc(high, 1)

                def take_mid(c):
                    act.wait_ge(left, c * TPC + TPC)
                    act.activation(parts[:, :, :, 1], rest[:], ACT.Copy).then_inc(mid, 1)
                    act.activation(A[:].rearrange("p t g w -> p (t g w)"),
                                   zero[:].to_broadcast([P, TPC * GROUPS * WIN5]), ACT.Copy)\
                       .then_inc(cleared, 1)

                def store_rows(c, j, r):
                    if r == 0 and (not known(c) or c >= 2):
                        act.wait_ge(bc, (c - 1) * WIN5)
                    act.wait_ge(turned, c * 3 + r + 1)
                    q, w = 2 * r, min(2, 5 - 2 * r)
                    act.activation(AT[j][:, q:q + w], p_tr[0:ROWS, 0:w], ACT.Copy).then_inc(stored, 1)

                def chunk(c, j, n):
                    for t in range(WIN5):
                        ahead = not known(c) or c + 1 < NCH
                        if ahead and t == 0:
                            take_high(c + 1)
                        if ahead and t == 5:
                            take_mid(c + 1)
                        if ahead and t in (13, 16, 20):
                            store_rows(c + 1, 1 - j, (13, 16, 20).index(t))
                        if kind[t] == "c":
                            i = TAPS["c"].index(t)
                            act.wait_ge(bc, c * WIN5 + t + 1)
                            if not known(c) or c * NC + i >= 2:
                                act.wait_ge(mul_c, c * NC + i - 1)
                            act.activation(wide[(j * NC + i) % 2][:], p_bc[t % NB][:], ACT.Copy)\
                               .then_inc(widened, 1)

                take_high(0)
                take_mid(0)
                for r in range(3):
                    store_rows(0, 0, r)
                chunks(act, chunk)

            @block.vector
            def _(dve):
                flat = "p r t k -> p r (t k)"
                WEIGHT_STEPS = 17

                def weights(c, k):
                    om = OM[:, bass.ds(c * TPC, TPC), :]
                    oy, ox, m = om[:, :, 0:GK], om[:, :, GK:2 * GK], om[:, :, 2 * GK:3 * GK]
                    b = c * STEPS
                    if k == 0:
                        dve.scalar_tensor_tensor(MY[:, 2], oy, 0.0, m, ALU.max, ALU.mult)
                        dve.scalar_tensor_tensor(MY[:, 0], oy, 0.0, m, ALU.min, ALU.mult).then_inc(step, 1)
                    elif k == 1:
                        dve.wait_ge(step, b + 1)
                        dve.tensor_tensor(MY[:, 1], m, MY[:, 2], ALU.subtract).then_inc(step, 1)
                    elif k == 2:
                        dve.wait_ge(step, b + 2)
                        dve.tensor_tensor(MY[:, 1], MY[:, 1], MY[:, 0], ALU.add).then_inc(step, 1)
                    elif k < 6:
                        if k == 3:
                            dve.wait_ge(step, b + 3)
                        for r, q, op in (((0, 2, ALU.max), (1, 2, ALU.max)), ((2, 2, ALU.max), (0, 0, ALU.min)),
                                         ((1, 0, ALU.min), (2, 0, ALU.min)))[k - 3]:
                            ins = dve.scalar_tensor_tensor(PR[:, r, q], ox, 0.0, MY[:, r], op, ALU.mult)
                        if k == 5:
                            ins.then_inc(step, 1)
                    elif k == 6:
                        dve.wait_ge(step, b + 4)
                        dve.tensor_tensor(PR[:, :, 1].rearrange(flat), MY[:].rearrange(flat),
                                          PR[:, :, 2].rearrange(flat), ALU.subtract).then_inc(step, 1)
                    elif k == 7:
                        dve.wait_ge(step, b + 5)
                        dve.tensor_tensor(PR[:, :, 1].rearrange(flat), PR[:, :, 1].rearrange(flat),
                                          PR[:, :, 0].rearrange(flat), ALU.add)
                    else:
                        i = k - 8
                        q, r = (0, 2, 1)[i // 3], i % 3
                        v = A[:].rearrange("p t g (a b) -> p (t g) a b", a=5)[:, :, r:r + 3, q:q + 3]
                        w = PR[:, r, q].rearrange("p t (g a b) -> p (t g) a b", a=3, b=3)
                        if i:
                            dve.wait_ge(coef, c * 9 + i)
                        else:
                            dve.wait_ge(cleared, c + 1)
                        dve.tensor_tensor(v, v, w, ALU.subtract if (r == 0) != (q == 0) else ALU.add)\
                           .then_inc(coef, 1)

                def split_rest(c):
                    for t in range(TPC):
                        dve.wait_ge(high, c * TPC + t + 1)
                        dve.tensor_tensor(rest[:, t].rearrange("p q (g b) -> p q g b", b=5),
                                          A[:, t].rearrange("p g (q b) -> p q g b", b=5),
                                          parts[:, t, :, 0].rearrange("p q (g b) -> p q g b", b=5),
                                          ALU.subtract).then_inc(left, 1)

                def split_low(c):
                    dve.wait_ge(mid, c + 1)
                    dve.tensor_tensor(parts[:, :, :, 2], rest[:], parts[:, :, :, 1], ALU.subtract)\
                       .then_inc(low, 1)

                def multiply(c, n, h, t):
                    dve.wait_ge(bc, c * WIN5 + t + 1)
                    if kind[t] == "a":
                        a = TAPS["a"].index(t)
                        out = prod_a[a % 3]
                        if not known(c) or c * NA + a >= 3:
                            dve.wait_ge(sum_a, c * NA + a - 2)
                    else:
                        b = TAPS["b"].index(t)
                        out = prod_b[b % 3]
                        if b >= 3:
                            dve.wait_ge(summed, c * (NBT - 1) + max(b - 3, 1))
                        elif not known(c) or c:
                            dve.wait_ge(summed, c * (NBT - 1) + b - 2)
                    dve.tensor_tensor(out[:].rearrange("p (a b) -> p a b", a=HALF),
                                      p_bc[t % NB][:].rearrange("p (a b) -> p a b", a=HALF),
                                      window(n, h, t), ALU.mult).then_inc(mul, 1)

                def residual(c, j):
                    dve.wait_ge(outp, c + 1)
                    cols = X[:, bass.ds(c * CH, CH)]
                    dve.tensor_tensor(cols, cols, p_out[j][:], ALU.add).then_inc(resid, 1)

                def chunk(c, j, n):
                    for t in range(WIN5):
                        if kind[t] != "c":
                            multiply(c, n, j, t)
                        if not known(c) or c + 1 < NCH:
                            if t == 1:
                                split_rest(c + 1)
                            if t == 5:
                                split_low(c + 1)
                        if (not known(c) or c + 2 < NCH) and 5 <= t < 5 + WEIGHT_STEPS:
                            weights(c + 2, t - 5)
                        if t == TAKE and (not known(c) or c):
                            residual(c - 1, 1 - j)

                dve.wait_ge(cast, 2)
                for k in range(WEIGHT_STEPS):
                    weights(0, k)
                split_rest(0)
                split_low(0)
                for k in range(WEIGHT_STEPS):
                    weights(1, k)
                chunks(dve, chunk)
                residual(NCH - 1, 1)

            @block.tensor
            def _(pe):
                pe.wait_ge(cast, 2)

                def turn(c, r):
                    if r == 0:
                        pe.wait_ge(low, c + 1)
                    if not known(c) or c * 3 + r:
                        pe.wait_ge(stored, c * 3 + r)
                    for q in range(2 * r, min(2 * r + 2, 5)):
                        for t in range(TPC):
                            last = pe.transpose(p_tr[0:ROWS, q % 2, t * P:(t + 1) * P],
                                                parts[:, t, q].rearrange("p a b -> p (a b)"), ident[:])
                    last.then_inc(turned, 1)

                def spread(c, j, t):
                    if t % 10 == 0:
                        pe.wait_ge(stored, c * 3 + t // 10 + 1)
                    b = (t - NB) % WIN5
                    back = 0 if t >= NB else 1
                    if not known(c) or c >= back:
                        if kind[b] == "c":
                            pe.wait_ge(widened, c * NC + (TAPS["c"].index(b) + 1 - back * NC))
                        else:
                            pe.wait_ge(mul, c * ND + (dve_taps.index(b) + 1 - back * ND))
                    pe.matmul(p_bc[t % NB][:], sel[:, t % 5, :], AT[j][:, t // 5, :],
                              start=True, stop=True).then_inc(bc, 1)

                def sum_up(c, j, t):
                    if kind[t] == "a":
                        a = TAPS["a"].index(t)
                        pe.wait_ge(mul, c * ND + dve_taps.index(t) + 1)
                        if a == 0 and (not known(c) or c >= 2):
                            pe.wait_ge(resid, c - 1)
                        pe.matmul(p_out[j][:], opT[:], prod_a[a % 3][:], start=(a == 0), stop=False)\
                          .then_inc(sum_a, 1)
                    else:
                        i = TAPS["c"].index(t)
                        pe.wait_ge(mul_c, c * NC + i + 1)
                        pe.matmul(p_out[j][:], opT[:], prod_c[(j * NC + i) % 2][:], start=False, stop=False)\
                          .then_inc(sum_c, 1)

                def close(c, j):
                    pe.wait_ge(summed, c * (NBT - 1) + (NBT - 1))
                    pe.matmul(p_out[j][:], opT[:], acc[j][:], start=False, stop=True).then_inc(outp, 1)

                def sums_due(c, j, t):
                    for k in "ac":
                        b = t - LAGS[k]
                        if b < 0 and kind[b + WIN5] == k and (not known(c) or c):
                            sum_up(c - 1, 1 - j, b + WIN5)
                        if 0 <= b < WIN5 and kind[b] == k:
                            sum_up(c, j, b)

                def chunk(c, j, n):
                    for t in range(WIN5):
                        spread(c, j, t)
                        sums_due(c, j, t)
                        if t in ROUNDS and (not known(c) or c + 1 < NCH):
                            turn(c + 1, ROUNDS.index(t))
                        if t == CLOSE and (not known(c) or c):
                            close(c - 1, 1 - j)

                for r in range(3):
                    turn(0, r)
                chunks(pe, chunk)
                for t in range(max(LAGS.values())):
                    for k in "ac":
                        b = t + WIN5 - LAGS[k]
                        if b < WIN5 and kind[b] == k:
                            sum_up(NCH - 1, 1, b)
                close(NCH - 1, 1)


def sample_general(nc, d, X, VP, OM, flag):
    TPI = PIX // P
    with ExitStack() as st:
        ident = sb(nc, st, "g_ident", [P, P])
        opT = sb(nc, st, "g_opT", [P, P])
        line = sb(nc, st, "g_line", [P, SIDE])
        pix = sb(nc, st, "g_pix", [P, TPI, 2])
        kern = sb(nc, st, "g_kern", [P, 2, GK])
        pos = sb(nc, st, "g_pos", [P, 2, GK])
        W = [sb(nc, st, f"g_W{a}", [P, GK, SIDE]) for a in range(2)]
        outer = sb(nc, st, "g_outer", [P, SIDE, SIDE])
        AG = sb(nc, st, "g_AG", [P, PIX])
        AGT = sb(nc, st, "g_AGT", [P, TPI, P])
        VC = sb(nc, st, "g_VC", [P, PIX])
        VT = sb(nc, st, "g_VT", [P, TPI, P])
        S = sb(nc, st, "g_S", [P, P])
        ST = sb(nc, st, "g_ST", [P, P])
        p_tr = [ps(nc, st, f"g_ptr{i}") for i in range(2)]
        p_s = ps(nc, st, "g_ps", (P, P))
        p_st = ps(nc, st, "g_pst", (P, P))
        p_o = ps(nc, st, "g_po", (P, P))
        w_in = sem(nc, st, "g_w_in")
        image = sem(nc, st, "g_image")
        vturn = sem(nc, st, "g_vturn")
        vout = sem(nc, st, "g_vout")
        step = sem(nc, st, "g_step")
        dist = sem(nc, st, "g_dist")
        tent = sem(nc, st, "g_tent")
        part = sem(nc, st, "g_part")
        wsum = sem(nc, st, "g_wsum")
        turned = sem(nc, st, "g_turned")
        moved = sem(nc, st, "g_moved")
        applied = sem(nc, st, "g_applied")
        sout = sem(nc, st, "g_sout")
        sturn = sem(nc, st, "g_sturn")
        stout = sem(nc, st, "g_stout")
        projected = sem(nc, st, "g_projected")
        added = sem(nc, st, "g_added")

        with nc.Block() as block:
            @block.sync
            def _(sp):
                far = sp.value_load(flag[0:1, 0:1])
                with sp.If(far > 0):
                    for n in range(IMAGES):
                        sp.dma_start(X[:, n * PIX:(n + 1) * PIX], d["x"][n]).then_inc(w_in, 16)
                    for dst, src in ((ident, "c_ident"), (opT, "op_wT"), (pix, "c_pixel"), (kern, "c_kernel"),
                                     (line, "c_line")):
                        sp.dma_start(dst[:], d[src]).then_inc(w_in, 16)
                sp.nop()

            @block.vector
            def _(dve):
                far = dve.value_load(flag[0:1, 0:1])
                with dve.If(far > 0):
                    dve.wait_ge(w_in, 16 * (IMAGES + 5))
                    with dve.Fori(0, IMAGES) as n:
                        dve.wait_ge(vturn, n)
                        dve.tensor_copy(VC[:].rearrange("p (a b) -> p a b", a=SIDE),
                                        VP[:, bass.ds(n, 1), 2:2 + SIDE, 2:2 + SIDE]
                                        .rearrange("p o a b -> p (o a) b")).then_inc(image, 1)
                        with dve.Fori(0, TPI) as t:
                            c = n * TPI + t
                            for a in range(2):
                                dve.scalar_tensor_tensor(
                                    pos[:, a], OM[:, bass.ds(c, 1), a * GK:(a + 1) * GK]
                                    .rearrange("p o k -> p (o k)"), pix[:, bass.ds(t, 1), a]
                                    , kern[:, a], ALU.add, ALU.add).then_inc(step, 1)
                            dve.wait_ge(step, c * 2 + 2)
                            for a in range(2):
                                dve.tensor_tensor(
                                    W[a][:], pos[:, a].rearrange("p (k o) -> p k o", o=1)
                                    .to_broadcast([P, GK, SIDE]),
                                    line[:].rearrange("p (o s) -> p o s", o=1).to_broadcast([P, GK, SIDE]),
                                    ALU.subtract).then_inc(dist, 1)
                            dve.wait_ge(tent, c * 2 + 2)
                            dve.tensor_tensor(
                                W[0][:], W[0][:], OM[:, bass.ds(c, 1), 2 * GK:3 * GK]
                                .rearrange("p o k -> p k o").to_broadcast([P, GK, SIDE]),
                                ALU.mult).then_inc(part, 1)
                            with dve.Fori(0, GROUPS) as g:
                                cg = c * GROUPS + g
                                dve.wait_ge(turned, cg * 2)
                                for k in range(K):
                                    wy = W[0][:, bass.ds(g * K + k, 1), :].rearrange("p o s -> p s o")\
                                        .to_broadcast([P, SIDE, SIDE])
                                    wx = W[1][:, bass.ds(g * K + k, 1), :].to_broadcast([P, SIDE, SIDE])
                                    dve.wait_ge(part, (c + 1) + cg * 17 + max(2 * k - 1, 0))
                                    out = AG[:].rearrange("p (a b) -> p a b", a=SIDE) if k == 0 else outer[:]
                                    dve.tensor_tensor(out, wy, wx, ALU.mult).then_inc(part, 1)
                                    if k:
                                        dve.wait_ge(part, (c + 1) + cg * 17 + 2 * k)
                                        dve.tensor_tensor(AG[:], AG[:], outer[:].rearrange("p a b -> p (a b)"),
                                                          ALU.add).then_inc(part, 1)
                                dve.wait_ge(part, (c + 1) + cg * 17 + 17)
                                dve.tensor_copy(pos[0:1, 0, 0:1], pos[0:1, 0, 0:1]).then_inc(wsum, 1)
                            dve.wait_ge(applied, c * GROUPS + GROUPS)
                            dve.tensor_copy(S[:], p_s[:]).then_inc(sout, 1)
                            dve.wait_ge(sturn, c + 1)
                            dve.tensor_copy(ST[:], p_st[:]).then_inc(stout, 1)
                            dve.wait_ge(projected, c + 1)
                            cols = X[:, bass.ds(c * P, P)]
                            dve.tensor_tensor(cols, cols, p_o[:], ALU.add).then_inc(added, 1)
                dve.engine_nop()

            @block.scalar
            def _(act):
                far = act.value_load(flag[0:1, 0:1])
                with act.If(far > 0):
                    with act.Fori(0, IMAGES) as n:
                        for h in range(2):
                            act.wait_ge(vturn, n + 1)
                            act.activation(VT[:, h * 4:h * 4 + 4].rearrange("p m c -> p (m c)"), p_tr[h][:],
                                           ACT.Copy).then_inc(vout, 1)
                        with act.Fori(0, TPI) as t:
                            c = n * TPI + t
                            for a in range(2):
                                act.wait_ge(dist, c * 2 + a + 1)
                                act.activation(W[a][:], W[a][:], ACT.Abs).then_inc(moved, 1)
                                act.wait_ge(moved, c * (2 + 2 * GROUPS) + a + 1)
                                act.activation(W[a][:], W[a][:], ACT.Relu, bias=1.0, scale=-1.0)\
                                   .then_inc(tent, 1)
                            with act.Fori(0, GROUPS) as g:
                                cg = c * GROUPS + g
                                act.wait_ge(applied, cg)
                                for h in range(2):
                                    act.wait_ge(turned, cg * 2 + h + 1)
                                    act.activation(AGT[:, h * 4:h * 4 + 4].rearrange("p m c -> p (m c)"),
                                                   p_tr[h][:], ACT.Copy).then_inc(moved, 1)
                act.nop()

            @block.tensor
            def _(pe):
                far = pe.value_load(flag[0:1, 0:1])
                with pe.If(far > 0):
                    pe.wait_ge(w_in, 16 * (IMAGES + 5))
                    with pe.Fori(0, IMAGES) as n:
                        pe.wait_ge(image, n + 1)
                        pe.wait_ge(moved, n * (TPI * (2 + 2 * GROUPS)))
                        for m in range(TPI):
                            last = pe.transpose(p_tr[m // 4][:, (m % 4) * P:(m % 4 + 1) * P],
                                                VC[:, m * P:(m + 1) * P], ident[:])
                        last.then_inc(vturn, 1)
                        with pe.Fori(0, TPI) as t:
                            c = n * TPI + t
                            with pe.Fori(0, GROUPS) as g:
                                cg = c * GROUPS + g
                                pe.wait_ge(vout, n * 2 + 2)
                                pe.wait_ge(sout, c)
                                pe.wait_ge(wsum, cg + 1)
                                for m in range(TPI):
                                    last = pe.transpose(p_tr[m // 4][:, (m % 4) * P:(m % 4 + 1) * P],
                                                        AG[:, m * P:(m + 1) * P], ident[:])
                                    if m % 4 == 3:
                                        last.then_inc(turned, 1)
                                pe.wait_ge(moved, c * (2 + 2 * GROUPS) + 2 + 2 * g + 2)
                                for m in range(TPI):
                                    last = pe.matmul(p_s[:, bass.ds(g * CG, CG)], AGT[:, m, :],
                                                     VT[:, m, bass.ds(g * CG, CG)],
                                                     start=(m == 0), stop=(m == TPI - 1))
                                last.then_inc(applied, 1)
                            pe.wait_ge(sout, c + 1)
                            pe.transpose(p_st[:], S[:], ident[:]).then_inc(sturn, 1)
                            pe.wait_ge(stout, c + 1)
                            pe.wait_ge(added, c)
                            pe.matmul(p_o[:], opT[:], ST[:], start=True, stop=True).then_inc(projected, 1)
                pe.nop()


def skewed(eng, steps, lags, body, period, first):
    for s in range(first):
        body(s, s % period, s // 2)
    with eng.Fori(first // period, steps // period) as i:
        for k in range(period):
            body(i * period + k, k, i * (period // 2) + k // 2)
    for s in range(steps, steps + lags):
        body(s, s % period, s // 2)


def within(c):
    return not isinstance(c, int) or 0 <= c < NCH


def some(c, n):
    return not isinstance(c, int) or c >= n


class Constants:

    def __init__(self, nc, st):
        self.center = sb(nc, st, "k_center", [P, P])
        self.ones = sb(nc, st, "k_ones", [P, P])
        self.ident = sb(nc, st, "k_ident", [P, P])
        self.eps = sb(nc, st, "k_eps", [P, 1])


def token_norm(nc, d, X, XA, const):
    LAGS = 1
    with ExitStack() as st:
        center, ones, eps = const.center, const.ones, const.eps
        sq = [sb(nc, st, f"n_sq{k}", [P, CH]) for k in range(4)]
        p_c = [ps(nc, st, f"n_pc{k}") for k in range(4)]
        p_v = [ps(nc, st, f"n_pv{k}") for k in range(4)]
        w_in = sem(nc, st, "n_w_in")
        cleared = sem(nc, st, "n_cleared")
        centered = sem(nc, st, "n_centered")
        squared = sem(nc, st, "n_squared")
        varied = sem(nc, st, "n_varied")
        inverted = sem(nc, st, "n_inverted")
        written = sem(nc, st, "n_written")

        with nc.Block() as block:
            @block.sync
            def _(sp):
                for dst, src in ((center, "c_center"), (ones, "c_ones"), (const.ident, "c_ident")):
                    sp.dma_start(dst[:], d[src]).then_inc(w_in, 16)

            @block.gpsimd
            def _(pool):
                nc.gpsimd.memset(eps[:], EPS).then_inc(cleared, 1)
                nc.gpsimd.memset(XA[:, :, 0:REACH], 0.0).then_inc(cleared, 1)
                nc.gpsimd.memset(XA[:, :, REACH + PIX:], 0.0).then_inc(cleared, 1)

            @block.tensor
            def _(pe):
                pe.wait_ge(w_in, 48)

                def step(s, k, h):
                    if within(s - 1):
                        pe.wait_ge(squared, s)
                        pe.matmul(p_v[(k - 1) % 4][:], ones[:], sq[(k - 1) % 4][:], start=True, stop=True)\
                          .then_inc(varied, 1)
                    if within(s):
                        if some(s, 4):
                            pe.wait_ge(written, s - 3)
                        pe.matmul(p_c[k][:], center[:], X[:, bass.ds(s * CH, CH)], start=True, stop=True)\
                          .then_inc(centered, 1)
                skewed(pe, NCH, LAGS, step, 4, 4)

            @block.scalar
            def _(act):
                act.preload_act_table_set("natural_log_exp_and_others")
                act.wait_ge(cleared, 3)

                def step(s, k, h):
                    if within(s):
                        act.wait_ge(centered, s + 1)
                        if some(s, 4):
                            act.wait_ge(written, s - 3)
                        act.activation(sq[k][:], p_c[k][:], ACT.Square).then_inc(squared, 1)
                    if within(s - 1):
                        b = (k - 1) % 4
                        act.wait_ge(varied, s)
                        act.activation(sq[b][:], p_v[b][:], ACT.Ln, bias=eps[:]).then_inc(inverted, 1)
                        act.wait_ge(inverted, s * 2 - 1)
                        act.activation(sq[b][:], sq[b][:], ACT.Exp, scale=-0.5).then_inc(inverted, 1)
                skewed(act, NCH, LAGS, step, 4, 4)

            @block.vector
            def _(dve):
                with dve.Fori(0, NCH // 4) as i:
                    for k in range(4):
                        c = i * 4 + k
                        dve.wait_ge(inverted, c * 2 + 2)
                        off = REACH + (k % 2) * CH
                        dve.tensor_tensor(XA[:, bass.ds(i * 2 + k // 2, 1), off:off + CH]
                                          .rearrange("p o w -> p (o w)"), p_c[k][:], sq[k][:],
                                          ALU.mult).then_inc(written, 1)


def attention(nc, d, XA, const):
    PADA = PIX + 2 * REACH
    VW = DV + 1
    NU = TOK // (UB * QB)
    NS = 2 * IMAGES
    US = NU // NS
    NB = US * UB
    NT = 2 * UB
    ROWS = CH + 2 * REACH
    with ExitStack() as st:
        ident = const.ident
        wq = sb(nc, st, "a_wq", [P, 2, P])
        wk = sb(nc, st, "a_wk", [P, 2, P])
        wv = sb(nc, st, "a_wv", [P, P])
        wo = sb(nc, st, "a_wo", [P, P])
        bq = sb(nc, st, "a_bq", [P, 2])
        bk = sb(nc, st, "a_bk", [P, 2])
        bv = sb(nc, st, "a_bv", [P, P])
        bo = sb(nc, st, "a_bo", [P, 1])
        bias = [sb(nc, st, f"a_bias{v}", [P, UB, 2, QW]) for v in range(3)]
        XS = [sb(nc, st, f"a_XS{j}", [P, ROWS]) for j in range(2)]
        Q = [sb(nc, st, f"a_Q{j}", [P, 2, NB, 4, QB]) for j in range(2)]
        KT = [sb(nc, st, f"a_KT{j}", [P, 2, PADA]) for j in range(2)]
        V = [sb(nc, st, f"a_V{j}", [QW, NB, HEADS, VW]) for j in range(2)]
        E = [sb(nc, st, f"a_E{b}", [P, NT, QW]) for b in range(2)]
        PT = [sb(nc, st, f"a_PT{b}", [QW, NT, P]) for b in range(2)]
        nm = sb(nc, st, "a_nm", [P, 2, NT])
        rsum = sb(nc, st, "a_rsum", [P, 2, HEADS])
        O = [sb(nc, st, f"a_O{b}", [P, P]) for b in range(2)]
        OT = [sb(nc, st, f"a_OT{j}", [P, CH]) for j in range(2)]
        p_s = ps(nc, st, "a_ps", (P, 2, CH))
        p_t = ps(nc, st, "a_pt", (P, 2, NT // 2, P))
        p_m = [ps(nc, st, f"a_pm{k}") for k in range(3)]
        p_o = ps(nc, st, "a_po")
        toeplitz = nc.dram_tensor("toeplitz", [4, QB, 2, QW], F32, kind="Internal").ap()

        w_in = sem(nc, st, "a_w_in")
        rel_in = sem(nc, st, "a_rel_in")
        masked = sem(nc, st, "a_masked")
        cleared = sem(nc, st, "a_cleared")
        staged = sem(nc, st, "a_staged")
        made = sem(nc, st, "a_made")
        act_took = sem(nc, st, "a_act_took")
        dve_took = sem(nc, st, "a_dve_took")
        scored = sem(nc, st, "a_scored")
        biased = sem(nc, st, "a_biased")
        maxed = sem(nc, st, "a_maxed")
        powered = sem(nc, st, "a_powered")
        turned = sem(nc, st, "a_turned")
        pt_dve = sem(nc, st, "a_pt_dve")
        pt_act = sem(nc, st, "a_pt_act")
        mixed = sem(nc, st, "a_mixed")
        scaled = sem(nc, st, "a_scaled")
        oturned = sem(nc, st, "a_oturned")
        ostored = sem(nc, st, "a_ostored")
        NW = 8

        LEAD = [(0, "q", 0, 0), (0, "q", 1, 0), (0, "k", 0, 0), (0, "k", 1, 0), (0, "v", 0, 0), (0, "v", 1, 0),
                (0, "v", 2, 0), (0, "v", 3, 0), (0, "k", 0, 1), (0, "k", 1, 1)]

        def plan(s):
            known = isinstance(s, int)
            ahead, keys, out = not known or s + 1 < NS, not known or s + 2 < NS, not known or s > 0
            return ([(0, "q", m, s + 1) for m in range(2)] * ahead + [(1, "k", m, s + 2) for m in range(2)] * keys
                    + [(2, "v", m, s + 1) for m in range(2)] * ahead + [(2, "o", 0, s - 1)] * out
                    + [(3, "v", m, s + 1) for m in range(2, 4)] * ahead)

        PER = len(plan(1))
        FIRST = len(LEAD) + len(plan(0))

        def start(s):
            if not isinstance(s, int) or 0 < s <= NS - 2:
                return s * PER + (FIRST - PER), s * (PER - 2) + (FIRST - 4 - (PER - 2)), s * 2 + 2
            kinds = [x[1] for x in LEAD + [y for h in range(s) for y in plan(h)]]
            return len(kinds), len(kinds) - kinds.count("q"), kinds.count("q")

        def numbered(s, unit=None):
            lead = isinstance(s, int) and s < 0
            items = LEAD if lead else plan(s)
            n0, d0, a0 = (0, 0, 0) if lead else start(s)
            if lead:
                before = []
            elif isinstance(s, int) and s == 0:
                before = [x[1] for x in LEAD]
            else:
                prev = plan(s - 1)
                before = [x[1] for x in prev] if len(prev) >= 3 else [x[1] for x in plan(s - 2) + prev]
            kinds = before + [x[1] for x in items]
            listed = []
            for i, item in enumerate(items):
                bank = (n0 + i) % 3 if isinstance(n0, int) else (FIRST + i) % 3
                here = [x[1] for x in items[:i]]
                at = len(before) + i - 3
                need = None
                if at >= 0:
                    q = kinds[at] == "q"
                    tail = kinds[at + 1:len(before) + i]
                    back = tail.count("q") if q else len(tail) - tail.count("q")
                    now = (a0 + here.count("q")) if q else (d0 + len(here) - here.count("q"))
                    need = (act_took if q else dve_took, now - back)
                if unit is None or item[0] == unit:
                    listed.append((item, n0 + i, bank, need))
            return listed

        def halves(eng, body):
            for s in range(2):
                body(s, s)
            with eng.Fori(0, (NS - 4) // 4) as i:
                for k in range(4):
                    body(i * 4 + (k + 2), (k + 2) % 4, i * 2 + (k + 2) // 2)
            for s in range(NS - 2, NS):
                body(s, s % 4)

        with nc.Block() as block:
            @block.sync
            def _(sp):
                for dst, src in ((wq, "wq"), (wk, "wk"), (wv, "wv"), (wo, "wo"), (bq, "bq"),
                                 (bk, "bk"), (bo, "bo")):
                    sp.dma_start(dst[:], d[src]).then_inc(w_in, 16)
                sp.dma_start(bv[:], d["bv"].partition_broadcast(P)).then_inc(w_in, 16)
                sp.wait_ge(masked, 1)
                flat = [[QB * 2 * QW, 4], [2 * QW + 1, QB], [1, 2 * REACH + 1]]
                sp.dma_start(toeplitz.rearrange("r i h w -> (r i) (h w)"),
                             bias[1][:, 0].rearrange("p h w -> p (h w)")).then_inc(rel_in, 16)
                sp.wait_ge(rel_in, 16)
                for hh in range(2):
                    dst = bass.AP(toeplitz.tensor, hh * QW, flat)
                    src = bass.AP(d["rel_bias"].tensor, hh * 4 * (2 * REACH + 1),
                                  [[2 * REACH + 1, 4], [0, QB], [1, 2 * REACH + 1]])
                    sp.dma_start(dst, src).then_inc(rel_in, 16)
                sp.wait_ge(rel_in, 48)
                for c in range(UB):
                    sp.dma_start(bias[1][:, c].rearrange("p h w -> p (h w)"),
                                 toeplitz.rearrange("r i h w -> (r i) (h w)")).then_inc(rel_in, 16)

            @block.gpsimd
            def _(pool):
                nc.gpsimd.memset(bias[1][:, 0], NEG).then_inc(masked, 1)
                nc.gpsimd.memset(Q[0][:], 0.0).then_inc(cleared, 1)
                for j in range(2):
                    nc.gpsimd.memset(KT[j][:, :, 0:REACH], 0.0).then_inc(cleared, 1)
                    nc.gpsimd.memset(KT[j][:, :, REACH + PIX:], 0.0).then_inc(cleared, 1)
                    nc.gpsimd.memset(V[j][:, :, :, DV:VW], 1.0).then_inc(cleared, 1)
                nc.gpsimd.memset(Q[1][:], 0.0).then_inc(cleared, 1)
                pool.wait_ge(rel_in, 16 * (3 + UB))
                for v in (0, 2):
                    nc.gpsimd.tensor_copy(bias[v][:], bias[1][:]).then_inc(masked, 1)
                pool.wait_ge(masked, 3)
                nc.gpsimd.memset(bias[0][:, 0, :, 0:REACH], NEG).then_inc(masked, 1)
                nc.gpsimd.memset(bias[2][:, UB - 1, :, QW - REACH:], NEG).then_inc(masked, 1)

            @block.tensor
            def _(pe):
                pe.wait_ge(w_in, 16 * NW)
                pe.wait_ge(cleared, 8)

                def product(item, number, bank, need, img=None):
                    _, kind, m, s = item
                    if need is not None:
                        pe.wait_ge(*need)
                    out = p_m[bank]
                    if kind in "qk":
                        w = wq if kind == "q" else wk
                        n, h = (img[kind] if img else (s // 2, s % 2))
                        src = XA[:, bass.ds(n, 1), REACH + h * CH:REACH + (h + 1) * CH] \
                            .rearrange("p o w -> p (o w)")
                        last = pe.matmul(out[:], w[:, m, :], src, start=True, stop=True)
                    elif kind == "v":
                        pe.wait_ge(staged, s + 1)
                        j = img["ring"] if img else s % 2
                        for b in range(UB):
                            at = (m * UB + b) * QB
                            last = pe.matmul(out[0:QW, b * P:(b + 1) * P], XS[j][:, at:at + QW], wv[:],
                                             start=True, stop=True)
                    else:
                        pe.wait_ge(ostored, (s + 1) * US)
                        j = (img["ring"] if img else s % 2)
                        last = pe.matmul(out[:], wo[:], OT[j][:], start=True, stop=True)
                    last.then_inc(made, 1)

                def scores(t, place, u, lead):
                    j, kj, hf = place % 2, (place // 2) % 2, place % 2
                    if lead:
                        pe.wait_ge(act_took, lead[0])
                        pe.wait_ge(dve_took, lead[1])
                    if not isinstance(t, int) or t:
                        pe.wait_ge(biased, t)
                    for c in range(UB):
                        for hh in range(2):
                            blk = u * UB + c
                            at = hf * CH + blk * QB
                            o = c * 2 + hh
                            last = pe.matmul(p_s[:, o // 4, (o % 4) * QW:(o % 4 + 1) * QW],
                                             Q[j][:, hh, blk].rearrange("p r q -> p (r q)"),
                                             KT[kj][:, hh, at:at + QW], start=True, stop=True)
                    last.then_inc(scored, 1)

                def turn(t, u):
                    for b in range(2):
                        for k in range(NT // 2):
                            o = b * (NT // 2) + k
                            pe.wait_ge(powered, t * NT + o + 1)
                            if k == 0 and (not isinstance(t, int) or t):
                                pe.wait_ge((pt_dve, pt_act)[b], t)
                            last = pe.transpose(p_t[0:QW, b, k, :], E[u % 2][:, o, :], ident[:])
                        last.then_inc(turned, 1)

                def mix(t, place, u):
                    j = place % 2
                    pe.wait_ge(pt_dve, t + 1)
                    pe.wait_ge(pt_act, t + 1)
                    if not isinstance(t, int) or t:
                        pe.wait_ge(scaled, t * 2)
                        pe.wait_ge(ostored, t)
                    for o in range(HEADS):
                        for c in range(UB):
                            hh, r = o // 4, o % 4
                            last = pe.matmul(p_o[c * QB:(c + 1) * QB, o * VW:(o + 1) * VW],
                                             PT[u % 2][:, c * 2 + hh, r * QB:(r + 1) * QB],
                                             V[j][:, u * UB + c, o, :], start=True, stop=True)
                    last.then_inc(mixed, 1)

                def turn_out(t, u):
                    pe.wait_ge(scaled, t * 2 + 2)
                    if not isinstance(t, int) or t:
                        pe.wait_ge(ostored, t)
                    pe.transpose(p_o[:, HEADS * VW:HEADS * VW + P], O[u % 2][:], ident[:])\
                      .then_inc(oturned, 1)

                for x in numbered(-1):
                    product(*x)
                scores(0, 0, 0, (2, 8))

                def body(s, place, n=None):
                    loop = n is not None
                    known = isinstance(s, int)
                    if loop:
                        img = dict(q=(n + (place % 2), (place + 1) % 2), k=(n + 1, place % 2))
                    for u in range(US):
                        t = s * US + u
                        if not known or t + 1 < NU:
                            nxt = (u + 1) // US
                            lead = None
                            if nxt:
                                _, dn, an = start(s)
                                lead = (an + 2, dn + (2 if not known or s + 2 < NS else 0))
                            scores(t + 1, (place + nxt) % 4, (u + 1) % US, lead)
                        if not known or t >= 2:
                            turn_out(t - 2, u)
                        due = numbered(s, u)
                        for k, x in enumerate(due):
                            if k == 1:
                                turn(t, u)
                            if loop:
                                ring = (place + 1) % 2
                                product(*x, img=dict(img, ring=ring))
                            else:
                                product(*x)
                        if len(due) < 2:
                            turn(t, u)
                        if not known or t >= 1:
                            if u == 1:
                                pe.wait_ge(dve_took, start(s)[1])
                            mix(t - 1, place if u else (place - 1) % 4, (u - 1) % US)
                halves(pe, body)
                turn_out(NU - 2, US)
                mix(NU - 1, (NS - 1) % 4, US - 1)
                turn_out(NU - 1, US + 1)
                n_all = start(NS)
                product((0, "o", 0, NS - 1), n_all[0], n_all[0] % 3, (dve_took, n_all[1]))

            @block.scalar
            def _(act):
                act.wait_ge(w_in, 16 * NW)
                act.wait_ge(cleared, 8)

                def take(item, number, bank, need, ring):
                    m = item[2]
                    act.wait_ge(made, number + 1)
                    for r in range(4):
                        rows = slice(r * QB, (r + 1) * QB)
                        ins = act.activation(Q[ring][rows, m, :, r, :],
                                             p_m[bank][rows].rearrange("p (b q) -> p b q", q=QB),
                                             ACT.Identity, bias=bq[rows, m:m + 1])
                    ins.then_inc(act_took, 1)

                def exps(t, u):
                    act.wait_ge(maxed, t + 1)
                    for o in range(NT):
                        act.activation(E[u % 2][:, o, :], E[u % 2][:, o, :], ACT.Exp,
                                       bias=nm[:, u % 2, o:o + 1]).then_inc(powered, 1)

                def copy_pt(t, u):
                    act.wait_ge(turned, t * 2 + 2)
                    if not isinstance(t, int) or t >= 2:
                        act.wait_ge(mixed, t - 1)
                    act.activation(PT[u % 2][:, NT // 2:, :], p_t[0:QW, 1], ACT.Copy).then_inc(pt_act, 1)

                def copy_out(t, place, u):
                    act.wait_ge(oturned, t + 1)
                    act.activation(OT[place % 2][:, u * P:(u + 1) * P],
                                   p_o[:, HEADS * VW:HEADS * VW + P], ACT.Copy).then_inc(ostored, 1)

                for x in numbered(-1):
                    if x[0][1] == "q":
                        take(*x, 0)
                exps(0, 0)

                def body(s, place, n=None):
                    known = isinstance(s, int)
                    for u in range(US):
                        t = s * US + u
                        if not known or t >= 2:
                            copy_out(t - 2, place if u >= 2 else (place - 1) % 4, (u - 2) % US)
                        for x in numbered(s, u):
                            if x[0][1] == "q":
                                take(*x, (place + 1) % 2)
                        if not known or t + 1 < NU:
                            exps(t + 1, u + 1)
                        copy_pt(t, u)
                halves(act, body)
                copy_out(NU - 2, (NS - 1) % 4, US - 2)
                copy_out(NU - 1, (NS - 1) % 4, US - 1)

            @block.vector
            def _(dve):
                dve.wait_ge(w_in, 16 * NW)
                dve.wait_ge(cleared, 8)

                def stage(s, ring, n, h):
                    dve.tensor_copy(XS[ring][:], XA[:, bass.ds(n, 1), h * CH:h * CH + ROWS]
                                    .rearrange("p o w -> p (o w)")).then_inc(staged, 1)

                def take(item, number, bank, need, ring, kj, kh, n, h):
                    _, kind, m, s = item
                    dve.wait_ge(made, number + 1)
                    if kind == "k":
                        at = REACH + kh * CH
                        dve.tensor_scalar(KT[kj][:, m, at:at + CH], p_m[bank][:], bk[:, m:m + 1], None,
                                          ALU.add).then_inc(dve_took, 1)
                    elif kind == "v":
                        dve.tensor_tensor(V[ring][:, m * UB:(m + 1) * UB, :, 0:DV],
                                          p_m[bank][0:QW].rearrange("p (b h w) -> p b h w", b=UB, h=HEADS),
                                          bv[0:QW].rearrange("p (o h w) -> p o h w", o=1, h=HEADS)
                                          .to_broadcast([QW, UB, HEADS, DV]), ALU.add).then_inc(dve_took, 1)
                    else:
                        cols = XA[:, bass.ds(n, 1), REACH + h * CH:REACH + (h + 1) * CH] \
                            .rearrange("p o w -> p (o w)")
                        dve.scalar_tensor_tensor(cols, p_m[bank][:], bo[:], cols, ALU.add, ALU.add)\
                           .then_inc(dve_took, 1)

                def soft(t, place, u):
                    which = 0 if (place % 2, u) == (0, 0) else 2 if (place % 2, u) == (1, US - 1) else 1
                    dve.wait_ge(scored, t + 1)
                    if not isinstance(t, int) or t >= 2:
                        dve.wait_ge(turned, (t - 1) * 2)
                    dve.scalar_tensor_tensor(
                        E[u % 2][:].rearrange("p (b o) w -> p b (o w)", b=2),
                        p_s[:, :, 0:NT // 2 * QW], float(DK) ** -0.5,
                        bias[which][:].rearrange("p (b c) h w -> p b (c h w)", b=2), ALU.mult, ALU.add)\
                       .then_inc(biased, 1)
                    dve.wait_ge(biased, t + 1)
                    dve.tensor_reduce(nm[:, u % 2, :], E[u % 2][:], AX.X, ALU.max, negate=True)\
                       .then_inc(maxed, 1)

                def copy_pt(t, u):
                    dve.wait_ge(turned, t * 2 + 1)
                    if not isinstance(t, int) or t >= 2:
                        dve.wait_ge(mixed, t - 1)
                    dve.tensor_copy(PT[u % 2][:, 0:NT // 2, :], p_t[0:QW, 0]).then_inc(pt_dve, 1)

                def scale(t, u):
                    dve.wait_ge(mixed, t + 1)
                    if not isinstance(t, int) or t >= 2:
                        dve.wait_ge(oturned, t - 1)
                    po = p_o[:, 0:HEADS * VW].rearrange("p (h w) -> p h w", h=HEADS)
                    dve.reciprocal(rsum[:, u % 2, :], po[:, :, DV]).then_inc(scaled, 1)
                    dve.wait_ge(scaled, t * 2 + 1)
                    dve.tensor_tensor(O[u % 2][:].rearrange("p (h w) -> p h w", h=HEADS), po[:, :, 0:DV],
                                      rsum[:, u % 2, :].rearrange("p (h o) -> p h o", o=1)
                                      .to_broadcast([P, HEADS, DV]), ALU.mult).then_inc(scaled, 1)

                stage(0, 0, 0, 0)
                for x in numbered(-1):
                    if x[0][1] != "q":
                        take(*x, 0, 0, x[0][3], 0, 0)
                stage(1, 1, 0, 1)
                dve.wait_ge(masked, 5)
                soft(0, 0, 0)

                def body(s, place, n=None):
                    known = isinstance(s, int)
                    n_ = s // 2 if known else n
                    for u in range(US):
                        t = s * US + u
                        if not known or t + 1 < NU:
                            soft(t + 1, (place + (u + 1) // US) % 4, (u + 1) % US)
                        for x in numbered(s, u):
                            if x[0][1] != "q":
                                take(*x, (place + 1) % 2, (place // 2 + 1) % 2, place % 2,
                                     n_ if place % 2 else n_ - 1, (place + 1) % 2)
                        copy_pt(t, u)
                        if not known or t >= 1:
                            scale(t - 1, u - 1)
                        if u == US - 1 and (not known or s + 2 < NS):
                            stage(s + 2, place % 2, n_ + 1, place % 2)
                halves(dve, body)
                scale(NU - 1, US - 1)
                n_all = start(NS)
                take((0, "o", 0, NS - 1), n_all[0], n_all[0] % 3, None, 0, 0, 0, IMAGES - 1, 1)


def feed_forward(nc, d, X, XA, const):
    LAGS = 4
    with ExitStack() as st:
        center, ones, eps = const.center, const.ones, const.eps
        lin = sb(nc, st, "l_lin", [P, P])
        vec = sb(nc, st, "l_vec", [P, 5])
        g1, b1, bl, g2, b2 = (vec[:, k:k + 1] for k in range(5))
        blin = sb(nc, st, "l_blin", [P, 1])
        sq1 = [sb(nc, st, f"l_sq1{k}", [P, CH]) for k in range(2)]
        sq2 = [sb(nc, st, f"l_sq2{k}", [P, CH]) for k in range(2)]
        xs = [sb(nc, st, f"l_xs{k}", [P, CH]) for k in range(2)]
        y = [sb(nc, st, f"l_y{k}", [P, CH]) for k in range(2)]
        z = [sb(nc, st, f"l_z{k}", [P, CH]) for k in range(2)]
        p_c1 = [ps(nc, st, f"l_pc1{k}") for k in range(2)]
        p_c2 = [ps(nc, st, f"l_pc2{k}") for k in range(2)]
        p_v1 = ps(nc, st, "l_pv1")
        p_v2 = ps(nc, st, "l_pv2")
        p_l = ps(nc, st, "l_pl")
        w_in = sem(nc, st, "l_w_in")
        bias_made = sem(nc, st, "l_bias_made")
        bias_out = sem(nc, st, "l_bias_out")
        centered, squared, varied, inverted, scaled = (
            [sem(nc, st, f"l_{name}{k}") for k in range(2)]
            for name in ("centered", "squared", "varied", "inverted", "scaled"))
        layered = sem(nc, st, "l_layered")
        clipped = sem(nc, st, "l_clipped")
        added = sem(nc, st, "l_added")

        with nc.Block() as block:
            @block.sync
            def _(sp):
                for dst, src in ((lin, "w_lin"), (vec, "mid_vec")):
                    sp.dma_start(dst[:], d[src]).then_inc(w_in, 16)

            @block.tensor
            def _(pe):
                pe.wait_ge(w_in, 32)
                pe.matmul(p_l[:, 0:1], lin[:], b1, start=True, stop=True).then_inc(bias_made, 1)
                pe.wait_ge(bias_out, 1)

                def step(s, k, h):
                    c = s - 4
                    if within(c):
                        pe.wait_ge(squared[1], c + 1)
                        if some(c, 1):
                            pe.wait_ge(inverted[1], c * 2 - 1)
                        pe.matmul(p_v2[:], ones[:], sq2[k][:], start=True, stop=True).then_inc(varied[1], 1)
                    c = s - 3
                    if within(c):
                        pe.wait_ge(added, c + 1)
                        if some(c, 2):
                            pe.wait_ge(scaled[1], c - 1)
                        pe.matmul(p_c2[1 - k][:], center[:], y[1 - k][:], start=True, stop=True)\
                          .then_inc(centered[1], 1)
                    c = s - 2
                    if within(c):
                        pe.wait_ge(scaled[0], c + 1)
                        if some(c, 1):
                            pe.wait_ge(clipped, c)
                        pe.matmul(p_l[:], lin[:], xs[k][:], start=True, stop=True).then_inc(layered, 1)
                    c = s - 1
                    if within(c):
                        pe.wait_ge(squared[0], c + 1)
                        if some(c, 1):
                            pe.wait_ge(inverted[0], c * 2 - 1)
                        pe.matmul(p_v1[:], ones[:], sq1[1 - k][:], start=True, stop=True).then_inc(varied[0], 1)
                    c = s
                    if within(c):
                        if some(c, 2):
                            pe.wait_ge(scaled[0], c - 1)
                        pe.matmul(p_c1[k][:], center[:],
                                  XA[:, bass.ds(h, 1), REACH + k * CH:REACH + (k + 1) * CH]
                                  .rearrange("p o w -> p (o w)"), start=True, stop=True)\
                          .then_inc(centered[0], 1)
                skewed(pe, NCH, LAGS, step, 2, LAGS + 2)

            @block.scalar
            def _(act):
                act.preload_act_table_set("natural_log_exp_and_others")
                act.wait_ge(w_in, 32)

                def invert(c, which, p_v, sq):
                    act.wait_ge(varied[which], c + 1)
                    act.activation(sq[:], p_v[:], ACT.Ln, bias=eps[:]).then_inc(inverted[which], 1)
                    act.wait_ge(inverted[which], c * 2 + 1)
                    act.activation(sq[:], sq[:], ACT.Exp, scale=-0.5).then_inc(inverted[which], 1)

                def square(c, which, p_c, sq):
                    act.wait_ge(centered[which], c + 1)
                    if some(c, 2):
                        act.wait_ge(scaled[which], c - 1)
                    act.activation(sq[:], p_c[:], ACT.Square).then_inc(squared[which], 1)

                def step(s, k, h):
                    if within(s - 4):
                        invert(s - 4, 1, p_v2, sq2[k])
                    if within(s - 3):
                        square(s - 3, 1, p_c2[1 - k], sq2[1 - k])
                    c = s - 2
                    if within(c):
                        if not some(c, 1):
                            act.wait_ge(bias_out, 1)
                        act.wait_ge(layered, c + 1)
                        if some(c, 2):
                            act.wait_ge(centered[1], c - 1)
                        act.activation(y[k][:], p_l[:], ACT.Relu, bias=blin[:]).then_inc(clipped, 1)
                    if within(s - 1):
                        invert(s - 1, 0, p_v1, sq1[1 - k])
                    if within(s):
                        square(s, 0, p_c1[k], sq1[k])
                skewed(act, NCH, LAGS, step, 2, LAGS + 2)

            @block.vector
            def _(dve):
                dve.wait_ge(w_in, 32)
                dve.wait_ge(bias_made, 1)
                dve.tensor_tensor(blin[:], bl, p_l[:, 0:1], ALU.add).then_inc(bias_out, 1)

                def step(s, k, h):
                    c = s - 4
                    if within(c):
                        dve.wait_ge(inverted[1], c * 2 + 2)
                        dve.scalar_tensor_tensor(z[k][:], p_c2[k][:], g2, sq2[k][:], ALU.mult, ALU.mult)\
                           .then_inc(scaled[1], 1)
                        dve.wait_ge(scaled[1], c + 1)
                        cols = X[:, bass.ds(c * CH, CH)]
                        dve.scalar_tensor_tensor(cols, z[k][:], b2, cols, ALU.add, ALU.add)
                    c = s - 2
                    if within(c):
                        dve.wait_ge(clipped, c + 1)
                        dve.scalar_tensor_tensor(y[k][:], y[k][:], b1, xs[k][:], ALU.add, ALU.add)\
                           .then_inc(added, 1)
                    c = s - 1
                    if within(c):
                        dve.wait_ge(inverted[0], c * 2 + 2)
                        if some(c, 2):
                            dve.wait_ge(layered, c - 1)
                        dve.scalar_tensor_tensor(xs[1 - k][:], p_c1[1 - k][:], g1, sq1[1 - k][:],
                                                 ALU.mult, ALU.mult).then_inc(scaled[0], 1)
                skewed(dve, NCH, LAGS, step, 2, LAGS + 2)


def dispatch(nc, d, X, const, ew, table, slots):
    LAGS = 4
    NT = 2 * TPC
    GRP = NCH // 2
    NR = 21
    with ExitStack() as st:
        center, ones, ident, eps = const.center, const.ones, const.ident, const.eps
        upper = sb(nc, st, "m_upper", [P, P])
        full = sb(nc, st, "m_full", [P, P])
        wr = sb(nc, st, "m_wr", [P, EXPERTS])
        br = sb(nc, st, "m_br", [P, EXPERTS])
        num = sb(nc, st, "m_num", [P, EXPERTS])
        region = sb(nc, st, "m_region", [P, EXPERTS])
        dest = sb(nc, st, "m_dest", [P, GRP, 2, NT], I32)
        pad = sb(nc, st, "m_pad", [P, PADS, ROW], I32)
        part = sb(nc, st, "m_part", [P, 1])
        blk = sb(nc, st, "m_blk", [P, BLOCKS])
        spare = sb(nc, st, "m_spare", [P, SPARE])
        sq1 = [sb(nc, st, f"m_sq1{k}", [P, CH]) for k in range(2)]
        sq2 = [sb(nc, st, f"m_sq2{k}", [P, CH]) for k in range(2)]
        y = [sb(nc, st, f"m_y{k}", [P, CH]) for k in range(2)]
        xn = [sb(nc, st, f"m_xn{k}", [P, CH]) for k in range(2)]
        pay = [[sb(nc, st, f"m_pay{c}{h}", [P, NT, ROW]) for h in range(2)] for c in range(2)]
        pos = [sb(nc, st, f"m_pos{h}", [P, 2, NT], I32) for h in range(2)]
        LT = sb(nc, st, "m_LT", [P, NT, EXPERTS])
        top = sb(nc, st, "m_top", [P, NT, 8])
        idx = sb(nc, st, "m_idx", [P, NT, 8], U32)
        fidx = sb(nc, st, "m_fidx", [P, NT, 2])
        dif = sb(nc, st, "m_dif", [P, NT])
        ex = sb(nc, st, "m_ex", [P, NT])
        sm = sb(nc, st, "m_sm", [P, NT])
        hot = sb(nc, st, "m_hot", [P, 2, NT, EXPERTS])
        both = sb(nc, st, "m_both", [P, NT, EXPERTS])
        cnt = sb(nc, st, "m_cnt", [P, 2, NT, EXPERTS])
        scan = [sb(nc, st, f"m_scan{k}", [P, NT, EXPERTS]) for k in range(2)]
        at = sb(nc, st, "m_at", [P, NT, EXPERTS])
        wpos = sb(nc, st, "m_wpos", [P, NT, EXPERTS])
        total = sb(nc, st, "m_total", [P, EXPERTS])
        fpos = sb(nc, st, "m_fpos", [P, 2, NT])
        fend = sb(nc, st, "m_fend", [P, PADS])
        end = sb(nc, st, "m_end", [P, PADS], I32)
        nblk = sb(nc, st, "m_nblk", [P, 3, EXPERTS])
        iblk = sb(nc, st, "m_iblk", [P, EXPERTS], I32)
        past = sb(nc, st, "m_past", [P, BLOCKS])
        etab = sb(nc, st, "m_etab", [P, BLOCKS])
        rtab = sb(nc, st, "m_rtab", [P, BLOCKS])
        p_c1 = [ps(nc, st, f"m_pc1{k}") for k in range(2)]
        p_c2 = [ps(nc, st, f"m_pc2{k}") for k in range(2)]
        p_v1 = ps(nc, st, "m_pv1")
        p_v2 = ps(nc, st, "m_pv2")
        p_t = ps(nc, st, "m_pt")
        p_r = ps(nc, st, "m_pr")
        COUNTS = NT * EXPERTS
        w_in = sem(nc, st, "m_w_in")
        cleared = sem(nc, st, "m_cleared")
        centered, squared, varied, inverted, scaled = (
            [sem(nc, st, f"m_{name}{k}") for k in range(2)]
            for name in ("centered", "squared", "varied", "inverted", "scaled"))
        judged = sem(nc, st, "m_judged")
        read = sem(nc, st, "m_read")
        turned = sem(nc, st, "m_turned")
        paid = sem(nc, st, "m_paid")
        tops = sem(nc, st, "m_tops")
        power = sem(nc, st, "m_power")
        route = sem(nc, st, "m_route")
        counted = sem(nc, st, "m_counted")
        labelled = sem(nc, st, "m_labelled")
        sent = [sem(nc, st, f"m_sent{h}") for h in range(2)]
        final = sem(nc, st, "m_final")
        ticked = sem(nc, st, "m_ticked")
        ew_in = sem(nc, st, "m_ew_in")
        NW, NEW = 11, 6

        with nc.Block() as block:
            @block.sync
            def _(sp):
                for dst, src in ((wr, "wr"), (upper, "c_upper"), (full, "c_full"), (num, "c_number"), (region, "c_region"),
                                 (dest, "c_dest"), (pad, "c_pad"), (part, "c_partition"), (blk, "c_block"),
                                 (spare, "c_spare")):
                    sp.dma_start(dst[:], d[src]).then_inc(w_in, 16)
                sp.dma_start(br[:], d["br"].partition_broadcast(P)).then_inc(w_in, 16)
                for dst, src in ((ew.w1, "w1"), (ew.w2, "w2"), (ew.lng, "ln_g"),
                                 (ew.lnb, "ln_b"), (ew.b1, "b1")):
                    sp.dma_start(dst[:], d[src]).then_inc(ew_in, 16)
                sp.dma_start(ew.b2[:].rearrange("p e c -> p (e c)"), d["b2_row"].partition_broadcast(P))\
                  .then_inc(ew_in, 16)

            @block.gpsimd
            def _(pool):
                nc.gpsimd.memset(total[:], 0.0).then_inc(cleared, 1)
                for h in range(2):
                    for c in range(2):
                        nc.gpsimd.memset(pay[c][h][:, :, P:ROW], 0.0).then_inc(cleared, 1)
                tick = sb(nc, st, "m_tick", [1, 2])
                nc.gpsimd.memset(tick[:], 0.0).then_inc(cleared, 1)
                pool.wait_ge(cleared, 6)
                with pool.Fori(0, GRP // 2) as i:
                    for h in range(2):
                        g = i * 2 + h
                        pool.wait_ge(ticked, g)
                        pool.wait_ge(labelled, g * 2 + 2)
                        pool.wait_ge(paid, g * 4 + 4)
                        nc.gpsimd.tensor_tensor(tick[:, 1:2], tick[:, 0:1], tick[:, 0:1], ALU.add)\
                          .then_inc(ticked, 1)
                        for c in range(2):
                            for t in range(NT):
                                nc.gpsimd.indirect_dma_start(
                                    out=slots, out_offset=bass.IndirectOffsetOnAxis(
                                        ap=pos[h][:, c, t:t + 1].bitcast(U32), axis=0),
                                    in_=pay[c][h][:, t, :], in_offset=None).then_inc(sent[h], 16)
                pool.wait_ge(final, 1)
                pool.wait_ge(w_in, 16 * NW)
                for e in range(PADS):
                    nc.gpsimd.indirect_dma_start(
                        out=slots, out_offset=bass.IndirectOffsetOnAxis(ap=end[:, e:e + 1].bitcast(U32), axis=0),
                        in_=pad[:, e, :].bitcast(F32), in_offset=None).then_inc(sent[0], 16)
                pool.wait_ge(sent[0], 16 * (NT * GRP + PADS))
                pool.wait_ge(sent[1], 16 * NT * GRP)

            @block.tensor
            def _(pe):
                def step(s, place, h):
                    k = place % 2
                    c = s - 4
                    if within(c):
                        pe.wait_ge(scaled[1], c + 1)
                        if some(c, 1):
                            pe.wait_ge(paid, c * 2)
                        for t in range(TPC):
                            last = pe.transpose(p_t[:, t * P:(t + 1) * P], xn[k][:, t * P:(t + 1) * P],
                                                ident[:])
                        last.then_inc(turned, 1)
                    c = s - 3
                    if within(c):
                        pe.wait_ge(squared[1], c + 1)
                        if some(c, 1):
                            pe.wait_ge(inverted[1], c * 2 - 1)
                        pe.matmul(p_v2[:], ones[:], sq2[1 - k][:], start=True, stop=True)\
                          .then_inc(varied[1], 1)
                    c = s - 2
                    if within(c):
                        pe.wait_ge(scaled[0], c + 1)
                        if some(c, 2):
                            pe.wait_ge(scaled[1], c - 1)
                        pe.matmul(p_c2[k][:], center[:], y[k][:], start=True, stop=True)\
                          .then_inc(centered[1], 1)
                        if some(c, 1):
                            pe.wait_ge(read, c)
                            if k == 0:
                                pe.wait_ge(route, (h - 2) * NR + 7)
                        if not some(c, 1):
                            pe.wait_ge(w_in, 16 * NW)
                        for t in range(TPC):
                            o = (k * TPC + t) * EXPERTS
                            last = pe.matmul(p_r[:, o:o + EXPERTS], y[k][:, t * P:(t + 1) * P], wr[:],
                                             start=True, stop=True)
                        last.then_inc(judged, 1)
                    c = s - 1
                    if within(c):
                        pe.wait_ge(squared[0], c + 1)
                        if some(c, 1):
                            pe.wait_ge(inverted[0], c * 2 - 1)
                        pe.matmul(p_v1[:], ones[:], sq1[1 - k][:], start=True, stop=True)\
                          .then_inc(varied[0], 1)
                    c = s
                    if within(c):
                        if some(c, 2):
                            pe.wait_ge(scaled[0], c - 1)
                        pe.matmul(p_c1[k][:], center[:], X[:, bass.ds(c * CH, CH)], start=True, stop=True)\
                          .then_inc(centered[0], 1)
                    if k == 1 and within(s - 3):
                        pe.wait_ge(route, (h - 1) * NR + 6)
                        bothf = both[:].rearrange("p t e -> p (t e)")
                        pe.matmul(p_r[:, COUNTS:2 * COUNTS], upper[:], bothf, start=True, stop=True)
                        pe.matmul(p_r[:, 2 * COUNTS:3 * COUNTS], full[:], bothf, start=True, stop=True)\
                          .then_inc(counted, 1)
                skewed(pe, NCH, LAGS, step, 4, 4)
                pe.wait_ge(ew_in, 16 * NEW)
                pe.wait_ge(scaled[0], NCH)
                for e in range(EXPERTS):
                    for q in range(HC):
                        last = pe.matmul(p_c1[0][:, e * HC + q:e * HC + q + 1], ew.w1[:, e, q * P:(q + 1) * P],
                                         ew.lnb[:, e:e + 1], start=True, stop=True)
                last.then_inc(counted, 1)

            @block.scalar
            def _(act):
                act.preload_act_table_set("natural_log_exp_and_others")
                act.wait_ge(cleared, 6)

                def invert(c, which, p_v, sq):
                    act.wait_ge(varied[which], c + 1)
                    act.activation(sq[:], p_v[:], ACT.Ln, bias=eps[:]).then_inc(inverted[which], 1)
                    act.wait_ge(inverted[which], c * 2 + 1)
                    act.activation(sq[:], sq[:], ACT.Exp, scale=-0.5).then_inc(inverted[which], 1)

                def square(c, which, p_c, sq):
                    act.wait_ge(centered[which], c + 1)
                    if some(c, 2):
                        act.wait_ge(scaled[which], c - 1)
                    act.activation(sq[:], p_c[:], ACT.Square).then_inc(squared[which], 1)

                def step(s, place, h):
                    k = place % 2
                    c = s - 4
                    if within(c):
                        if k == 0:
                            act.wait_ge(tops, h - 1)
                            act.activation(ex[:], dif[:], ACT.Exp).then_inc(power, 1)
                            if some(c, 4):
                                act.wait_ge(sent[place // 2], (h - 2 - place // 2) * (16 * NT))
                        act.wait_ge(turned, c + 1)
                        for w in range(2):
                            act.activation(pay[w][place // 2][:, k * TPC:(k + 1) * TPC, 0:P],
                                           p_t[:].rearrange("p (t c) -> p t c", t=TPC), ACT.Copy)\
                               .then_inc(paid, 1)
                    if within(s - 3):
                        invert(s - 3, 1, p_v2, sq2[1 - k])
                    if within(s - 2):
                        square(s - 2, 1, p_c2[k], sq2[k])
                    if within(s - 1):
                        invert(s - 1, 0, p_v1, sq1[1 - k])
                    if within(s):
                        square(s, 0, p_c1[k], sq1[k])
                skewed(act, NCH, LAGS, step, 4, 4)

            @block.vector
            def _(dve):
                dve.wait_ge(cleared, 6)
                tiles = "p (t e) -> p t e"

                def scale(c, which, out, p_c, sq):
                    dve.wait_ge(inverted[which], c * 2 + 2)
                    dve.tensor_tensor(out[:], p_c[:], sq[:], ALU.mult).then_inc(scaled[which], 1)

                def choose(g):
                    r = g * NR
                    dve.wait_ge(read, g * 2 + 2)
                    dve.tensor_copy(sm[:, 0:1], LT[:, 0, 0:1])
                    for t in range(NT):
                        ins = dve.max(top[:, t, :], LT[:, t, :])
                    ins.then_inc(route, 1)
                    dve.wait_ge(route, r + 1)
                    dve.tensor_tensor(dif[:], top[:, :, 1], top[:, :, 0], ALU.subtract).then_inc(tops, 1)
                    for t in range(NT):
                        ins = dve.max_index(idx[:, t, :], top[:, t, :], LT[:, t, :])
                    ins.then_inc(route, 1)
                    dve.wait_ge(route, r + 2)
                    dve.tensor_copy(fidx[:], idx[:, :, 0:2]).then_inc(route, 1)
                    dve.wait_ge(route, r + 3)
                    numb = num[:].rearrange("p (o e) -> p o e", o=1).to_broadcast([P, NT, EXPERTS])
                    for c in range(2):
                        dve.tensor_tensor(hot[:, c], numb, fidx[:, :, c:c + 1].to_broadcast([P, NT, EXPERTS]),
                                          ALU.is_equal).then_inc(route, 1)
                    dve.wait_ge(route, r + 5)
                    dve.tensor_tensor(both[:], hot[:, 0], hot[:, 1], ALU.add).then_inc(route, 1)

                def take_counts(g):
                    dve.wait_ge(counted, g + 1)
                    dve.tensor_copy(cnt[:].rearrange("p c t e -> p (c t e)"), p_r[:, COUNTS:3 * COUNTS])\
                       .then_inc(route, 1)

                def place_rows(g, h):
                    r = g * NR
                    dve.wait_ge(power, g + 1)
                    dve.tensor_scalar(sm[:], ex[:], 1.0, None, ALU.add).then_inc(route, 1)
                    dve.wait_ge(route, r + 8)
                    dve.reciprocal(sm[:], sm[:]).then_inc(route, 1)
                    src, shift, n = cnt[:, 1], 1, 9
                    while shift < NT:
                        dst = scan[n % 2]
                        dve.wait_ge(route, r + n)
                        dve.tensor_copy(dst[:, 0:shift], src[:, 0:shift])
                        dve.tensor_tensor(dst[:, shift:], src[:, shift:], src[:, :NT - shift], ALU.add)\
                           .then_inc(route, 1)
                        src, shift, n = dst, shift * 2, n + 1
                    dst = scan[n % 2]
                    dve.wait_ge(route, r + n)
                    dve.tensor_tensor(at[:], src[:], cnt[:, 1], ALU.subtract).then_inc(route, 1)
                    dve.tensor_tensor(dst[:, 0, :], total[:], region[:], ALU.add).then_inc(route, 1)
                    dve.wait_ge(route, r + 14)
                    dve.tensor_tensor(at[:], at[:], dst[:, 0:1, :].to_broadcast([P, NT, EXPERTS]), ALU.add)\
                       .then_inc(route, 1)
                    dve.tensor_tensor(total[:], total[:], src[:, NT - 1, :], ALU.add).then_inc(route, 1)
                    dve.wait_ge(route, r + 16)
                    dve.tensor_tensor(at[:], at[:], cnt[:, 0], ALU.add).then_inc(route, 1)
                    for c in range(2):
                        dve.wait_ge(route, r + 17 + 2 * c)
                        dve.tensor_tensor(wpos[:], at[:], hot[:, c], ALU.mult).then_inc(route, 1)
                        dve.wait_ge(route, r + 18 + 2 * c)
                        dve.tensor_reduce(fpos[:, c, :], wpos[:], AX.X, ALU.add).then_inc(route, 1)
                    if not isinstance(g, int) or g >= 2:
                        dve.wait_ge(sent[h], (g - h) * (16 * NT))
                    for c in range(2):
                        dve.tensor_copy(pay[c][h][:, :, P:P + 1].bitcast(I32), dest[:, bass.ds(g, 1), c, :]
                                        .rearrange("p o t -> p t o"))
                    dve.tensor_copy(pay[0][h][:, :, P + 1:P + 2], sm[:].rearrange("p (t o) -> p t o", o=1))
                    dve.tensor_tensor(pay[1][h][:, :, P + 1:P + 2], sm[:].rearrange("p (t o) -> p t o", o=1),
                                      ex[:].rearrange("p (t o) -> p t o", o=1), ALU.mult).then_inc(labelled, 1)
                    dve.wait_ge(route, r + 21)
                    dve.tensor_copy(pos[h][:], fpos[:]).then_inc(labelled, 1)

                def step(s, place, h):
                    k = place % 2
                    if k == 0 and within(s - 4):
                        take_counts(h - 2)
                    if within(s - 3):
                        scale(s - 3, 1, xn[1 - k], p_c2[1 - k], sq2[1 - k])
                    c = s - 2
                    if within(c):
                        dve.wait_ge(judged, c + 1)
                        if not some(c, 1):
                            dve.wait_ge(w_in, 16 * NW)
                        dve.tensor_tensor(LT[:, k * TPC:(k + 1) * TPC, :],
                                          p_r[:, k * TPC * EXPERTS:(k + 1) * TPC * EXPERTS]
                                          .rearrange(tiles, t=TPC),
                                          br[:].rearrange("p (o e) -> p o e", o=1)
                                          .to_broadcast([P, TPC, EXPERTS]), ALU.add).then_inc(read, 1)
                    if within(s - 1):
                        if some(s - 1, 2):
                            dve.wait_ge(judged, s - 2)
                        scale(s - 1, 0, y[1 - k], p_c1[1 - k], sq1[1 - k])
                    if k == 0 and within(s - 4):
                        place_rows(h - 2, place // 2)
                    if k == 1 and within(s - 3):
                        choose(h - 1)
                skewed(dve, NCH, LAGS, step, 4, 4)

                base, n = NR * GRP, 0
                dve.tensor_tensor(fend[:, 0:EXPERTS], total[:], region[:], ALU.add).then_inc(route, 1)
                dve.tensor_copy(fend[:, EXPERTS:], spare[:]).then_inc(route, 1)
                dve.tensor_scalar(iblk[:], total[:], float(P - 1), None, ALU.add).then_inc(route, 1)
                dve.wait_ge(route, base + 3)
                dve.tensor_scalar(end[:], fend[:], part[:], None, ALU.add).then_inc(final, 1)
                dve.tensor_scalar(iblk[:], iblk[:], 7, None, ALU.arith_shift_right).then_inc(route, 1)
                dve.wait_ge(route, base + 4)
                dve.tensor_copy(nblk[:, 0, :], iblk[:]).then_inc(route, 1)
                dve.memset(etab[:], 0.0).then_inc(route, 1)
                dve.tensor_scalar(rtab[:], blk[:], float(P), None, ALU.mult).then_inc(route, 1)
                dve.wait_ge(route, base + 7)
                dve.tensor_scalar(nblk[:, 2, :], nblk[:, 0, :], -float(P), float(REGION), ALU.mult, ALU.add)
                dve.tensor_copy(nblk[:, 1, 0:1], nblk[:, 0, 0:1]).then_inc(route, 1)
                for e in range(1, EXPERTS):
                    dve.wait_ge(route, base + 7 + e)
                    dve.tensor_tensor(nblk[:, 1, e:e + 1], nblk[:, 1, e - 1:e], nblk[:, 0, e:e + 1], ALU.add)\
                       .then_inc(route, 1)
                n = base + 7 + EXPERTS
                for e in range(EXPERTS):
                    dve.wait_ge(route, n)
                    dve.tensor_scalar(past[:], blk[:], nblk[:, 1, e:e + 1], None, ALU.is_ge).then_inc(route, 1)
                    dve.wait_ge(route, n + 1)
                    dve.tensor_tensor(etab[:], etab[:], past[:], ALU.add)
                    dve.scalar_tensor_tensor(rtab[:], past[:], nblk[:, 2, e:e + 1], rtab[:], ALU.mult, ALU.add)\
                       .then_inc(route, 1)
                    n += 2
                dve.wait_ge(route, n)
                dve.tensor_copy(table[:, 0, :], rtab[0:1, :]).then_inc(final, 1)
                dve.tensor_scalar(table[:, 1, :], etab[0:1, :], float(EXPERTS - 1), None, ALU.min)\
                   .then_inc(final, 1)
                dve.wait_ge(counted, GRP + 1)
                for e in range(EXPERTS):
                    dve.tensor_scalar(ew.w1[:, e, :], ew.w1[:, e, :], ew.lng[:, e:e + 1], None, ALU.mult)\
                       .then_inc(final, 1)
                b1 = ew.b1[:].rearrange("p e q -> p (e q)")
                dve.tensor_tensor(b1, b1, p_c1[0][:, 0:EXPERTS * HC], ALU.add).then_inc(final, 1)


class ExpertWeights:

    def __init__(self, nc, st):
        self.w1 = sb(nc, st, "e_w1", [P, EXPERTS, HID])
        self.w2 = sb(nc, st, "e_w2", [P, EXPERTS, HC * P])
        self.lng = sb(nc, st, "e_lng", [P, EXPERTS])
        self.lnb = sb(nc, st, "e_lnb", [P, EXPERTS])
        self.b1 = sb(nc, st, "e_b1", [P, EXPERTS, HC])
        self.b2 = sb(nc, st, "e_b2", [P, EXPERTS, P])
        self.loaded = [sem(nc, st, f"e_loaded{j}") for j in range(NBX)]


def experts(nc, const, ew, table, slots, picks):
    with ExitStack() as st:
        ident, w1, w2, b1, b2 = const.ident, ew.w1, ew.w2, ew.b1, ew.b2
        rows = [sb(nc, st, f"e_rows{j}", [P, ROW]) for j in range(NBX)]
        xT = [sb(nc, st, f"e_xT{j}", [P, P]) for j in range(2)]
        hp = [sb(nc, st, f"e_hp{j}", [P, HID]) for j in range(2)]
        hT = [sb(nc, st, f"e_hT{j}", [P, HC, P]) for j in range(2)]
        yb = [sb(nc, st, f"e_yb{j}", [P, P]) for j in range(NBX)]
        yw = [sb(nc, st, f"e_yw{j}", [P, P]) for j in range(NBX)]
        p_x = [ps(nc, st, f"e_px{j}") for j in range(2)]
        p_h = [ps(nc, st, f"e_ph{j}") for j in range(2)]
        p_t = [ps(nc, st, f"e_pt{j}") for j in range(2)]
        p_y = [ps(nc, st, f"e_py{j}") for j in range(2)]
        rows_in = ew.loaded
        sent = [sem(nc, st, f"e_sent{j}") for j in range(NBX)]
        x_turned = sem(nc, st, "e_x_turned")
        x_out = sem(nc, st, "e_x_out")
        up = sem(nc, st, "e_up")
        up_out = sem(nc, st, "e_up_out")
        h_turned = sem(nc, st, "e_h_turned")
        gelu = sem(nc, st, "e_gelu")
        down = sem(nc, st, "e_down")
        biased = sem(nc, st, "e_biased")
        weighted = sem(nc, st, "e_weighted")
        cleared = sem(nc, st, "e_cleared")
        ticked = sem(nc, st, "e_ticked")
        with nc.Block() as block:
            @block.sync
            def _(sp):
                def load(b, j):
                    row = sp.value_load(table[0:1, 0, bass.ds(b, 1)], min_val=0, max_val=SLOTS - P)
                    sp.dma_start(rows[j][:], slots[bass.ds(row, P), :]).then_inc(rows_in[j], 16)

                for b in range(NBX):
                    load(b, b)
                with sp.Fori(1, BLOCKS // NBX) as i:
                    for j in range(NBX):
                        sp.wait_ge(sent[j], i * 16)
                        load(i * NBX + j, j)

            @block.gpsimd
            def _(pool):
                tick = sb(nc, st, "e_tick", [1, 2])
                nc.gpsimd.memset(tick[:], 0.0).then_inc(cleared, 1)
                pool.wait_ge(cleared, 1)
                with pool.Fori(0, BLOCKS // NBX) as i:
                    for j in range(NBX):
                        pool.wait_ge(ticked, i * NBX + j)
                        pool.wait_ge(weighted, i * NBX + j + 1)
                        nc.gpsimd.tensor_tensor(tick[:, 1:2], tick[:, 0:1], tick[:, 0:1], ALU.add)\
                          .then_inc(ticked, 1)
                        nc.gpsimd.indirect_dma_start(
                            out=picks, out_offset=bass.IndirectOffsetOnAxis(
                                ap=rows[j][:, P:P + 1].bitcast(U32), axis=0),
                            in_=yw[j][:], in_offset=None).then_inc(sent[j], 16)
                for j in range(NBX):
                    pool.wait_ge(sent[j], 16 * (BLOCKS // NBX))

            @block.tensor
            def _(pe):
                def turn_x(b, j, i):
                    pe.wait_ge(rows_in[j], (i + 1) * 16)
                    pe.transpose(p_x[j % 2][:, 0:P], rows[j][:, 0:P], ident[:]).then_inc(x_turned, 1)

                def first(b, j):
                    e = pe.value_load(table[0:1, 1, bass.ds(b, 1)], min_val=0, max_val=EXPERTS - 1)
                    pe.wait_ge(x_out, b + 1)
                    pe.matmul(p_h[j % 2][:], xT[j % 2][:], w1[:, bass.ds(e, 1), :].rearrange("p o h -> p (o h)"),
                              start=True, stop=True).then_inc(up, 1)

                def turn_h(b, j):
                    pe.wait_ge(up_out, b + 1)
                    for q in range(HC):
                        last = pe.transpose(p_t[j % 2][:, q * P:(q + 1) * P], hp[j % 2][:, q * P:(q + 1) * P],
                                            ident[:])
                    last.then_inc(h_turned, 1)

                def second(b, j):
                    e = pe.value_load(table[0:1, 1, bass.ds(b, 1)], min_val=0, max_val=EXPERTS - 1)
                    pe.wait_ge(gelu, b + 1)
                    if not isinstance(b, int) or b >= 2:
                        pe.wait_ge(biased, b - 1)
                    for q in range(HC):
                        last = pe.matmul(p_y[j % 2][:, 0:P], hT[j % 2][:, q, :],
                                         w2[:, bass.ds(e, 1), q * P:(q + 1) * P].rearrange("p o h -> p (o h)"),
                                         start=(q == 0), stop=(q == HC - 1))
                    last.then_inc(down, 1)

                def step(s, j, i, lo=0, hi=BLOCKS):
                    if hi:
                        turn_x(s, j, i)
                    for back, stage in ((1, first), (2, turn_h), (3, second)):
                        if back >= lo and (not isinstance(s, int) or 0 <= s - back < BLOCKS):
                            stage(s - back, (j - back) % NBX)

                for s in range(NBX):
                    step(s, s, 0)
                with pe.Fori(1, BLOCKS // NBX) as i:
                    for j in range(NBX):
                        step(i * NBX + j, j, i)
                for s in range(BLOCKS, BLOCKS + 3):
                    step(s, s % NBX, 0, hi=0)

            @block.scalar
            def _(act):
                def scale_out(b, j):
                    act.wait_ge(biased, b + 1)
                    act.activation(yw[j][:], yb[j][:], ACT.Copy, scale=rows[j][:, P + 1:P + 2])\
                       .then_inc(weighted, 1)

                def gelus(b, j):
                    e = act.value_load(table[0:1, 1, bass.ds(b, 1)], min_val=0, max_val=EXPERTS - 1)
                    act.wait_ge(h_turned, b + 1)
                    for q in range(HC):
                        ins = act.activation(hT[j % 2][:, q, :], p_t[j % 2][:, q * P:(q + 1) * P], ACT.Gelu,
                                             bias=b1[:, bass.ds(e, 1), q:q + 1].rearrange("p o h -> p (o h)"))
                    ins.then_inc(gelu, 1)

                def step(s, j):
                    if not isinstance(s, int) or s < BLOCKS:
                        gelus(s, j)
                    if not isinstance(s, int) or s >= 2:
                        scale_out(s - 2, (j - 2) % NBX)

                for s in range(NBX):
                    step(s, s)
                with act.Fori(1, BLOCKS // NBX) as i:
                    for j in range(NBX):
                        step(i * NBX + j, j)
                for s in range(BLOCKS, BLOCKS + 2):
                    step(s, s % NBX)

            @block.vector
            def _(dve):
                def copy_x(b, j):
                    dve.wait_ge(x_turned, b + 1)
                    dve.tensor_copy(xT[j % 2][:], p_x[j % 2][:, 0:P]).then_inc(x_out, 1)

                def copy_h(b, j):
                    dve.wait_ge(up, b + 1)
                    dve.tensor_copy(hp[j % 2][:], p_h[j % 2][:]).then_inc(up_out, 1)

                def add_bias(b, j):
                    e = dve.value_load(table[0:1, 1, bass.ds(b, 1)], min_val=0, max_val=EXPERTS - 1)
                    dve.wait_ge(down, b + 1)
                    dve.tensor_tensor(yb[j][:], p_y[j % 2][:, 0:P],
                                      b2[:, bass.ds(e, 1), :].rearrange("p o c -> p (o c)"), ALU.add)\
                       .then_inc(biased, 1)

                def step(s, j):
                    for back, stage in ((0, copy_x), (1, copy_h), (3, add_bias)):
                        if not isinstance(s, int) or 0 <= s - back < BLOCKS:
                            stage(s - back, (j - back) % NBX)

                for s in range(NBX):
                    step(s, s)
                with dve.Fori(1, BLOCKS // NBX) as i:
                    for j in range(NBX):
                        step(i * NBX + j, j)
                for s in range(BLOCKS, BLOCKS + 3):
                    step(s, s % NBX)


def combine(nc, const, ew, X, picks, out):
    NB = 3
    with ExitStack() as st:
        y = [[sb(nc, st, f"c_y{c}{j}", [P, TPC, P]) for j in range(NB)] for c in range(2)]
        o = [sb(nc, st, f"c_o{j}", [P, CH]) for j in range(NB)]
        p_t = [ps(nc, st, f"c_pt{j}") for j in range(NB)]
        y_in, stored, base = ew.loaded[:NB], ew.loaded[NB:2 * NB], 16 * (BLOCKS // NBX)
        both = sem(nc, st, "c_both")
        turned = sem(nc, st, "c_turned")
        added = sem(nc, st, "c_added")
        with nc.Block() as block:
            @block.sync
            def _(sp):
                for c in range(NCH):
                    j = c % NB
                    if c >= NB:
                        sp.wait_ge(turned, c - NB + 1)
                    for k in range(2):
                        src = picks[k * TOK + c * CH:k * TOK + (c + 1) * CH, :]
                        sp.dma_start(y[k][j][:], src.rearrange("(t p) c -> p t c", p=P)).then_inc(y_in[j], 16)

            @block.vector
            def _(dve):
                for c in range(NCH + 1):
                    if c < NCH:
                        j = c % NB
                        dve.wait_ge(y_in[j], base + 32 * (c // NB + 1))
                        dve.tensor_tensor(y[0][j][:], y[0][j][:], y[1][j][:], ALU.add).then_inc(both, 1)
                    if c:
                        b = c - 1
                        dve.wait_ge(turned, b + 1)
                        if b >= NB:
                            dve.wait_ge(stored[b % NB], base + 16 * (b // NB))
                        dve.tensor_tensor(o[b % NB][:], p_t[b % NB][:], X[:, b * CH:(b + 1) * CH], ALU.add)\
                           .then_inc(added, 1)

            @block.tensor
            def _(pe):
                for c in range(NCH):
                    j = c % NB
                    pe.wait_ge(both, c + 1)
                    if c >= NB:
                        pe.wait_ge(added, c - NB + 1)
                    for t in range(TPC):
                        last = pe.transpose(p_t[j][:, t * P:(t + 1) * P], y[0][j][:, t, :], const.ident[:])
                    last.then_inc(turned, 1)

            @block.scalar
            def _(act):
                for c in range(NCH):
                    act.wait_ge(added, c + 1)
                    act.dma_start(out[c // 2, :, (c % 2) * CH:(c % 2 + 1) * CH], o[c % NB][:])\
                       .then_inc(stored[c % NB], 16)
                for j in range(NB):
                    act.wait_ge(stored[j], base + 16 * len(range(j, NCH, NB)))


def program(nc, d, out, dbg=None):
    with ExitStack() as st:
        X = sb(nc, st, "X", [P, TOK])
        with ExitStack() as st1:
            VP = sb(nc, st1, "VP", [P, IMAGES, PAD5, PAD5])
            OM = sb(nc, st1, "OM", [P, TOK // P, 3 * GK])
            flag = sb(nc, st1, "flag", [1, 1], I32)
            front(nc, d, X, VP, OM, flag)
            if dbg: dbg("front", dict(VP=VP, OM=OM, flag=flag))
            sample_fast(nc, d, X, VP, OM)
            sample_general(nc, d, X, VP, OM, flag)
            if dbg: dbg("fast", dict(X=X))
        table = sb(nc, st, "table", [1, 2, BLOCKS], I32)
        with ExitStack() as st1:
            XA = sb(nc, st1, "XA", [P, IMAGES, PIX + 2 * REACH])
            const = Constants(nc, st1)
            token_norm(nc, d, X, XA, const)
            if dbg: dbg("ln", dict(XA=XA))
            attention(nc, d, XA, const)
            if dbg: dbg("attn", dict(XA=XA))
            slots = nc.dram_tensor("slots", [SLOTS, ROW], F32, kind="Internal").ap()
            picks = nc.dram_tensor("picks", [2 * TOK + PADS * P, P], F32, kind="Internal").ap()
            ew = ExpertWeights(nc, st1)
            feed_forward(nc, d, X, XA, const)
            dispatch(nc, d, X, const, ew, table, slots)
            if dbg: dbg("mid", dict(X=X, table=table))
            experts(nc, const, ew, table, slots, picks)
            combine(nc, const, ew, X, picks, out)


def arrays_of(inp):
    import numpy as np

    n = {}
    n["x"] = np.ascontiguousarray(inp["x"]).reshape(IMAGES, P, PIX)
    g = lambda k: np.ascontiguousarray(inp[k])
    n["dw_w"] = g("L0_conv_dw_w").reshape(P, K)
    n["dw_b"] = g("L0_conv_dw_b").reshape(P, 1)
    om = g("L0_conv_om_w").reshape(GROUPS, 3 * K, P)
    ob = g("L0_conv_om_b").reshape(GROUPS, 3 * K)
    parts = [slice(0, 2 * K, 2), slice(1, 2 * K, 2), slice(2 * K, 3 * K)]
    n["om_wT"] = np.ascontiguousarray(np.concatenate([om[:, s].reshape(GK, P) for s in parts]).T)
    n["om_b"] = np.concatenate([ob[:, s].reshape(GK) for s in parts])
    n["vp_wT"] = np.ascontiguousarray(g("L0_conv_vp_w").T)
    n["vp_b"] = g("L0_conv_vp_b").reshape(P, 1)
    n["op_wT"] = np.ascontiguousarray(g("L0_conv_op_w").T)
    n["c_ident"] = np.eye(P, dtype=np.float32)
    n["c_group4"] = np.kron(np.eye(P // 4), np.full((4, 4), 0.25)).astype(np.float32)
    sel = np.zeros((3, GROUPS, 5, 5, P), np.float32)
    for g_ in range(GROUPS):
        for b in range(5):
            sel[:, g_, b, b, g_ * CG:(g_ + 1) * CG] = 1
    n["c_select"] = sel.reshape(3 * GROUPS * 5, 5, P)
    n["c_center"] = (np.eye(P) - np.full((P, P), 1 / P)).astype(np.float32)
    n["c_ones"] = np.full((P, P), 1 / P, np.float32)
    n["wq"] = g("L1_attn_Wq").reshape(P, 2, P)
    n["wk"] = g("L1_attn_Wk").reshape(P, 2, P)
    n["wv"], n["wo"] = g("L1_attn_Wv"), g("L1_attn_Wo")
    n["bq"] = np.ascontiguousarray(g("L1_attn_bq").reshape(2, P).T)
    n["bk"] = np.ascontiguousarray(g("L1_attn_bk").reshape(2, P).T)
    n["bv"], n["bo"] = g("L1_attn_bv"), g("L1_attn_bo").reshape(P, 1)
    n["rel_bias"] = g("L1_attn_rel_bias")
    n["w_lin"] = g("L1_attn_W_lin")
    n["mid_vec"] = np.stack([g("L1_attn_" + k) for k in ("ln1_g", "ln1_b", "b_lin", "ln2_g", "ln2_b")], -1)
    n["w1"] = np.ascontiguousarray(g("L1_ffn_W1").transpose(1, 0, 2))
    n["w2"] = np.ascontiguousarray(g("L1_ffn_W2").reshape(EXPERTS, HC, P, P).transpose(2, 0, 1, 3))
    n["wr"], n["br"] = g("L1_ffn_Wr"), g("L1_ffn_br")
    n["ln_g"] = np.ascontiguousarray(g("L1_ffn_ln_g").T)
    n["ln_b"] = np.ascontiguousarray(g("L1_ffn_ln_b").T)
    n["b1"] = np.ascontiguousarray(g("L1_ffn_b1").reshape(EXPERTS, HC, P).transpose(2, 0, 1))
    n["b2"] = np.ascontiguousarray(g("L1_ffn_b2").T)
    n["b2_row"] = g("L1_ffn_b2").reshape(EXPERTS * P)
    n["c_upper"] = np.triu(np.ones((P, P), np.float32), 1)
    n["c_full"] = np.ones((P, P), np.float32)
    n["c_region"] = np.broadcast_to(np.arange(EXPERTS, dtype=np.float32) * REGION, (P, EXPERTS)).copy()
    n["c_dest"] = (np.arange(TOK, dtype=np.int32).reshape(NCH // 2, 2 * TPC, P).transpose(2, 0, 1)[:, :, None]
                   + np.array([0, TOK], np.int32)[:, None]).astype(np.int32)
    n["c_pad"] = np.zeros((P, PADS, ROW), np.int32)
    n["c_pad"][:, :, P] = 2 * TOK + np.arange(PADS) * P + np.arange(P)[:, None]
    n["c_spare"] = np.broadcast_to(EXPERTS * REGION + np.arange(SPARE, dtype=np.float32) * P, (P, SPARE)).copy()
    n["c_partition"] = np.arange(P, dtype=np.float32).reshape(P, 1)
    n["c_block"] = np.broadcast_to(np.arange(BLOCKS, dtype=np.float32), (P, BLOCKS)).copy()
    n["c_number"] = np.broadcast_to(np.arange(EXPERTS, dtype=np.float32), (P, EXPERTS)).copy()
    n["c_line"] = np.broadcast_to(np.arange(SIDE, dtype=np.float32), (P, SIDE)).copy()
    tok = np.arange(PIX).reshape(PIX // P, P).T
    n["c_pixel"] = np.stack([tok // SIDE, tok % SIDE], -1).astype(np.float32)
    point = np.tile(np.arange(K), GROUPS)
    kern = np.stack([point // 3 - 1, point % 3 - 1]).astype(np.float32)
    n["c_kernel"] = np.broadcast_to(kern, (P, 2, GK)).copy()
    return n


def kernel(**inputs):
    import numpy as np
    import concourse.bacc as bacc
    from concourse.bass_utils import run_bass_kernel_spmd

    nc = bacc.Bacc("TRN2", target_bir_lowering=False, num_devices=1)
    arrays = arrays_of(inputs)
    d = {k: nc.dram_tensor("in_" + k, list(a.shape), mybir.dt.from_np(a.dtype), kind="ExternalInput").ap()
         for k, a in arrays.items()}
    out = nc.dram_tensor("out", [IMAGES, P, PIX], F32, kind="ExternalOutput").ap()
    program(nc, d, out)
    r = run_bass_kernel_spmd(nc, [{"in_" + k: a for k, a in arrays.items()}], core_ids=[0])
    return r.results[0]["out"].reshape(IMAGES, P, SIDE, SIDE)
```
